# Optimizing a Trainium2 kernel written in Bass

```python
import numpy as np
import jax
import jax.numpy as jnp

def _softmax(x, axis=-1):
    return jax.nn.softmax(x, axis=axis)

def _gelu(x):
    return jax.nn.gelu(x, approximate=True)

def _silu(x):
    return jax.nn.silu(x)

def _sigmoid(x):
    return jax.nn.sigmoid(x)

def _layernorm(x, axis=-1, eps=1e-05):
    m = jnp.mean(x, axis=axis, keepdims=True)
    v = jnp.var(x, axis=axis, keepdims=True)
    return (x - m) / jnp.sqrt(v + eps)

def _scatter_add(tgt, idx, src, axis=0):
    return tgt.at[idx].add(src)

def _segment_sum(src, seg, n):
    return jax.ops.segment_sum(src, seg, n)
kernel_name = 'mk_decoder_postln_d1_seqx_r8_19d6f7'

def setup_inputs(seed: int=0):
    np.random.seed(seed)
    _w = jnp.asarray

    def _rec_inputs():
        import jax
        import jax.numpy as jnp
        _rk = jax.random.key(seed)
        x = -0.0002928 + 1 * jax.random.normal(jax.random.fold_in(_rk, 1), (16, 128, 128), jnp.float32)
        _lenS = 128 - jax.random.randint(jax.random.fold_in(_rk, 7), (16,), 0, max(1, 128 // 4) + 1, jnp.int32)
        _lenS2 = 77 - jax.random.randint(jax.random.fold_in(_rk, 8), (16,), 0, max(1, 77 // 4) + 1, jnp.int32)
        _ctx_512P = jax.random.normal(jax.random.fold_in(_rk, 11), (16, 16, 64), jnp.float32)
        _ctx_512c = jax.random.dirichlet(jax.random.fold_in(_rk, 511), 0.3 * jnp.ones((16,), jnp.float32), (16, 77))
        _ctx_512t = jnp.einsum('bsk,bkd->bsd', _ctx_512c, _ctx_512P)
        _ctx_512t = _ctx_512t * jax.lax.rsqrt(jnp.mean(jnp.square(_ctx_512t)) + 1e-12) * 0.953939
        ctx_512 = 0.00222621 + 0.99962 * (_ctx_512t + 0.3 * jax.random.normal(jax.random.fold_in(_rk, 611), (16, 77, 64), jnp.float32))
        return (x, ctx_512)
    x, ctx_512 = _rec_inputs()

    def _L0_attn_setup():
        import jax, jax.numpy as jnp
        import numpy as np
        H = 128
        NH = 8
        DQK = H // NH
        DV = 2 * H // NH
        VDIM = 2 * H
        B, L = (2, 256)
        EPS = 1e-05
        ROPE_BASE = 10000.0

        def rope(x):
            b, t, h, d = x.shape
            inv_freq = 1.0 / ROPE_BASE ** (jnp.arange(0, d, 2, dtype=jnp.float32) / d)
            ang = jnp.arange(t, dtype=jnp.float32)[:, None] * inv_freq[None, :]
            cos = jnp.cos(ang)[None, :, None, :]
            sin = jnp.sin(ang)[None, :, None, :]
            xp = x.reshape(b, t, h, d // 2, 2)
            x0, x1 = (xp[..., 0], xp[..., 1])
            out = jnp.stack([x0 * cos - x1 * sin, x1 * cos + x0 * sin], axis=-1)
            return out.reshape(b, t, h, d).astype(x.dtype)
        key = jax.random.key(seed)
        ks = jax.random.split(key, 6)

        def w(k, shape):
            lim = 2 ** (-2.5) * np.sqrt(6.0 / (shape[0] + shape[1]))
            return jax.random.uniform(k, shape, jnp.float32, -lim, lim)
        return {'hidden_states': jax.random.normal(ks[0], (B, L, H), jnp.float32), 'Wq': w(ks[1], (H, H)), 'Wk': w(ks[2], (H, H)), 'Wv': w(ks[3], (H, VDIM)), 'Wg': w(ks[4], (H, VDIM)), 'Wo': w(ks[5], (VDIM, H)), 'g_norm_w': jnp.ones((DV,), jnp.float32)}
    _L0_attn_all = _L0_attn_setup()
    _L0_attn_in = {k: v for k, v in _L0_attn_all.items() if k in ('Wq', 'Wk', 'Wv', 'Wg', 'Wo', 'g_norm_w')}
    del _L0_attn_all

    def _L0_xattn_setup():
        import jax, jax.numpy as jnp
        import numpy as np
        H, D, C1, C2, S, M, B, W = (16, 32, 128, 64, 256, 64, 2, 4)

        def _ln(x, g, b):
            m = jnp.mean(x, -1, keepdims=True)
            v = jnp.var(x, -1, keepdims=True)
            return (x - m) * jax.lax.rsqrt(v + 1e-05) * g + b

        def _mha(x, y, wq, wk, wv, li1_w, li1_b, lnx_g, lnx_b, lny_g, lny_b, ln3_g, ln3_b, li2_w, li2_b, li3_w, li3_b, causal):
            xn = _ln(x, lnx_g, lnx_b)
            yn = _ln(y, lny_g, lny_b)
            q = jnp.einsum('bsc,hcd->bhsd', xn, wq)
            k = jnp.einsum('btc,hcd->bhtd', yn, wk)
            v = jnp.einsum('btc,hcd->bhtd', yn, wv)
            a = jax.nn.softmax(jnp.einsum('bhsd,bhtd->bhst', q, k) * D ** (-0.5), axis=-1)
            if causal:
                s, t = (a.shape[-2], a.shape[-1])
                mask = (jnp.arange(t)[None, :] > jnp.arange(s)[:, None]).astype(a.dtype)
                a = a * mask
            o = jnp.einsum('bhst,bhtd->bhsd', a, v)
            o = o.transpose(0, 2, 1, 3).reshape(x.shape[0], x.shape[1], H * D)
            x_out = x + o @ li1_w + li1_b
            h = jax.nn.gelu(_ln(x_out, ln3_g, ln3_b) @ li2_w + li2_b, approximate=False)
            return x_out + h @ li3_w + li3_b
        key = jax.random.key(seed)
        ks = iter(jax.random.split(key, 64))

        def w(shape, scale=0.02):
            return jax.random.normal(next(ks), shape, jnp.float32) * scale
        inp = {'xx': jax.random.normal(next(ks), (B, S, C1), jnp.float32), 'ee': jax.random.normal(next(ks), (B, M, C2), jnp.float32), 'ln1_g': jnp.ones(C1, jnp.float32), 'ln1_b': jnp.zeros(C1, jnp.float32), 'ln2_g': jnp.ones(C1, jnp.float32), 'ln2_b': jnp.zeros(C1, jnp.float32)}
        for pfx, cy in (('a1', C1), ('a2', C2)):
            inp[pfx + '_wq'] = w((H, C1, D))
            inp[pfx + '_wk'] = w((H, cy, D))
            inp[pfx + '_wv'] = w((H, cy, D))
            inp[pfx + '_li1_w'] = w((H * D, C1))
            inp[pfx + '_li1_b'] = jnp.zeros(C1, jnp.float32)
            inp[pfx + '_lnx_g'] = jnp.ones(C1, jnp.float32)
            inp[pfx + '_lnx_b'] = jnp.zeros(C1, jnp.float32)
            inp[pfx + '_lny_g'] = jnp.ones(cy, jnp.float32)
            inp[pfx + '_lny_b'] = jnp.zeros(cy, jnp.float32)
            inp[pfx + '_ln3_g'] = jnp.ones(C1, jnp.float32)
            inp[pfx + '_ln3_b'] = jnp.zeros(C1, jnp.float32)
            inp[pfx + '_li2_w'] = w((C1, C1 * W))
            inp[pfx + '_li2_b'] = jnp.zeros(C1 * W, jnp.float32)
            inp[pfx + '_li3_w'] = w((C1 * W, C1))
            inp[pfx + '_li3_b'] = jnp.zeros(C1, jnp.float32)
        inp['training'] = 0
        return inp
    _L0_xattn_all = _L0_xattn_setup()
    _L0_xattn_in = {k: v for k, v in _L0_xattn_all.items() if k in ('ln1_g', 'ln1_b', 'ln2_g', 'ln2_b', 'a1_wq', 'a1_wk', 'a1_wv', 'a1_li1_w', 'a1_li1_b', 'a1_lnx_g', 'a1_lnx_b', 'a1_lny_g', 'a1_lny_b', 'a1_ln3_g', 'a1_ln3_b', 'a1_li2_w', 'a1_li2_b', 'a1_li3_w', 'a1_li3_b', 'a2_wq', 'a2_wk', 'a2_wv', 'a2_li1_w', 'a2_li1_b', 'a2_lnx_g', 'a2_lnx_b', 'a2_lny_g', 'a2_lny_b', 'a2_ln3_g', 'a2_ln3_b', 'a2_li2_w', 'a2_li2_b', 'a2_li3_w', 'a2_li3_b')}
    del _L0_xattn_all

    def _L0_ffn_setup():
        import jax, jax.numpy as jnp
        import numpy as np
        S, B, H, I, E = (64, 2, 128, 352, 8)
        key = jax.random.key(seed)
        ks = jax.random.split(key, 5)
        return {'hidden_states': jax.random.normal(ks[0], (S, B, H), dtype=jnp.float32), 'router_w': jax.random.normal(ks[1], (E, H), dtype=jnp.float32) * 0.02, 'gate_w': jax.random.normal(ks[2], (E, I, H), dtype=jnp.float32) * 0.02, 'up_w': jax.random.normal(ks[3], (E, I, H), dtype=jnp.float32) * 0.02, 'down_w': jax.random.normal(ks[4], (E, H, I), dtype=jnp.float32) * 0.02}
    _L0_ffn_all = _L0_ffn_setup()
    _L0_ffn_in = {k: v for k, v in _L0_ffn_all.items() if k in ('router_w', 'gate_w', 'up_w', 'down_w')}
    del _L0_ffn_all
    return {'x': x, 'ctx_512': ctx_512, 'L0_attn_Wq': _L0_attn_in['Wq'], 'L0_attn_Wk': _L0_attn_in['Wk'], 'L0_attn_Wv': _L0_attn_in['Wv'], 'L0_attn_Wg': _L0_attn_in['Wg'], 'L0_attn_Wo': _L0_attn_in['Wo'], 'L0_attn_g_norm_w': _L0_attn_in['g_norm_w'], 'L0_xattn_ln1_g': _L0_xattn_in['ln1_g'], 'L0_xattn_ln1_b': _L0_xattn_in['ln1_b'], 'L0_xattn_ln2_g': _L0_xattn_in['ln2_g'], 'L0_xattn_ln2_b': _L0_xattn_in['ln2_b'], 'L0_xattn_a1_wq': _L0_xattn_in['a1_wq'], 'L0_xattn_a1_wk': _L0_xattn_in['a1_wk'], 'L0_xattn_a1_wv': _L0_xattn_in['a1_wv'], 'L0_xattn_a1_li1_w': _L0_xattn_in['a1_li1_w'], 'L0_xattn_a1_li1_b': _L0_xattn_in['a1_li1_b'], 'L0_xattn_a1_lnx_g': _L0_xattn_in['a1_lnx_g'], 'L0_xattn_a1_lnx_b': _L0_xattn_in['a1_lnx_b'], 'L0_xattn_a1_lny_g': _L0_xattn_in['a1_lny_g'], 'L0_xattn_a1_lny_b': _L0_xattn_in['a1_lny_b'], 'L0_xattn_a1_ln3_g': _L0_xattn_in['a1_ln3_g'], 'L0_xattn_a1_ln3_b': _L0_xattn_in['a1_ln3_b'], 'L0_xattn_a1_li2_w': _L0_xattn_in['a1_li2_w'], 'L0_xattn_a1_li2_b': _L0_xattn_in['a1_li2_b'], 'L0_xattn_a1_li3_w': _L0_xattn_in['a1_li3_w'], 'L0_xattn_a1_li3_b': _L0_xattn_in['a1_li3_b'], 'L0_xattn_a2_wq': _L0_xattn_in['a2_wq'], 'L0_xattn_a2_wk': _L0_xattn_in['a2_wk'], 'L0_xattn_a2_wv': _L0_xattn_in['a2_wv'], 'L0_xattn_a2_li1_w': _L0_xattn_in['a2_li1_w'], 'L0_xattn_a2_li1_b': _L0_xattn_in['a2_li1_b'], 'L0_xattn_a2_lnx_g': _L0_xattn_in['a2_lnx_g'], 'L0_xattn_a2_lnx_b': _L0_xattn_in['a2_lnx_b'], 'L0_xattn_a2_lny_g': _L0_xattn_in['a2_lny_g'], 'L0_xattn_a2_lny_b': _L0_xattn_in['a2_lny_b'], 'L0_xattn_a2_ln3_g': _L0_xattn_in['a2_ln3_g'], 'L0_xattn_a2_ln3_b': _L0_xattn_in['a2_ln3_b'], 'L0_xattn_a2_li2_w': _L0_xattn_in['a2_li2_w'], 'L0_xattn_a2_li2_b': _L0_xattn_in['a2_li2_b'], 'L0_xattn_a2_li3_w': _L0_xattn_in['a2_li3_w'], 'L0_xattn_a2_li3_b': _L0_xattn_in['a2_li3_b'], 'L0_ffn_router_w': _L0_ffn_in['router_w'], 'L0_ffn_gate_w': _L0_ffn_in['gate_w'], 'L0_ffn_up_w': _L0_ffn_in['up_w'], 'L0_ffn_down_w': _L0_ffn_in['down_w']}

def reference(x, ctx_512, L0_attn_Wq, L0_attn_Wk, L0_attn_Wv, L0_attn_Wg, L0_attn_Wo, L0_attn_g_norm_w, L0_xattn_ln1_g, L0_xattn_ln1_b, L0_xattn_ln2_g, L0_xattn_ln2_b, L0_xattn_a1_wq, L0_xattn_a1_wk, L0_xattn_a1_wv, L0_xattn_a1_li1_w, L0_xattn_a1_li1_b, L0_xattn_a1_lnx_g, L0_xattn_a1_lnx_b, L0_xattn_a1_lny_g, L0_xattn_a1_lny_b, L0_xattn_a1_ln3_g, L0_xattn_a1_ln3_b, L0_xattn_a1_li2_w, L0_xattn_a1_li2_b, L0_xattn_a1_li3_w, L0_xattn_a1_li3_b, L0_xattn_a2_wq, L0_xattn_a2_wk, L0_xattn_a2_wv, L0_xattn_a2_li1_w, L0_xattn_a2_li1_b, L0_xattn_a2_lnx_g, L0_xattn_a2_lnx_b, L0_xattn_a2_lny_g, L0_xattn_a2_lny_b, L0_xattn_a2_ln3_g, L0_xattn_a2_ln3_b, L0_xattn_a2_li2_w, L0_xattn_a2_li2_b, L0_xattn_a2_li3_w, L0_xattn_a2_li3_b, L0_ffn_router_w, L0_ffn_gate_w, L0_ffn_up_w, L0_ffn_down_w):
    import jax
    import jax.numpy as jnp

    def _L0_attn_ref(hidden_states, Wq, Wk, Wv, Wg, Wo, g_norm_w):
        import jax, jax.numpy as jnp
        import numpy as np
        H = 128
        NH = 8
        DQK = H // NH
        DV = 2 * H // NH
        VDIM = 2 * H
        B, L = (2, 256)
        EPS = 1e-05
        ROPE_BASE = 10000.0

        def rope(x):
            b, t, h, d = x.shape
            inv_freq = 1.0 / ROPE_BASE ** (jnp.arange(0, d, 2, dtype=jnp.float32) / d)
            ang = jnp.arange(t, dtype=jnp.float32)[:, None] * inv_freq[None, :]
            cos = jnp.cos(ang)[None, :, None, :]
            sin = jnp.sin(ang)[None, :, None, :]
            xp = x.reshape(b, t, h, d // 2, 2)
            x0, x1 = (xp[..., 0], xp[..., 1])
            out = jnp.stack([x0 * cos - x1 * sin, x1 * cos + x0 * sin], axis=-1)
            return out.reshape(b, t, h, d).astype(x.dtype)
        b, l, _ = hidden_states.shape
        q = (hidden_states @ Wq).reshape(b, l, NH, DQK)
        k = (hidden_states @ Wk).reshape(b, l, NH, DQK)
        v = (hidden_states @ Wv).reshape(b, l, NH, DV)
        q = rope(q)
        k = rope(k)
        q = jnp.transpose(q, (0, 2, 1, 3)).astype(jnp.float32)
        k = jnp.transpose(k, (0, 2, 1, 3)).astype(jnp.float32)
        v = jnp.transpose(v, (0, 2, 1, 3)).astype(jnp.float32)
        s = jnp.log2(1.0 - jnp.exp2(-5.0 - jnp.arange(NH, dtype=jnp.float32)))
        pos = jnp.arange(l, dtype=jnp.float32)
        diff = pos[:, None] - pos[None, :]
        decay = jnp.where(diff >= 0, jnp.exp2(diff[None] * s[:, None, None]), 0.0)
        scores = jnp.einsum('bhqd,bhkd,hqk->bhqk', q * DQK ** (-0.5), k, decay)
        o = jnp.einsum('bhqk,bhkd->bhqd', scores, v)
        o = jnp.transpose(o, (0, 2, 1, 3))
        o = o * jax.lax.rsqrt(jnp.mean(o * o, axis=-1, keepdims=True) + EPS) * g_norm_w
        g = hidden_states @ Wg
        o = o.reshape(b, l, VDIM) * (g * jax.nn.sigmoid(g))
        return o @ Wo

    def _L0_xattn_ref(xx, ee, ln1_g, ln1_b, ln2_g, ln2_b, a1_wq, a1_wk, a1_wv, a1_li1_w, a1_li1_b, a1_lnx_g, a1_lnx_b, a1_lny_g, a1_lny_b, a1_ln3_g, a1_ln3_b, a1_li2_w, a1_li2_b, a1_li3_w, a1_li3_b, a2_wq, a2_wk, a2_wv, a2_li1_w, a2_li1_b, a2_lnx_g, a2_lnx_b, a2_lny_g, a2_lny_b, a2_ln3_g, a2_ln3_b, a2_li2_w, a2_li2_b, a2_li3_w, a2_li3_b, training):
        import jax, jax.numpy as jnp
        import numpy as np
        H, D, C1, C2, S, M, B, W = (16, 32, 128, 64, 256, 64, 2, 4)

        def _ln(x, g, b):
            m = jnp.mean(x, -1, keepdims=True)
            v = jnp.var(x, -1, keepdims=True)
            return (x - m) * jax.lax.rsqrt(v + 1e-05) * g + b

        def _mha(x, y, wq, wk, wv, li1_w, li1_b, lnx_g, lnx_b, lny_g, lny_b, ln3_g, ln3_b, li2_w, li2_b, li3_w, li3_b, causal):
            xn = _ln(x, lnx_g, lnx_b)
            yn = _ln(y, lny_g, lny_b)
            q = jnp.einsum('bsc,hcd->bhsd', xn, wq)
            k = jnp.einsum('btc,hcd->bhtd', yn, wk)
            v = jnp.einsum('btc,hcd->bhtd', yn, wv)
            a = jax.nn.softmax(jnp.einsum('bhsd,bhtd->bhst', q, k) * D ** (-0.5), axis=-1)
            if causal:
                s, t = (a.shape[-2], a.shape[-1])
                mask = (jnp.arange(t)[None, :] > jnp.arange(s)[:, None]).astype(a.dtype)
                a = a * mask
            o = jnp.einsum('bhst,bhtd->bhsd', a, v)
            o = o.transpose(0, 2, 1, 3).reshape(x.shape[0], x.shape[1], H * D)
            x_out = x + o @ li1_w + li1_b
            h = jax.nn.gelu(_ln(x_out, ln3_g, ln3_b) @ li2_w + li2_b, approximate=False)
            return x_out + h @ li3_w + li3_b
        x = _ln(xx, ln1_g, ln1_b)
        x = x + _mha(x, x, a1_wq, a1_wk, a1_wv, a1_li1_w, a1_li1_b, a1_lnx_g, a1_lnx_b, a1_lny_g, a1_lny_b, a1_ln3_g, a1_ln3_b, a1_li2_w, a1_li2_b, a1_li3_w, a1_li3_b, causal=True)
        x = _ln(x, ln2_g, ln2_b)
        return x + _mha(x, ee, a2_wq, a2_wk, a2_wv, a2_li1_w, a2_li1_b, a2_lnx_g, a2_lnx_b, a2_lny_g, a2_lny_b, a2_ln3_g, a2_ln3_b, a2_li2_w, a2_li2_b, a2_li3_w, a2_li3_b, causal=False)

    def _L0_ffn_ref(hidden_states, router_w, gate_w, up_w, down_w):
        import jax, jax.numpy as jnp
        import numpy as np
        S, B, H, I, E = (64, 2, 128, 352, 8)
        router_logits = jnp.einsum('sbh,eh->sbe', hidden_states, router_w)
        routing_indices = jnp.argmax(router_logits, axis=-1)
        out = jnp.zeros_like(hidden_states)
        for e in range(E):
            mask = (routing_indices == e)[..., None]
            xe = jnp.where(mask, hidden_states, 0.0)
            g = jnp.einsum('sbh,ih->sbi', xe, gate_w[e])
            u = jnp.einsum('sbh,ih->sbi', xe, up_w[e])
            ye = jnp.einsum('sbi,hi->sbh', jax.nn.silu(g) * u, down_w[e])
            out = out + jnp.where(mask, ye, 0.0)
        return out
    x = _layernorm(x + _L0_attn_ref(x, L0_attn_Wq, L0_attn_Wk, L0_attn_Wv, L0_attn_Wg, L0_attn_Wo, L0_attn_g_norm_w), axis=-1)
    x = _layernorm(x + _L0_xattn_ref(x, ctx_512, L0_xattn_ln1_g, L0_xattn_ln1_b, L0_xattn_ln2_g, L0_xattn_ln2_b, L0_xattn_a1_wq, L0_xattn_a1_wk, L0_xattn_a1_wv, L0_xattn_a1_li1_w, L0_xattn_a1_li1_b, L0_xattn_a1_lnx_g, L0_xattn_a1_lnx_b, L0_xattn_a1_lny_g, L0_xattn_a1_lny_b, L0_xattn_a1_ln3_g, L0_xattn_a1_ln3_b, L0_xattn_a1_li2_w, L0_xattn_a1_li2_b, L0_xattn_a1_li3_w, L0_xattn_a1_li3_b, L0_xattn_a2_wq, L0_xattn_a2_wk, L0_xattn_a2_wv, L0_xattn_a2_li1_w, L0_xattn_a2_li1_b, L0_xattn_a2_lnx_g, L0_xattn_a2_lnx_b, L0_xattn_a2_lny_g, L0_xattn_a2_lny_b, L0_xattn_a2_ln3_g, L0_xattn_a2_ln3_b, L0_xattn_a2_li2_w, L0_xattn_a2_li2_b, L0_xattn_a2_li3_w, L0_xattn_a2_li3_b, 0), axis=-1)
    x = _layernorm(x + _L0_ffn_ref(x, L0_ffn_router_w, L0_ffn_gate_w, L0_ffn_up_w, L0_ffn_down_w), axis=-1)
    return x

_drawn_inputs = setup_inputs


def setup_inputs(seed=0):
    import zlib

    import numpy as np

    out = dict(_drawn_inputs(seed))
    spreads = {'L0_attn_g_norm_w': (1.0, 0.6),
     'L0_xattn_ln1_g': (1.0, 0.2),
     'L0_xattn_ln1_b': (0.0, 0.1),
     'L0_xattn_ln2_g': (1.0, 0.2),
     'L0_xattn_ln2_b': (0.0, 0.1),
     'L0_xattn_a1_li1_b': (0.0, 0.1),
     'L0_xattn_a1_lnx_g': (1.0, 0.6),
     'L0_xattn_a1_lnx_b': (0.0, 0.8),
     'L0_xattn_a1_lny_g': (1.0, 0.6),
     'L0_xattn_a1_lny_b': (0.0, 0.8),
     'L0_xattn_a1_ln3_g': (1.0, 0.6),
     'L0_xattn_a1_ln3_b': (0.0, 0.8),
     'L0_xattn_a1_li2_b': (0.0, 0.8),
     'L0_xattn_a1_li3_b': (0.0, 0.1),
     'L0_xattn_a2_li1_b': (0.0, 0.1),
     'L0_xattn_a2_lnx_g': (1.0, 0.6),
     'L0_xattn_a2_lnx_b': (0.0, 0.8),
     'L0_xattn_a2_lny_g': (1.0, 0.6),
     'L0_xattn_a2_lny_b': (0.0, 0.8),
     'L0_xattn_a2_ln3_g': (1.0, 0.6),
     'L0_xattn_a2_ln3_b': (0.0, 0.8),
     'L0_xattn_a2_li2_b': (0.0, 0.8),
     'L0_xattn_a2_li3_b': (0.0, 0.1)}
    factors = {'ctx_512': 4.96,
     'L0_attn_Wq': 3.801,
     'L0_attn_Wk': 3.806,
     'L0_attn_Wv': 3.764,
     'L0_attn_Wg': 3.81,
     'L0_attn_Wo': 3.81,
     'L0_xattn_a1_wq': 8.0,
     'L0_xattn_a1_wk': 8.0,
     'L0_xattn_a1_wv': 8.0,
     'L0_xattn_a1_li1_w': 8.0,
     'L0_xattn_a1_li2_w': 3.247,
     'L0_xattn_a1_li3_w': 2.927,
     'L0_xattn_a2_wq': 8.0,
     'L0_xattn_a2_wk': 8.0,
     'L0_xattn_a2_wv': 4.077,
     'L0_xattn_a2_li1_w': 4.037,
     'L0_xattn_a2_li2_w': 3.061,
     'L0_xattn_a2_li3_w': 2.778,
     'L0_ffn_router_w': 6.279,
     'L0_ffn_gate_w': 5.899,
     'L0_ffn_up_w': 5.866,
     'L0_ffn_down_w': 5.876}
    for name, (base, spread) in spreads.items():
        noise = np.random.default_rng([zlib.crc32(name.encode()), seed]).standard_normal(out[name].shape)
        drawn = base * np.exp(spread * noise) if base else spread * noise
        out[name] = jnp.asarray(drawn.astype(out[name].dtype))
    for name, factor in factors.items():
        out[name] = (out[name] * factor).astype(out[name].dtype)
    return out
```

```python
import concourse.bass as bass
import numpy as np
from concourse import mybir
from contextlib import ExitStack

F32 = mybir.dt.float32
F32R = mybir.dt.float32r
I32 = mybir.dt.int32
ACT = mybir.ActivationFunctionType
ALU = mybir.AluOpType
AX = mybir.AxisListType

B, S, C = 16, 128, 128
CT, CC = 77, 64
RH, RD, RV = 8, 16, 32
AH, AD = 16, 32
HG = AH // 4
FF = 4 * C
NE, EI = 8, 352
EC = [128, 128, 96]
NT = B + NE - 1
EPS = 1e-5


class Steps:

    def __init__(self, sem, per):
        self.sem, self.per = sem, per

    def at(self, b, k=None):
        return b * self.per + (self.per if k is None else k)


def wait(eng, steps, b, k=None):
    if isinstance(b, int) and b < 0:
        return
    eng.wait_ge(steps.sem, steps.at(b, k))


def live(b, n=B):
    return not isinstance(b, int) or 0 <= b < n


def slots(eng, slot, peel, skew, n=B):
    last = peel + (n - peel) // 2 * 2
    for t in range(peel):
        slot(t, t % 2)
    with eng.Fori(peel // 2, last // 2) as i:
        slot(i * 2, 0)
        slot(i * 2 + 1, 1)
    for t in range(last, n + skew):
        slot(t, t % 2)


def one(b):
    return bass.ds(b, 1)


def build(nc, A, out):
    ctx = ExitStack()
    with ctx:
        def sb(name, shape, dt=F32):
            return ctx.enter_context(nc.sbuf_tensor(name, shape, dt))

        def sem(name):
            return ctx.enter_context(nc.semaphore(name))

        ticks = sem("ticks")

        def free(eng):
            eng.sem_inc(ticks, 1)

        def steps(name, per=1):
            return Steps(sem(name), per)

        bank = [ctx.enter_context(nc.psum_tensor(f"bank{k}", [128, 512], F32)) for k in range(8)]
        xs_dram = nc.dram_tensor("sorted_x", [NT * S, C], F32, kind="Internal").ap()
        ys_dram = nc.dram_tensor("sorted_y", [NT * S, C], F32, kind="Internal").ap()

        xin = sb("xin", [S, B, C])
        x1 = sb("x1", [S, B, C])
        xa = sb("xa", [S, B, C])
        xo = sb("xo", [S, B, C])
        z = xin
        x3 = sb("x3", [S, B, C])
        ctxn = sb("ctxn", [CT, B, CC])

        wqk = sb("wqk", [C, 2 * RH * RD])
        wvg = sb("wvg", [C, 2 * RH * RV])
        wo = sb("wo", [128, 2, C])
        gw = sb("gw", [S, RH * RV])
        cos_t = sb("cos_t", [S, 2 * RH * RD])
        sin_t = sb("sin_t", [S, 2 * RH * RD])
        decay = sb("decay", [S, 4, 2, S])
        ident = sb("ident", [128, 128])
        att_w, mlp_w = [], []
        for a, kc in (("a1", C), ("a2", CC)):
            att_w.append({"wq": sb(a + "wq", [C, 512]), "wk": sb(a + "wk", [kc, 512]), "wv": sb(a + "wv", [kc, 512]),
                          "li1": sb(a + "li1", [128, HG, C]), "li1b": sb(a + "li1b", [S, C]),
                          "lnx": sb(a + "lnx", [C, 2]), "lny": sb(a + "lny", [kc, 2]),
                          "g": sb(a + "g", [S, C]), "b": sb(a + "b", [S, C])})
            mlp_w.append({"li2": sb(a + "li2", [C, FF]), "li2b": sb(a + "li2b", [128, 4]),
                          "li3": sb(a + "li3", [128, 4, C]), "li3b": sb(a + "li3b", [S, C]), "ln3": sb(a + "ln3", [C, 2])})
        router = sb("router", [C, NE])
        egu = sb("egu", [C, NE, 2 * EI])
        edn = sb("edn", [128, NE, 3, C])

        later = sb("later", [S, S])
        bc_f = sb("bc_f", [128, HG, 128])
        bc_sel = sb("bc_sel", [128, HG, 128], F32R)
        mhalf = sb("mhalf", [128, RH])

        ctx_in = sb("ctx_in", [CT, B, CC])
        zrow = sb("zrow", [S, C])
        rank_code = sb("rank_code", [S, NE])
        tri = sb("tri", [S, S])
        tile_at = sb("tile_at", [S, NE, B])
        tile_no = sb("tile_no", [S, NT])

        def rows(ap, n=S):
            return ap.to_broadcast((n, ap.shape[1]))

        loads_first = [("ret", wqk[:, :], A["wqk"]), ("ret", wvg[:, :], A["wvg"]), ("ret", cos_t[:, :], A["cos"]),
                       ("ret", sin_t[:, :], A["sin"]), ("ret", ident[:, :], A["ident"]), ("ret", decay[:, :, :, :], A["decay"]),
                       ("ret", wo[:, :, :], A["wo"]), ("ret", gw[:, :], rows(A["gw"])),
                       ("ctx", ctx_in[:, :, :], A["ctx"].rearrange("b t c -> t b c")),
                       ("x", xin[:, :, :], A["x"].rearrange("b s c -> s b c"))]
        loads_later = [("const", bc_f[:, :, :], A["bc_sel"]), ("a1", later[:, :], A["later"])]
        for n, a in enumerate(("a1", "a2")):
            wa, wm = att_w[n], mlp_w[n]
            loads_later += [(a, wa["wq"][:, :], A[a + "_wq"]), (a, wa["wk"][:, :], A[a + "_wk"]), (a, wa["wv"][:, :], A[a + "_wv"]),
                            (a, wa["li1"][:, :, :], A[a + "_li1"]), (a, wa["li1b"][:, :], rows(A[a + "_li1b"])),
                            (a, wa["lnx"][:, :], A[a + "_lnx"]), (a, wa["lny"][:, :], A[a + "_lny"]),
                            (a, wa["g"][:, :], rows(A[a + "_g"])), (a, wa["b"][:, :], rows(A[a + "_b"]))]
            m = "m" + a[1]
            loads_later += [(m, wm["li2"][:, :], A[a + "_li2"]), (m, wm["li2b"][:, :], A[a + "_li2b"]), (m, wm["li3"][:, :, :], A[a + "_li3"]),
                            (m, wm["li3b"][:, :], rows(A[a + "_li3b"])), (m, wm["ln3"][:, :], A[a + "_ln3"])]
        loads_later += [("exp", router[:, :], A["router"]), ("exp", egu[:, :, :], A["egu"])]
        loads_later += [("exp", edn[0:n, :, c, :], A["edn"][c * 128:c * 128 + n, :, :]) for c, n in enumerate(EC)]
        loads_later += [("exp", rank_code[:, :], rows(A["rank_code"])), ("exp", tri[:, :], A["tri"]),
                        ("exp", tile_at[:, :, :].rearrange("p a b -> p (a b)"), rows(A["tile_at"])), ("exp", tile_no[:, :], rows(A["tile_no"]))]
        ld = {k: sem("ld_" + k) for k in ("ret", "ctx", "x", "const", "a1", "m1", "a2", "m2", "exp")}
        ld_n = {k: 16 * sum(g == k for g, _, _ in loads_first + loads_later) for k in ld}
        const_ready = sem("const_ready")
        made = sem("made")
        made2 = sem("made2")
        ctx_half = sb("ctx_half", [CT, B])

        arena = sb("arena", [128, 4 * 4 * 512])
        taken = [0]

        def carve(name, shape):
            n = int(np.prod(shape[1:]))
            ap = arena[0:shape[0], taken[0]:taken[0] + n]
            taken[0] += n
            if len(shape) == 3:
                ap = ap.rearrange("p (a b) -> p a b", b=shape[2])
            if len(shape) == 4:
                ap = ap.rearrange("p (a b c) -> p a b c", b=shape[2], c=shape[3])
            return ap

        xT = [sb(f"xT{p}", [C, S]) for p in range(2)]
        rope_c = carve("rope_c", [S, 2 * RH * RD])
        rope_s = carve("rope_s", [S, 2 * RH * RD])
        qkr = [carve(f"qkr{p}", [S, 2 * RH, 32]) for p in range(2)]
        qkT = [carve(f"qkT{p}", [128, 4, S]) for p in range(2)]
        rv = [carve(f"rv{p}", [S, RH * RV]) for p in range(2)]
        rsg = carve("rsg", [S, RH * RV])
        rgate = [carve(f"rgate{p}", [S, RH * RV]) for p in range(2)]
        rprob = [carve(f"rprob{p}", [S, 4, 2, S]) for p in range(2)]
        roT = carve("roT", [128, 2 * S])
        rnat = [carve(f"rnat{p}", [S, RH * RV]) for p in range(2)]
        rsq = carve("rsq", [S, RH * RV])
        rms = [carve(f"rms{p}", [S, RH]) for p in range(2)]
        rrs = [carve(f"rrs{p}", [S, RH]) for p in range(2)]
        ry0 = carve("ry_part", [S, RH * RV])
        ry = [carve(f"ry{p}", [S, RH * RV]) for p in range(2)]
        ryT = carve("ryT", [128, 2, S])
        taken[0] = 0
        zt = [sb(f"zt{p}", [S, C]) for p in range(2)]
        st = [sb(f"st{p}", [S, 6]) for p in range(2)]
        mv = [sb(f"mv{p}", [S, 2]) for p in range(2)]
        ve = [sb(f"ve{p}", [S, 1]) for p in range(2)]
        rs = [sb(f"rs{p}", [S, 1]) for p in range(2)]
        st2 = [sb(f"st2{p}", [S, 6]) for p in range(2)]
        mv2 = [sb(f"mv2{p}", [S, 2]) for p in range(2)]
        ve2 = [sb(f"ve2{p}", [S, 1]) for p in range(2)]
        rs2 = [sb(f"rs2{p}", [S, 1]) for p in range(2)]

        xT_in = [sem(f"xT_in{p}") for p in range(2)]
        R = {k: steps("r_" + k, n) for k, n in {
            "qk": 1, "vg": 1, "rope": 3, "t4": 1, "qkT": 1, "silu": 1, "v": 1, "gate": 1, "st": 1, "prob": 4, "av": 1,
            "oT": 1, "to": 1, "nat": 2, "ms": 2, "rs": 1, "y": 2, "ty": 1, "yT": 1, "wo": 1, "ln": 5, "lnp": 1}.items()}
        bQK, bVG, bT, bO = bank[0], bank[1], bank[2], bank[3]
        bS = bank[4:8]

        def retention_sync(sp):
            def slot(t, p):
                if live(t):
                    wait(sp, R["vg"], t - 2)
                    sp.dma_start(xT[p][:, :], A["xT"][:, one(t), :]).then_inc(xT_in[p], 16)
            slots(sp, slot, 2, 0)

        def retention_tensor(pe):
            pe.wait_ge(ld["ret"], ld_n["ret"])

            def slot(t, p):
                o = 1 - p
                if live(t):
                    pe.wait_ge(xT_in[p], (t - p) * 8 + 16)
                    wait(pe, R["rope"], t - 1, 2)
                    pe.matmul(bQK[:, 0:256], xT[p][:, :], wqk[:, :], start=True, stop=True).then_inc(R["qk"].sem, 1)
                    wait(pe, R["silu"], t - 1)
                    wait(pe, R["v"], t - 1)
                    pe.matmul(bVG[:, :], xT[p][:, :], wvg[:, :], start=True, stop=True).then_inc(R["vg"].sem, 1)
                b = t - 1
                if live(b):
                    wait(pe, R["rope"], b)
                    wait(pe, R["nat"], b - 2)
                    for c in range(4):
                        src = qkr[o][:, 4 * c:4 * c + 4, :].rearrange("p a b -> p (a b)")
                        last = pe.transpose(bT[:, c * 128:(c + 1) * 128], src, ident[:, :])
                    last.then_inc(R["t4"].sem, 1)
                b = t - 2
                if live(b):
                    wait(pe, R["prob"], b)
                    wait(pe, R["v"], b)
                    wait(pe, R["ln"], b - 2, 1)
                    wait(pe, R["yT"], b - 2)
                    for c in range(2):
                        for g in range(4):
                            h = 4 * c + g
                            last = pe.matmul(bO[32 * g:32 * g + 32, c * S:(c + 1) * S], rv[p][:, h * RV:(h + 1) * RV],
                                             rprob[p][:, g, c, :], start=True, stop=True)
                    last.then_inc(R["av"].sem, 1)
                b = t - 1
                if live(b):
                    wait(pe, R["qkT"], b)
                    wait(pe, R["prob"], b - 1)
                    for c in range(2):
                        for g in range(4):
                            last = pe.matmul(bS[g][:, c * S:(c + 1) * S], qkT[o][32 * g:32 * g + RD, 2 + c, :],
                                             qkT[o][32 * g:32 * g + RD, c, :], start=True, stop=True)
                    last.then_inc(R["st"].sem, 1)
                b = t - 2
                if live(b):
                    wait(pe, R["oT"], b)
                    if live(b + 1):
                        wait(pe, R["qkT"], b + 1)
                    for c in range(2):
                        last = pe.transpose(bT[:, c * 128:(c + 1) * 128], roT[:, c * S:(c + 1) * S], ident[:, :])
                    last.then_inc(R["to"].sem, 1)
                b = t - 3
                if live(b):
                    wait(pe, R["y"], b)
                    if live(b + 1):
                        wait(pe, R["oT"], b + 1)
                    for c in range(2):
                        last = pe.transpose(bO[:, c * 128:(c + 1) * 128], ry[o][:, c * 128:(c + 1) * 128], ident[:, :])
                    last.then_inc(R["ty"].sem, 1)
                    wait(pe, R["yT"], b)
                    for c in range(2):
                        last = pe.matmul(bO[:, 256:384], ryT[:, c, :], wo[:, c, :], start=(c == 0), stop=(c == 1))
                    last.then_inc(R["wo"].sem, 1)
            slots(pe, slot, 6, 3)

        def retention_scalar(act):
            def slot(t, p):
                o = 1 - p
                if live(t):
                    wait(act, R["vg"], t)
                    wait(act, R["gate"], t - 1)
                    act.activation(rsg[:, :], bVG[:, 256:512], ACT.Silu).then_inc(R["silu"].sem, 1)
                    wait(act, R["av"], t - 2)
                    act.activation(rv[p][:, :], bVG[:, 0:256], ACT.Copy).then_inc(R["v"].sem, 1)
                b = t - 1
                if live(b):
                    wait(act, R["t4"], b)
                    wait(act, R["st"], b - 2)
                    act.activation(qkT[o][:, :, :].rearrange("p a b -> p (a b)"), bT[:, :], ACT.Copy).then_inc(R["qkT"].sem, 1)
                b = t - 2
                if live(b):
                    wait(act, R["av"], b)
                    wait(act, R["to"], b - 1)
                    act.activation(roT[:, :], bO[:, 0:256], ACT.Copy).then_inc(R["oT"].sem, 1)
                    wait(act, R["to"], b)
                    wait(act, R["y"], b - 2, 1)
                    act.activation(rnat[p][:, :], bT[:, 0:256], ACT.Copy).then_inc(R["nat"].sem, 1)
                    wait(act, R["ms"], b - 1, 1)
                    act.activation(rsq[:, :], bT[:, 0:256], ACT.Square).then_inc(R["nat"].sem, 1)
                b = t - 3
                if live(b):
                    wait(act, R["ty"], b)
                    wait(act, R["wo"], b - 1)
                    act.activation(ryT[:, :, :].rearrange("p a b -> p (a b)"), bO[:, 0:256], ACT.Copy).then_inc(R["yT"].sem, 1)
            slots(act, slot, 6, 3)

        def retention_vector(dve):
            dve.wait_ge(ld["ret"], ld_n["ret"])
            dve.wait_ge(ld["x"], ld_n["x"])

            def slot(t, p):
                o = 1 - p
                if live(t):
                    wait(dve, R["qk"], t)
                    wait(dve, R["rope"], t - 1)
                    dve.tensor_tensor(rope_c[:, :], bQK[:, 0:256], cos_t[:, :], ALU.mult).then_inc(R["rope"].sem, 1)
                    swapped = bQK[:, 0:256].rearrange("p (n two) -> p n two", two=2)[:, :, ::-1]
                    dve.tensor_tensor(rope_s[:, :].rearrange("p (n two) -> p n two", two=2), swapped,
                                      sin_t[:, :].rearrange("p (n two) -> p n two", two=2), ALU.mult).then_inc(R["rope"].sem, 1)
                b = t - 1
                if live(b):
                    wait(dve, R["st"], b)
                    wait(dve, R["av"], b - 2)
                    for g in range(4):
                        dve.tensor_tensor(rprob[o][:, g, :, :].rearrange("p a b -> p (a b)"), bS[g][:, 0:256],
                                          decay[:, g, :, :].rearrange("p a b -> p (a b)"), ALU.mult).then_inc(R["prob"].sem, 1)
                if live(t):
                    wait(dve, R["rope"], t, 2)
                    wait(dve, R["t4"], t - 2)
                    dve.tensor_tensor(qkr[p][:, :, 0:RD], rope_c[:, :].rearrange("p (a b) -> p a b", b=RD),
                                      rope_s[:, :].rearrange("p (a b) -> p a b", b=RD), ALU.add).then_inc(R["rope"].sem, 1)
                b = t - 2
                if live(b):
                    wait(dve, R["nat"], b)
                    dve.tensor_reduce(rms[p][:, :], rsq[:, :].rearrange("p (h d) -> p h d", h=RH), AX.X, ALU.add).then_inc(R["ms"].sem, 1)
                    wait(dve, R["ms"], b, 1)
                    wait(dve, R["rs"], b - 2)
                    dve.tensor_scalar(rms[p][:, :], rms[p][:, :], 1.0 / RV, EPS, ALU.mult, ALU.add).then_inc(R["ms"].sem, 1)
                b = t - 3
                if live(b):
                    wait(dve, R["wo"], b)
                    dve.tensor_tensor(zt[o][:, :], bO[:, 256:384], xin[:, one(b), :].rearrange("p a b -> p (a b)"), ALU.add)\
                       .then_inc(R["ln"].sem, 1)
                    wait(dve, R["ln"], b, 1)
                    free(dve)
                    dve.bn_stats(st[o][:, :], zt[o][:, :]).then_inc(R["ln"].sem, 1)
                    wait(dve, R["ln"], b, 2)
                    free(dve)
                    dve.bn_aggr(mv[o][:, :], st[o][:, :]).then_inc(R["ln"].sem, 1)
                    wait(dve, R["ln"], b, 3)
                    dve.tensor_scalar(ve[o][:, :], mv[o][:, 1:2], EPS, None, ALU.add).then_inc(R["ln"].sem, 1)
                b = t - 2
                if live(b):
                    wait(dve, R["rs"], b)
                    wait(dve, R["y"], b - 1)
                    rb = rrs[p][:, :].rearrange("p (h o) -> p h o", o=1).to_broadcast((S, RH, RV))
                    dve.tensor_tensor(ry0[:, :].rearrange("p (h d) -> p h d", h=RH),
                                      rnat[p][:, :].rearrange("p (h d) -> p h d", h=RH), rb, ALU.mult).then_inc(R["y"].sem, 1)
                    wait(dve, R["y"], b, 1)
                    wait(dve, R["gate"], b)
                    wait(dve, R["ty"], b - 2)
                    dve.tensor_tensor(ry[p][:, :], ry0[:, :], rgate[p][:, :], ALU.mult).then_inc(R["y"].sem, 1)
                b = t - 3
                if live(b):
                    wait(dve, R["lnp"], b)
                    dve.tensor_scalar(x1[:, one(b), :].rearrange("p a b -> p (a b)"), zt[o][:, :], mv[o][:, 0:1], rs[o][:, :],
                                      ALU.subtract, ALU.mult).then_inc(R["ln"].sem, 1)
            slots(dve, slot, 6, 3)

        def retention_gpsimd(pool):
            def slot(t, p):
                o = 1 - p
                b = t - 2
                if live(b):
                    wait(pool, R["ms"], b)
                    pool.tensor_tensor(rrs[p][:, :], rms[p][:, :], mhalf[:, :], ALU.pow).then_inc(R["rs"].sem, 1)
                b = t - 3
                if live(b):
                    wait(pool, R["ln"], b, 4)
                    pool.tensor_tensor(rs[o][:, :], ve[o][:, :], mhalf[:, 0:1], ALU.pow).then_inc(R["lnp"].sem, 1)
                if live(t):
                    wait(pool, R["silu"], t)
                    wait(pool, R["y"], t - 2)
                    pool.tensor_tensor(rgate[p][:, :], rsg[:, :], gw[:, :], ALU.mult).then_inc(R["gate"].sem, 1)
            slots(pool, slot, 6, 3)

        nat = [sb(f"nat{p}", [S, C]) for p in range(2)]
        cnat = [sb(f"cnat{p}", [CT, CC]) for p in range(2)]
        lnt = sb("lnt", [S, C])
        xnT = sb("xnT", [C, S])
        ynT = sb("ynT", [C, S])
        cnT = sb("cnT", [CC, CT])
        qT = [sb(f"qT{p}", [128, 512]) for p in range(2)]
        kT = [sb(f"kT{p}", [128, 512]) for p in range(2)]
        vv = [sb(f"vv{p}", [S, 512]) for p in range(2)]
        E = [carve(f"E{p}", [S, 4, 512]) for p in range(2)]
        ET = carve("ET", [S, 4, 512])
        mx = [sb(f"mx{p}", [S, 4, HG]) for p in range(2)]
        den = [sb(f"den{p}", [S, 4, HG]) for p in range(2)]
        rden = sb("rden", [S, 4, HG])
        parts = sb("parts", [S, 4, 32])
        partsT = sb("partsT", [128, S], F32R)
        rbs = sb("rbs", [128, 512])
        oN = sb("oN", [128, 512])
        r1 = [sb(f"r1{p}", [S, C]) for p in range(2)]

        def attention(name, w, src, self_attention, before):
            TK, KC = (S, C) if self_attention else (CT, CC)
            keysT = ynT if self_attention else cnT
            P = {k: steps(name + "_" + k, n) for k, n in {
                "ln": 9, "lnp": 2, "cn": 1, "t": 1, "xy": 2, "q": 1, "qe": 1, "k": 1, "ke": 1, "v": 1, "ve": 1, "s": 1, "max": 4,
                "exp": 4, "et": 4, "ete": 4, "rd": 3, "rt": 1, "rte": 1, "av": 1, "rb": 1, "rbe": 1, "mul": 1, "li": 1, "res": 1,
                "r1": 1}.items()}
            if self_attention:
                del P["cn"]
            bQ, bK, bO, bE = bank[0], bank[1], bank[2], bank[3]
            bS = bank[4:8]

            def enter(eng):
                for s in before:
                    eng.wait_ge(s.sem, s.at(B - 1))

            def tensor(pe):
                enter(pe)
                pe.wait_ge(ld[name], ld_n[name])

                def normed(b, o):
                    wait(pe, P["ln"], b)
                    wait(pe, P["ke"], b - 1)
                    free(pe)
                    last = pe.transpose(bK[:, 0:S], nat[o][:, :], ident[:, :])
                    if not self_attention:
                        wait(pe, P["cn"], b)
                        free(pe)
                        last = pe.transpose(bK[0:CC, S:S + CT], cnat[o][:, :], ident[0:CT, 0:CT])
                    last.then_inc(P["t"].sem, 1)

                def scores(b, p, groups):
                    if groups[0] == 0:
                        wait(pe, P["qe"], b)
                        wait(pe, P["ke"], b)
                        wait(pe, P["exp"], b - 1)
                    for hg in groups:
                        for g in range(4):
                            last = pe.matmul(bS[g][:, hg * TK:(hg + 1) * TK], qT[p][32 * g:32 * g + 32, hg * S:(hg + 1) * S],
                                             kT[p][32 * g:32 * g + 32, hg * TK:(hg + 1) * TK], start=True, stop=True)
                    if groups[-1] == HG - 1:
                        last.then_inc(P["s"].sem, 1)

                def exp_transposed(b, o, g):
                    pe.wait_ge(P["exp"].sem, P["exp"].at(b, g + 1))
                    if g:
                        wait(pe, P["ete"], b, g)
                    else:
                        wait(pe, P["rbe"], b - 1)
                    free(pe)
                    for hg in range(HG):
                        last = pe.transpose(bE[0:TK, hg * S:(hg + 1) * S], E[o][:, g, hg * TK:(hg + 1) * TK], ident[:, :])
                    last.then_inc(P["et"].sem, 1)

                def slot(t, p):
                    o = 1 - p
                    if live(t - 1):
                        normed(t - 1, o)
                    if live(t - 2):
                        scores(t - 2, p, [0, 1])
                    if live(t - 3):
                        exp_transposed(t - 3, o, 0)
                    b = t - 1
                    if live(b):
                        wait(pe, P["xy"], b)
                        wait(pe, P["ve"], b - 1)
                        for hg in range(HG):
                            last = pe.matmul(bQ[:, hg * S:(hg + 1) * S], w["wq"][:, hg * 128:(hg + 1) * 128], xnT[:, :],
                                             start=True, stop=True)
                        last.then_inc(P["q"].sem, 1)
                    if live(t - 2):
                        scores(t - 2, p, [2, 3])
                    if live(t - 3):
                        exp_transposed(t - 3, o, 1)
                    if live(b):
                        for hg in range(HG):
                            last = pe.matmul(bK[:, hg * TK:(hg + 1) * TK], w["wk"][:, hg * 128:(hg + 1) * 128], keysT[0:KC, 0:TK],
                                             start=True, stop=True)
                        last.then_inc(P["k"].sem, 1)
                    if live(t - 3):
                        exp_transposed(t - 3, o, 2)
                    b = t - 4
                    if live(b):
                        wait(pe, P["mul"], b)
                        for hg in range(HG):
                            last = pe.matmul(bO[:, 0:C], oN[:, hg * S:(hg + 1) * S], w["li1"][:, hg, :],
                                             start=(hg == 0), stop=(hg == HG - 1))
                        last.then_inc(P["li"].sem, 1)
                    b = t - 1
                    if live(b):
                        wait(pe, P["qe"], b)
                        pe.matmul(bQ[0:TK, :], keysT[0:KC, 0:TK], w["wv"][:, :], start=True, stop=True).then_inc(P["v"].sem, 1)
                    b = t - 3
                    if live(b):
                        exp_transposed(b, o, 3)
                        wait(pe, P["ve"], b)
                        wait(pe, P["res"], b - 1)
                        wait(pe, P["ete"], b)
                        for hg in range(HG):
                            for g in range(4):
                                h = 4 * hg + g
                                last = pe.matmul(bO[32 * g:32 * g + 32, hg * S:(hg + 1) * S], vv[o][0:TK, h * AD:(h + 1) * AD],
                                                 ET[0:TK, g, hg * S:(hg + 1) * S], start=True, stop=True)
                        last.then_inc(P["av"].sem, 1)
                        wait(pe, P["rd"], b)
                        free(pe)
                        pe.transpose(bE[:, 0:S], parts[:, :, :].rearrange("p a b -> p (a b)"), ident[:, :]).then_inc(P["rt"].sem, 1)
                        wait(pe, P["rte"], b)
                        for hg in range(HG):
                            last = pe.matmul(bE[:, hg * S:(hg + 1) * S], bc_sel[:, hg, :], partsT[:, :], start=True, stop=True)
                        last.then_inc(P["rb"].sem, 1)
                slots(pe, slot, 6, 4)

            def scalar(act):
                enter(act)
                act.wait_ge(ld[name], ld_n[name])

                def exps(b, p, g):
                    wait(act, P["max"], b, g + 1)
                    for hg in range(HG):
                        last = act.activation(E[p][:, g, hg * TK:(hg + 1) * TK], bS[g][:, hg * TK:(hg + 1) * TK], ACT.Exp,
                                              bias=mx[p][:, g, hg:hg + 1], accum_out=den[p][:, g, hg:hg + 1])
                    last.then_inc(P["exp"].sem, 1)

                def slot(t, p):
                    o = 1 - p
                    b = t - 1
                    if live(b):
                        wait(act, P["t"], b)
                        wait(act, P["v"], b - 1)
                        act.activation(xnT[:, :], bK[:, 0:S], ACT.Identity, bias=w["lnx"][:, 1:2], scale=w["lnx"][:, 0:1])\
                           .then_inc(P["xy"].sem, 1)
                        ky = bK[0:KC, 0:S] if self_attention else bK[0:KC, S:S + CT]
                        act.activation(keysT[0:KC, 0:TK], ky, ACT.Identity, bias=w["lny"][:, 1:2], scale=w["lny"][:, 0:1])\
                           .then_inc(P["xy"].sem, 1)
                        wait(act, P["q"], b)
                        wait(act, P["s"], b - 2)
                        act.activation(qT[o][:, :], bQ[:, :], ACT.Copy, scale=AD ** -0.5).then_inc(P["qe"].sem, 1)
                    if live(t - 2):
                        wait(act, P["et"], t - 4)
                        wait(act, P["rd"], t - 4, 1)
                        exps(t - 2, p, 0)
                    if live(b):
                        wait(act, P["k"], b)
                        wait(act, P["s"], b - 2)
                        act.activation(kT[o][:, 0:HG * TK], bK[:, 0:HG * TK], ACT.Copy).then_inc(P["ke"].sem, 1)
                    if live(t - 2):
                        exps(t - 2, p, 1)
                        exps(t - 2, p, 2)
                    if live(b):
                        wait(act, P["v"], b)
                        wait(act, P["av"], b - 2)
                        act.activation(vv[o][0:TK, :], bQ[0:TK, :], ACT.Copy).then_inc(P["ve"].sem, 1)
                    if live(t - 2):
                        exps(t - 2, p, 3)
                    b = t - 3
                    if live(b):
                        wait(act, P["rb"], b)
                        wait(act, P["mul"], b - 1)
                        act.activation(rbs[:, :], bE[:, :], ACT.Copy).then_inc(P["rbe"].sem, 1)
                slots(act, slot, 6, 4)

            def vector(dve):
                enter(dve)
                dve.wait_ge(ld[name], ld_n[name])

                def maximum(b, p, g):
                    dve.tensor_reduce(mx[p][:, g, :], bS[g][:, 0:HG * TK].rearrange("p (h t) -> p h t", h=HG), AX.X, ALU.max,
                                      negate=True).then_inc(P["max"].sem, 1)

                def exp_transposed(b, g):
                    wait(dve, P["et"], b, g + 1)
                    if g == 0:
                        wait(dve, P["av"], b - 1)
                    if self_attention:
                        dve.tensor_tensor(ET[:, g, :].rearrange("p (h s) -> p h s", h=HG), bE[:, :].rearrange("p (h s) -> p h s", h=HG),
                                          later[:, :].rearrange("p (o s) -> p o s", o=1).to_broadcast((S, HG, S)), ALU.mult)\
                           .then_inc(P["ete"].sem, 1)
                    else:
                        dve.tensor_copy(ET[0:TK, g, :], bE[0:TK, :]).then_inc(P["ete"].sem, 1)

                def slot(t, p):
                    o = 1 - p
                    ln, lnp = P["ln"], P["lnp"]
                    b = t - 3
                    if live(b):
                        exp_transposed(b, 0)
                        wait(dve, P["exp"], b)
                        wait(dve, P["rd"], b - 1)
                        dve.reciprocal(rden[:, :, :], den[o][:, :, :]).then_inc(P["rd"].sem, 1)
                        wait(dve, P["rd"], b, 1)
                        wait(dve, P["rt"], b - 1)
                        dve.tensor_copy(parts[:, :, 0:HG].bitcast(F32R), rden[:, :, :]).then_inc(P["rd"].sem, 1)
                        wait(dve, P["rd"], b, 2)
                        dve.tensor_tensor(parts[:, :, 16:16 + HG].bitcast(F32R), rden[:, :, :], parts[:, :, 0:HG], ALU.subtract)\
                           .then_inc(P["rd"].sem, 1)
                    b = t
                    if live(b):
                        x_in = src[:, one(b), :].rearrange("p a b -> p (a b)")
                        x_out = xa[:, one(b), :].rearrange("p a b -> p (a b)")
                        wait(dve, ln, b - 1)
                        free(dve)
                        dve.bn_stats(st[p][:, :], x_in).then_inc(ln.sem, 1)
                        wait(dve, ln, b, 1)
                        free(dve)
                        dve.bn_aggr(mv[p][:, :], st[p][:, :]).then_inc(ln.sem, 1)
                        wait(dve, ln, b, 2)
                        dve.tensor_scalar(ve[p][:, :], mv[p][:, 1:2], EPS, None, ALU.add).then_inc(ln.sem, 1)
                        dve.scalar_tensor_tensor(lnt[:, :], x_in, mv[p][:, 0:1], w["g"][:, :], ALU.subtract, ALU.mult)\
                           .then_inc(ln.sem, 1)
                    b = t - 2
                    if live(b):
                        wait(dve, P["s"], b)
                        wait(dve, P["exp"], b - 2)
                        maximum(b, p, 0)
                        maximum(b, p, 1)
                    if live(t - 3):
                        exp_transposed(t - 3, 1)
                    if live(b):
                        maximum(b, p, 2)
                        maximum(b, p, 3)
                    b = t
                    if live(b):
                        wait(dve, lnp, b, 1)
                        wait(dve, ln, b, 4)
                        dve.scalar_tensor_tensor(x_out, lnt[:, :], rs[p][:, 0:1], w["b"][:, :], ALU.mult, ALU.add)\
                           .then_inc(ln.sem, 1)
                        wait(dve, ln, b, 5)
                        free(dve)
                        dve.bn_stats(st2[p][:, :], x_out).then_inc(ln.sem, 1)
                    if live(t - 3):
                        exp_transposed(t - 3, 2)
                    if live(b):
                        wait(dve, ln, b, 6)
                        free(dve)
                        dve.bn_aggr(mv2[p][:, :], st2[p][:, :]).then_inc(ln.sem, 1)
                        wait(dve, ln, b, 7)
                        dve.tensor_scalar(ve2[p][:, :], mv2[p][:, 1:2], EPS, None, ALU.add).then_inc(ln.sem, 1)
                    b = t - 4
                    if live(b):
                        wait(dve, P["li"], b)
                        wait(dve, P["r1"], b)
                        dve.tensor_tensor(xo[:, one(b), :].rearrange("p a b -> p (a b)"), bO[:, 0:C], r1[p][:, :], ALU.add)\
                           .then_inc(P["res"].sem, 1)
                    b = t
                    if live(b):
                        if not self_attention:
                            wait(dve, P["t"], b - 2)
                            free(dve)
                            dve.tensor_copy(cnat[p][:, :], ctxn[:, one(b), :].rearrange("p a b -> p (a b)")).then_inc(P["cn"].sem, 1)
                        wait(dve, lnp, b, 2)
                        wait(dve, P["t"], b - 2)
                        dve.tensor_scalar(nat[p][:, :], x_out, mv2[p][:, 0:1], rs2[p][:, 0:1], ALU.subtract, ALU.mult)\
                           .then_inc(ln.sem, 1)
                    b = t - 3
                    if live(b):
                        exp_transposed(b, 3)
                        wait(dve, P["rt"], b)
                        wait(dve, P["rb"], b - 1)
                        dve.tensor_copy(partsT[:, :], bE[:, 0:S]).then_inc(P["rte"].sem, 1)
                        wait(dve, P["av"], b)
                        wait(dve, P["rbe"], b)
                        wait(dve, P["li"], b - 1)
                        dve.tensor_tensor(oN[:, :], bO[:, :], rbs[:, :], ALU.mult).then_inc(P["mul"].sem, 1)
                slots(dve, slot, 6, 4)

            def gpsimd(pool):
                enter(pool)
                pool.wait_ge(ld[name], ld_n[name])

                def slot(t, p):
                    b = t
                    if live(b):
                        wait(pool, P["ln"], b, 3)
                        pool.tensor_tensor(rs[p][:, :], ve[p][:, :], mhalf[:, 0:1], ALU.pow).then_inc(P["lnp"].sem, 1)
                        wait(pool, P["ln"], b, 8)
                        pool.tensor_tensor(rs2[p][:, :], ve2[p][:, :], mhalf[:, 0:1], ALU.pow).then_inc(P["lnp"].sem, 1)
                    b = t - 2
                    if live(b):
                        wait(pool, P["res"], b - 2)
                        pool.tensor_tensor(r1[p][:, :], xa[:, one(b), :].rearrange("p a b -> p (a b)"), w["li1b"][:, :], ALU.add)\
                            .then_inc(P["r1"].sem, 1)
                slots(pool, slot, 6, 4)

            return {"tensor": tensor, "scalar": scalar, "vector": vector, "gpsimd": gpsimd, "steps": list(P.values())}

        n3T = [sb(f"n3T{p}", [C, S]) for p in range(2)]
        hT = [sb(f"hT{p}", [128, 4, S]) for p in range(2)]
        r2 = [sb(f"r2{p}", [S, C]) for p in range(2)]
        r2t = [sb(f"r2t{k}", [S, C]) for k in range(2)]

        def mlp(name, w, residuals, before):
            NR = len(residuals)
            P = {k: steps(name + "_" + k, n) for k, n in {
                "ln": 4, "lnp": 1, "t": 1, "te": 1, "up": 1, "gelu": 4, "down": 1, "fin": 1, "r2": NR}.items()}
            bT, bD = bank[0], bank[3]
            bU = bank[1:3]

            def enter(eng):
                for s in before:
                    eng.wait_ge(s.sem, s.at(B - 1))

            def tensor(pe):
                enter(pe)
                pe.wait_ge(ld[name], ld_n[name])

                def slot(t, p):
                    o = 1 - p
                    b = t - 1
                    if live(b):
                        wait(pe, P["ln"], b)
                        wait(pe, P["te"], b - 1)
                        pe.transpose(bT[:, 0:S], nat[o][:, :], ident[:, :]).then_inc(P["t"].sem, 1)
                    b = t - 3
                    if live(b):
                        wait(pe, P["gelu"], b)
                        wait(pe, P["fin"], b - 1)
                        for c in range(4):
                            last = pe.matmul(bD[:, 0:C], hT[o][:, c, :], w["li3"][:, c, :], start=(c == 0), stop=(c == 3))
                        last.then_inc(P["down"].sem, 1)
                    b = t - 2
                    if live(b):
                        wait(pe, P["te"], b)
                        wait(pe, P["gelu"], b - 2)
                        for c in range(4):
                            last = pe.matmul(bU[p][:, c * S:(c + 1) * S], w["li2"][:, c * 128:(c + 1) * 128], n3T[p][:, :],
                                             start=True, stop=True)
                        last.then_inc(P["up"].sem, 1)
                slots(pe, slot, 6, 3)

            def scalar(act):
                enter(act)
                act.wait_ge(ld[name], ld_n[name])

                def slot(t, p):
                    o = 1 - p
                    b = t - 2
                    if live(b):
                        wait(act, P["up"], b)
                        wait(act, P["down"], b - 2)
                        for c in range(4):
                            act.activation(hT[p][:, c, :], bU[p][:, c * S:(c + 1) * S], ACT.Gelu, bias=w["li2b"][:, c:c + 1])\
                               .then_inc(P["gelu"].sem, 1)
                    b = t - 1
                    if live(b):
                        wait(act, P["t"], b)
                        wait(act, P["up"], b - 2)
                        act.activation(n3T[o][:, :], bT[:, 0:S], ACT.Identity, bias=w["ln3"][:, 1:2], scale=w["ln3"][:, 0:1])\
                           .then_inc(P["te"].sem, 1)
                slots(act, slot, 6, 3)

            def vector(dve):
                enter(dve)

                def slot(t, p):
                    o = 1 - p
                    b = t
                    ln = P["ln"]
                    if live(b):
                        x_in = xo[:, one(b), :].rearrange("p a b -> p (a b)")
                        wait(dve, ln, b - 1)
                        free(dve)
                        dve.bn_stats(st[p][:, :], x_in).then_inc(ln.sem, 1)
                        wait(dve, ln, b, 1)
                        free(dve)
                        dve.bn_aggr(mv[p][:, :], st[p][:, :]).then_inc(ln.sem, 1)
                        wait(dve, ln, b, 2)
                        dve.tensor_scalar(ve[p][:, :], mv[p][:, 1:2], EPS, None, ALU.add).then_inc(ln.sem, 1)
                    b = t - 3
                    if live(b):
                        wait(dve, P["down"], b)
                        wait(dve, P["r2"], b)
                        dve.tensor_tensor(z[:, one(b), :].rearrange("p a b -> p (a b)"), bD[:, 0:C], r2[o][:, :], ALU.add)\
                           .then_inc(P["fin"].sem, 1)
                    b = t
                    if live(b):
                        wait(dve, P["lnp"], b)
                        wait(dve, P["t"], b - 2)
                        dve.tensor_scalar(nat[p][:, :], x_in, mv[p][:, 0:1], rs[p][:, 0:1], ALU.subtract, ALU.mult).then_inc(ln.sem, 1)
                slots(dve, slot, 6, 3)

            def gpsimd(pool):
                enter(pool)
                pool.wait_ge(ld[name], ld_n[name])

                def slot(t, p):
                    if live(t):
                        wait(pool, P["ln"], t, 3)
                        pool.tensor_tensor(rs[p][:, :], ve[p][:, :], mhalf[:, 0:1], ALU.pow).then_inc(P["lnp"].sem, 1)
                        wait(pool, P["fin"], t - 2)
                        wait(pool, P["r2"], t - 1)
                        acc = w["li3b"][:, :]
                        for k, r in enumerate(residuals):
                            dst = r2[p] if k == NR - 1 else r2t[k % 2]
                            pool.tensor_tensor(dst[:, :], r[:, one(t), :].rearrange("p a b -> p (a b)"), acc, ALU.add)\
                                .then_inc(P["r2"].sem, 1)
                            if k < NR - 1:
                                wait(pool, P["r2"], t, k + 1)
                            acc = dst[:, :]
                slots(pool, slot, 6, 3)

            return {"tensor": tensor, "scalar": scalar, "vector": vector, "gpsimd": gpsimd, "steps": list(P.values())}

        self_att = attention("a1", att_w[0], x1, True, list(R.values()))
        mlp1 = mlp("m1", mlp_w[0], [xa, xo], self_att["steps"])
        cross_att = attention("a2", att_w[1], z, False, mlp1["steps"])
        mlp2 = mlp("m2", mlp_w[1], [xa, xo, x1], cross_att["steps"])
        phases = [self_att, mlp1, cross_att, mlp2]

        x3T = [sb(f"x3T{p}", [C, S]) for p in range(2)]
        logit = sb("logit", [S, B, NE])
        L = {k: steps("l_" + k, n) for k, n in {"ln": 4, "lnp": 1, "x3": 1, "t": 1, "te": 1, "mm": 1, "lg": 1}.items()}

        def router_tensor(pe):
            for s in mlp2["steps"]:
                pe.wait_ge(s.sem, s.at(B - 1))
            pe.wait_ge(ld["exp"], ld_n["exp"])

            def slot(t, p):
                o = 1 - p
                b = t - 1
                if live(b):
                    wait(pe, L["ln"], b)
                    wait(pe, L["te"], b - 1)
                    pe.transpose(bank[0][:, 0:S], nat[o][:, :], ident[:, :]).then_inc(L["t"].sem, 1)
                b = t - 2
                if live(b):
                    wait(pe, L["te"], b)
                    wait(pe, L["lg"], b - 1)
                    pe.matmul(bank[1][:, 0:NE], x3T[p][:, :], router[:, :], start=True, stop=True).then_inc(L["mm"].sem, 1)
            slots(pe, slot, 4, 2)

        def router_scalar(act):
            def slot(t, p):
                o = 1 - p
                if live(t):
                    wait(act, L["ln"], t)
                    act.activation(x3[:, one(t), :].rearrange("p a b -> p (a b)"), nat[p][:, :], ACT.Copy).then_inc(L["x3"].sem, 1)
                b = t - 1
                if live(b):
                    wait(act, L["t"], b)
                    wait(act, L["mm"], b - 2)
                    act.activation(x3T[o][:, :], bank[0][:, 0:S], ACT.Copy).then_inc(L["te"].sem, 1)
            slots(act, slot, 4, 2)

        def router_vector(dve):
            for s in mlp2["steps"]:
                dve.wait_ge(s.sem, s.at(B - 1))

            def slot(t, p):
                o = 1 - p
                ln = L["ln"]
                if live(t):
                    x_in = z[:, one(t), :].rearrange("p a b -> p (a b)")
                    dve.bn_stats(st[p][:, :], x_in).then_inc(ln.sem, 1)
                    wait(dve, ln, t, 1)
                    free(dve)
                    dve.bn_aggr(mv[p][:, :], st[p][:, :]).then_inc(ln.sem, 1)
                    wait(dve, ln, t, 2)
                    dve.tensor_scalar(ve[p][:, :], mv[p][:, 1:2], EPS, None, ALU.add).then_inc(ln.sem, 1)
                b = t - 2
                if live(b):
                    wait(dve, L["mm"], b)
                    dve.tensor_copy(logit[:, one(b), :].rearrange("p a b -> p (a b)"), bank[1][:, 0:NE]).then_inc(L["lg"].sem, 1)
                if live(t):
                    wait(dve, L["lnp"], t)
                    wait(dve, L["t"], t - 2)
                    wait(dve, L["x3"], t - 2)
                    dve.tensor_scalar(nat[p][:, :], x_in, mv[p][:, 0:1], rs[p][:, 0:1], ALU.subtract, ALU.mult).then_inc(ln.sem, 1)
            slots(dve, slot, 4, 2)

        def router_gpsimd(pool):
            def slot(t, p):
                if live(t):
                    wait(pool, L["ln"], t, 3)
                    pool.tensor_tensor(rs[p][:, :], ve[p][:, :], mhalf[:, 0:1], ALU.pow).then_inc(L["lnp"].sem, 1)
            slots(pool, slot, 4, 2)

        taken[0] = 0
        lmax = sb("lmax", [S, B])
        code = carve("code", [S, B, NE])
        cmax = sb("cmax", [S, B])
        hot = carve("hot", [S, B, NE])
        ones = sb("ones", [S, S])
        tot = carve("tot", [S, NE, B])
        base_b = sb("base_b", [S, NE, B + 1])
        full = carve("full", [S, NE, B])
        ntile = sb("ntile", [S, NE])
        tend = sb("tend", [S, NE + 1])
        start_e = sb("start_e", [S, NE])
        pos = carve("pos", [S, B, NE])
        pos2 = carve("pos2", [S, B, NE])
        place_f = sb("place_f", [S, B])
        place = sb("place", [S, B], I32)
        after = carve("after", [S, NE, NT])
        eid_f = sb("eid_f", [S, NT])
        eid = sb("eid", [S, NT], I32)
        placing = sem("placing")
        placed_mm = sem("placed_mm")
        n_place = [0]
        marks = {}

        def place_vector(dve):
            def link(ins, mark=None):
                n_place[0] += 1
                ins.then_inc(placing, 1)
                dve.wait_ge(placing, n_place[0])
                if mark:
                    marks[mark] = n_place[0]

            def bc(ap, shape):
                return ap.to_broadcast(shape)

            dve.wait_ge(L["lg"].sem, L["lg"].at(B - 1))
            link(dve.tensor_reduce(lmax[:, :], logit[:, :, :], AX.X, ALU.max))
            link(dve.tensor_tensor(code[:, :, :], logit[:, :, :], bc(lmax[:, :].rearrange("p (b o) -> p b o", o=1), (S, B, NE)), ALU.is_ge))
            link(dve.tensor_tensor(code[:, :, :], code[:, :, :], bc(rank_code[:, :].rearrange("p (o e) -> p o e", o=1), (S, B, NE)), ALU.mult))
            link(dve.tensor_reduce(cmax[:, :], code[:, :, :], AX.X, ALU.max))
            link(dve.tensor_tensor(hot[:, :, :], bc(rank_code[:, :].rearrange("p (o e) -> p o e", o=1), (S, B, NE)),
                                   bc(cmax[:, :].rearrange("p (b o) -> p b o", o=1), (S, B, NE)), ALU.is_equal), "hot")
            dve.wait_ge(placed_mm, 2)
            link(dve.tensor_copy(tot[:, :, :], bank[2][:, 0:B * NE].rearrange("p (b e) -> p e b", e=NE)))
            for b in range(B):
                link(dve.tensor_tensor(base_b[:, :, b + 1:b + 2], base_b[:, :, b:b + 1], tot[:, :, b:b + 1], ALU.add))
            link(dve.tensor_tensor(full[:, :, :], bc(base_b[:, :, B:B + 1], (S, NE, B)), tile_at[:, :, :], ALU.is_gt))
            link(dve.tensor_reduce(ntile[:, :], full[:, :, :], AX.X, ALU.add))
            for e in range(NE):
                link(dve.tensor_tensor(tend[:, e + 1:e + 2], tend[:, e:e + 1], ntile[:, e:e + 1], ALU.add))
            link(dve.tensor_scalar(start_e[:, :], tend[:, 0:NE], float(S), None, ALU.mult))
            link(dve.tensor_tensor(pos[:, :, :], bank[1][:, 0:B * NE].rearrange("p (b e) -> p b e", e=NE),
                                   base_b[:, :, 0:B].rearrange("p e b -> p b e"), ALU.add))
            link(dve.tensor_tensor(pos2[:, :, :], pos[:, :, :], bc(start_e[:, :].rearrange("p (o e) -> p o e", o=1), (S, B, NE)), ALU.add))
            link(dve.tensor_tensor(pos[:, :, :], pos2[:, :, :], hot[:, :, :], ALU.mult))
            link(dve.tensor_reduce(place_f[:, :], pos[:, :, :], AX.X, ALU.add))
            link(dve.tensor_copy(place[:, :], place_f[:, :]), "place")
            link(dve.tensor_tensor(after[:, :, :], bc(tile_no[:, :].rearrange("p (o j) -> p o j", o=1), (S, NE, NT)),
                                   bc(tend[:, 1:NE + 1].rearrange("p (e o) -> p e o", o=1), (S, NE, NT)), ALU.is_ge))
            link(dve.tensor_reduce(eid_f[:, :], after[:, :, :].rearrange("p e j -> p j e"), AX.X, ALU.add))
            link(dve.tensor_scalar(eid_f[:, :], eid_f[:, :], float(NE - 1), None, ALU.min))
            link(dve.tensor_copy(eid[:, :], eid_f[:, :]), "eid")

        def place_tensor(pe):
            pe.wait_ge(placing, 5)
            hot2 = hot[:, :, :].rearrange("p b e -> p (b e)")
            pe.wait_ge(L["lg"].sem, L["lg"].at(B - 1))
            pe.matmul(bank[1][:, 0:B * NE], tri[:, :], hot2, start=True, stop=True).then_inc(placed_mm, 1)
            pe.matmul(bank[2][:, 0:B * NE], ones[:, :], hot2, start=True, stop=True).then_inc(placed_mm, 1)

        scattered, zeroed = sem("scattered"), sem("zeroed")

        def place_gpsimd(pool):
            pool.wait_ge(placing, marks["place"])
            pool.wait_ge(L["x3"].sem, L["x3"].at(B - 1))
            pool.wait_ge(zeroed, 16)
            for b in range(B):
                pool.indirect_dma_start(xs_dram, bass.IndirectOffsetOnAxis(ap=place[:, b:b + 1], axis=0), x3[:, b, :], None)\
                    .then_inc(scattered, 16)

        xt = [carve(f"xt{p}", [S, C]) for p in range(2)]
        xtT = [carve(f"xtT{p}", [C, S]) for p in range(2)]
        gs = carve("gs", [S, EI])
        he = [carve(f"he{p}", [S, EI]) for p in range(2)]
        heT = carve("heT", [128, 3, S])
        ye = [carve(f"ye{p}", [S, C]) for p in range(2)]
        X = {k: steps("x_" + k, n) for k, n in {"t": 1, "te": 1, "up": 1, "silu": 1, "h": 1, "ht": 1, "hte": 1, "dn": 1, "ye": 1}.items()}
        xt_in = [sem(f"xt_in{p}") for p in range(2)]
        y_out = [sem(f"y_out{p}") for p in range(2)]

        def experts_sync(sp):
            sp.wait_ge(scattered, 16 * B)

            def slot(t, p):
                if live(t, NT):
                    wait(sp, X["t"], t - 2)
                    sp.dma_start(xt[p][:, :], xs_dram.rearrange("(j p) c -> p j c", p=S)[:, one(t), :]).then_inc(xt_in[p], 16)
            slots(sp, slot, 4, 3, NT)

        def experts_tensor(pe):
            pe.wait_ge(placing, marks["eid"])

            def slot(t, p):
                o = 1 - p
                if live(t, NT):
                    pe.wait_ge(xt_in[p], (t - p) * 8 + 16)
                    wait(pe, X["te"], t - 1)
                    pe.transpose(bank[0][:, 0:S], xt[p][:, :], ident[:, :]).then_inc(X["t"].sem, 1)
                b = t - 2
                if live(b, NT):
                    wait(pe, X["h"], b)
                    wait(pe, X["hte"], b - 1)
                    for c, n in enumerate(EC):
                        last = pe.transpose(bank[3][0:n, c * S:(c + 1) * S], he[p][:, c * 128:c * 128 + n], ident[:, :])
                    last.then_inc(X["ht"].sem, 1)
                b = t - 1
                if live(b, NT):
                    wait(pe, X["te"], b)
                    wait(pe, X["h"], b - 1)
                    free(pe)
                    e = pe.value_load(eid[0:1, one(b)], min_val=0, max_val=NE - 1)
                    pe.matmul(bank[1][:, 0:EI], xtT[o][:, :], egu[:, one(e), 0:EI], start=True, stop=True)
                    pe.matmul(bank[2][:, 0:EI], xtT[o][:, :], egu[:, one(e), EI:2 * EI], start=True, stop=True).then_inc(X["up"].sem, 1)
                b = t - 2
                if live(b, NT):
                    wait(pe, X["hte"], b)
                    wait(pe, X["ye"], b - 1)
                    free(pe)
                    e = pe.value_load(eid[0:1, one(b)], min_val=0, max_val=NE - 1)
                    for c, n in enumerate(EC):
                        last = pe.matmul(bank[4][:, 0:C], heT[0:n, c, :], edn[0:n, one(e), c, :], start=(c == 0), stop=(c == 2))
                    last.then_inc(X["dn"].sem, 1)
            slots(pe, slot, 4, 2, NT)

        def experts_scalar(act):
            def slot(t, p):
                o = 1 - p
                if live(t, NT):
                    wait(act, X["t"], t)
                    wait(act, X["up"], t - 2)
                    act.activation(xtT[p][:, :], bank[0][:, 0:S], ACT.Copy).then_inc(X["te"].sem, 1)
                b = t - 2
                if live(b, NT):
                    wait(act, X["ht"], b)
                    wait(act, X["dn"], b - 1)
                    act.activation(heT[:, 0:2, :].rearrange("p a b -> p (a b)"), bank[3][:, 0:2 * S], ACT.Copy)
                    act.activation(heT[0:EC[2], 2, :], bank[3][0:EC[2], 2 * S:3 * S], ACT.Copy).then_inc(X["hte"].sem, 1)
                b = t - 1
                if live(b, NT):
                    wait(act, X["up"], b)
                    wait(act, X["h"], b - 1)
                    act.activation(gs[:, :], bank[1][:, 0:EI], ACT.Silu).then_inc(X["silu"].sem, 1)
            slots(act, slot, 4, 2, NT)

        def experts_vector(dve):
            def slot(t, p):
                o = 1 - p
                b = t - 1
                if live(b, NT):
                    wait(dve, X["silu"], b)
                    wait(dve, X["ht"], b - 2)
                    dve.tensor_tensor(he[o][:, :], bank[2][:, 0:EI], gs[:, :], ALU.mult).then_inc(X["h"].sem, 1)
                b = t - 2
                if live(b, NT):
                    wait(dve, X["dn"], b)
                    if not isinstance(b, int) or b >= 2:
                        dve.wait_ge(y_out[p], (b - p) * 8)
                    dve.tensor_copy(ye[p][:, :], bank[4][:, 0:C]).then_inc(X["ye"].sem, 1)
            slots(dve, slot, 4, 2, NT)

        def experts_gpsimd(pool):
            def slot(t, p):
                b = t - 2
                if live(b, NT):
                    wait(pool, X["ye"], b)
                    pool.dma_start(ys_dram.rearrange("(j p) c -> p j c", p=S)[:, one(b), :], ye[p][:, :]).then_inc(y_out[p], 16)
            slots(pool, slot, 4, 2, NT)

        yg = xa
        gathered = [sem(f"gathered{b}") for b in range(B)]
        F = {k: steps("f_" + k, n) for k, n in {"ln": 5, "lnp": 1}.items()}
        stored = sem("stored")

        def final_gpsimd(pool):
            for p in range(2):
                pool.wait_ge(y_out[p], 16 * ((NT - p + 1) // 2))
            for b in range(B):
                pool.indirect_dma_start(yg[:, b, :], None, ys_dram, bass.IndirectOffsetOnAxis(ap=place[:, b:b + 1], axis=0))\
                    .then_inc(gathered[b], 16)
            for b in range(B):
                wait(pool, F["ln"], b, 4)
                pool.tensor_tensor(rs[b % 2][:, :], ve[b % 2][:, :], mhalf[:, 0:1], ALU.pow).then_inc(F["lnp"].sem, 1)

        def final_vector(dve):
            ln = F["ln"]

            def apply(b):
                p = b % 2
                wait(dve, F["lnp"], b)
                dve.tensor_scalar(x1[:, b, :], xo[:, b, :], mv[p][:, 0:1], rs[p][:, 0:1], ALU.subtract, ALU.mult).then_inc(ln.sem, 1)

            for b in range(B):
                p = b % 2
                dve.wait_ge(gathered[b], 16)
                dve.tensor_tensor(xo[:, b, :], yg[:, b, :], x3[:, b, :], ALU.add).then_inc(ln.sem, 1)
                wait(dve, ln, b, 1)
                free(dve)
                dve.bn_stats(st[p][:, :], xo[:, b, :]).then_inc(ln.sem, 1)
                wait(dve, ln, b, 2)
                free(dve)
                dve.bn_aggr(mv[p][:, :], st[p][:, :]).then_inc(ln.sem, 1)
                wait(dve, ln, b, 3)
                dve.tensor_scalar(ve[p][:, :], mv[p][:, 1:2], EPS, None, ALU.add).then_inc(ln.sem, 1)
                apply(b)

        def final_sync(sp):
            n = 0
            for b in range(B):
                wait(sp, F["ln"], b)
                sp.dma_start(out[b, :, :], x1[:, b, :]).then_inc(stored, 16)
            sp.wait_ge(stored, 16 * B)

        cmean = sb("cmean", [CT, B])
        cvar = sb("cvar", [CT, B])
        crs = sb("crs", [CT, B])
        cdev = sb("cdev", [CT, B, CC])
        csq = sb("csq", [CT, B, CC])
        c_steps = sem("c_steps")
        c_rs = sem("c_rs")

        def setup_vector(dve):
            def link(ins, n):
                ins.then_inc(c_steps, 1)
                dve.wait_ge(c_steps, n)

            for t in (qkr[0], qkr[1]):
                dve.memset(t[:, :, :], 0.0)
            dve.memset(parts[:, :, :], 0.0)
            dve.memset(zrow[:, :], 0.0)
            dve.memset(ones[:, :], 1.0)
            dve.memset(base_b[:, :, 0:1], 0.0)
            dve.memset(tend[:, 0:1], 0.0).then_inc(made, 1)
            dve.wait_ge(made, 1)
            dve.wait_ge(ld["ctx"], ld_n["ctx"])

            def per_token(ap):
                return ap.rearrange("p (b o) -> p b o", o=1).to_broadcast((CT, B, CC))

            link(dve.tensor_reduce(cmean[:, :], ctx_in[:, :, :], AX.X, ALU.add), 1)
            link(dve.tensor_scalar(cmean[:, :], cmean[:, :], 1.0 / CC, None, ALU.mult), 2)
            link(dve.tensor_tensor(cdev[:, :, :], ctx_in[:, :, :], per_token(cmean[:, :]), ALU.subtract), 3)
            link(dve.tensor_tensor(csq[:, :, :], cdev[:, :, :], cdev[:, :, :], ALU.mult), 4)
            link(dve.tensor_reduce(cvar[:, :], csq[:, :, :], AX.X, ALU.add), 5)
            link(dve.tensor_scalar(cvar[:, :], cvar[:, :], 1.0 / CC, EPS, ALU.mult, ALU.add), 6)
            dve.wait_ge(c_rs, 1)
            link(dve.tensor_tensor(ctxn[:, :, :], cdev[:, :, :], per_token(crs[:, :]), ALU.mult), 7)

        def constants_vector(dve):
            dve.wait_ge(ld["const"], ld_n["const"])
            dve.tensor_copy(bc_sel[:, :, :], bc_f[:, :, :]).then_inc(const_ready, 1)

        block = ctx.enter_context(nc.Block())

        @block.vector
        def _(dve):
            setup_vector(dve)
            retention_vector(dve)
            constants_vector(dve)
            for phase in phases:
                phase["vector"](dve)
            router_vector(dve)
            place_vector(dve)
            experts_vector(dve)
            final_vector(dve)

        @block.sync
        def _(sp):
            def load(group, dst, src):
                sp.dma_start(dst, src).then_inc(ld[group], 16)
            for group, dst, src in loads_first:
                load(group, dst, src)
            retention_sync(sp)
            for group, dst, src in loads_later:
                load(group, dst, src)
            sp.wait_ge(made, 1)
            sp.dma_start(xs_dram.rearrange("(j p) c -> p j c", p=S),
                         zrow[:, :].rearrange("p (o c) -> p o c", o=1).to_broadcast((S, NT, C))).then_inc(zeroed, 16)
            experts_sync(sp)
            final_sync(sp)

        @block.tensor
        def _(pe):
            retention_tensor(pe)
            pe.wait_ge(const_ready, 1)
            for phase in phases:
                phase["tensor"](pe)
            router_tensor(pe)
            place_tensor(pe)
            experts_tensor(pe)

        @block.scalar
        def _(act):
            retention_scalar(act)
            for phase in phases:
                phase["scalar"](act)
            router_scalar(act)
            experts_scalar(act)

        @block.gpsimd
        def _(pool):
            pool.memset(mhalf[:, :], -0.5).then_inc(made2, 1)
            pool.memset(ctx_half[:, :], -0.5).then_inc(made2, 1)
            pool.wait_ge(made2, 2)
            pool.wait_ge(c_steps, 6)
            pool.tensor_tensor(crs[:, :], cvar[:, :], ctx_half[:, :], ALU.pow).then_inc(c_rs, 1)
            pool.wait_ge(ld["ret"], ld_n["ret"])
            retention_gpsimd(pool)
            for phase in phases:
                phase["gpsimd"](pool)
            router_gpsimd(pool)
            place_gpsimd(pool)
            experts_gpsimd(pool)
            final_gpsimd(pool)


def constants():
    f = np.float32
    inv = (f(1.0) / f(10000.0) ** (np.arange(0, RD, 2, dtype=f) / f(RD))).astype(f)
    ang = np.arange(S, dtype=f)[:, None] * inv[None, :]
    cos, sin = np.cos(ang), np.sin(ang)
    cos = np.repeat(cos, 2, axis=1)
    sin = np.stack([-sin, sin], axis=-1).reshape(S, RD)
    decay = np.zeros((S, 4, 2, S))
    diff = np.arange(S)[None, :] - np.arange(S)[:, None]
    for h in range(RH):
        slope = np.log2(1.0 - 2.0 ** (-5.0 - h))
        decay[:, h % 4, h // 4, :] = np.where(diff >= 0, np.exp2(np.maximum(diff, 0) * slope), 0.0) * RD ** -0.5
    bc = np.zeros((128, HG, 128))
    for hg in range(HG):
        for g in range(4):
            for j in (hg, 16 + hg):
                bc[32 * g + j, hg, 32 * g:32 * g + 32] = 1.0
    out = {"cos": np.tile(cos, (1, 2 * RH)), "sin": np.tile(sin, (1, 2 * RH)), "decay": decay, "ident": np.eye(128),
           "bc_sel": bc, "later": np.tril(np.ones((S, S)), -1), "tri": np.triu(np.ones((S, S)), 1),
           "rank_code": NE - np.arange(NE)[None, :], "tile_at": np.tile(S * np.arange(B), NE)[None, :], "tile_no": np.arange(NT)[None, :]}
    return {k: np.ascontiguousarray(v.astype(f)) for k, v in out.items()}


def laid_out(i):
    t = {"x": i["x"], "xT": i["x"].transpose(2, 0, 1), "ctx": i["ctx_512"],
         "wqk": np.concatenate([i["L0_attn_Wq"], i["L0_attn_Wk"]], 1), "wvg": np.concatenate([i["L0_attn_Wv"], i["L0_attn_Wg"]], 1),
         "wo": i["L0_attn_Wo"].reshape(2, 128, C).transpose(1, 0, 2), "gw": np.tile(i["L0_attn_g_norm_w"], RH)[None, :],
         "router": i["L0_ffn_router_w"].T,
         "egu": np.concatenate([i["L0_ffn_gate_w"], i["L0_ffn_up_w"]], 1).transpose(2, 0, 1),
         "edn": i["L0_ffn_down_w"].transpose(2, 0, 1)}
    for n, a in enumerate(("a1", "a2")):
        p = f"L0_xattn_{a}_"
        for k in ("wq", "wk", "wv"):
            w = i[p + k]
            t[f"{a}_{k}"] = w.transpose(1, 0, 2).reshape(w.shape[1], AH * AD)
        t[a + "_li1"] = i[p + "li1_w"].reshape(HG, 128, C).transpose(1, 0, 2)
        t[a + "_li1b"] = i[p + "li1_b"][None, :]
        for k in ("lnx", "lny", "ln3"):
            t[f"{a}_{k}"] = np.stack([i[p + k + "_g"], i[p + k + "_b"]], 1)
        t[a + "_g"] = i[f"L0_xattn_ln{n + 1}_g"][None, :]
        t[a + "_b"] = i[f"L0_xattn_ln{n + 1}_b"][None, :]
        t[a + "_li2"] = i[p + "li2_w"]
        t[a + "_li2b"] = i[p + "li2_b"].reshape(4, 128).T
        t[a + "_li3"] = i[p + "li3_w"].reshape(4, 128, C).transpose(1, 0, 2)
        t[a + "_li3b"] = i[p + "li3_b"][None, :]
    return {k: np.ascontiguousarray(v) for k, v in t.items()} | constants()


def kernel(**inputs):
    import concourse.bacc as _bacc
    from concourse.bass_utils import run_bass_kernel_spmd as _run

    arrays = laid_out({k: np.asarray(v) for k, v in inputs.items()})
    nc = _bacc.Bacc("TRN2", target_bir_lowering=False, num_devices=1)
    aps = {k: nc.dram_tensor("in_" + k, v.shape, mybir.dt.from_np(v.dtype), kind="ExternalInput").ap() for k, v in arrays.items()}
    out = nc.dram_tensor("out", (B, S, C), F32, kind="ExternalOutput").ap()
    build(nc, aps, out)
    r = _run(nc, [{"in_" + k: v for k, v in arrays.items()}], core_ids=[0])
    return r.results[0]["out"]
```

```python
import concourse.bass as bass
import numpy as np
from concourse import mybir
from contextlib import ExitStack

F32 = mybir.dt.float32
F32R = mybir.dt.float32r
I32 = mybir.dt.int32
ACT = mybir.ActivationFunctionType
ALU = mybir.AluOpType
AX = mybir.AxisListType

B, S, C = 16, 128, 128
CT, CC = 77, 64
RH, RD, RV = 8, 16, 32
AH, AD = 16, 32
HG = AH // 4
FF = 4 * C
NE, EI = 8, 352
EC = [128, 128, 96]
NT = B + NE - 1
EPS = 1e-5


class Steps:

    def __init__(self, sem, per, start=0):
        self.sem, self.per, self.start = sem, per, start

    def next_phase(self):
        return Steps(self.sem, self.per, self.start + B)

    def at(self, b, k=None):
        return (b + self.start) * self.per + (self.per if k is None else k)


def wait(eng, steps, b, k=None):
    if isinstance(b, int) and b < 0:
        return
    eng.wait_ge(steps.sem, steps.at(b, k))


def live(b, n=B):
    return not isinstance(b, int) or 0 <= b < n


def per_batch_of(n):
    def per_batch(step):
        def run(b, p, *which):
            if live(b, n):
                step(b, p, *which)
        return run
    return per_batch


per_batch = per_batch_of(B)


def slots(eng, slot, peel, skew, n=B):
    last = peel + (n - peel) // 2 * 2

    def at(t, parity):
        return lambda k: (t - k, (parity + k) % 2)
    for t in range(peel):
        slot(at(t, t % 2))
    with eng.Fori(peel // 2, last // 2) as i:
        slot(at(i * 2, 0))
        slot(at(i * 2 + 1, 1))
    for t in range(last, n + skew):
        slot(at(t, t % 2))


def one(b):
    return bass.ds(b, 1)


def build(nc, A, out):
    ctx = ExitStack()
    with ctx:
        def sb(name, shape, dt=F32):
            return ctx.enter_context(nc.sbuf_tensor(name, shape, dt))

        def sem(name):
            return ctx.enter_context(nc.semaphore(name))

        ticks = sem("ticks")

        def free(eng):
            eng.sem_inc(ticks, 1)

        def steps(name, per=1):
            return Steps(sem(name), per)

        bank = [ctx.enter_context(nc.psum_tensor(f"bank{k}", [128, 512], F32)) for k in range(8)]
        CW = C + 1
        xs_dram = nc.dram_tensor("sorted_x", [NT * S, CW], F32, kind="Internal").ap()

        xin = sb("xin", [S, B, C])
        x1 = sb("x1", [S, B, C])
        xa = sb("xa", [S, B, C])
        xo = sb("xo", [S, B, C])
        z = xin
        x3 = sb("x3", [S, B, CW])
        ctxn = sb("ctxn", [CT, B, CC])

        wqk = sb("wqk", [C, 2 * RH * RD])
        wvg = sb("wvg", [C, 2 * RH * RV])
        wo = sb("wo", [128, 2, C])
        gw = sb("gw", [S, RH * RV])
        cos_t = sb("cos_t", [S, 2 * RH * RD])
        sin_t = sb("sin_t", [S, 2 * RH * RD])
        decay = sb("decay", [S, 2, 4, S])
        ident = sb("ident", [128, 128])
        att_w, mlp_w = [], []
        for a, kc in (("a1", C), ("a2", CC)):
            att_w.append({"wq": sb(a + "wq", [C, 512]), "wk": sb(a + "wk", [kc, 512]), "wv": sb(a + "wv", [kc, 512]),
                          "li1": sb(a + "li1", [128, HG, C]), "li1b": sb(a + "li1b", [S, C]),
                          "lnx": sb(a + "lnx", [C, 2]), "lny": sb(a + "lny", [kc, 2]),
                          "g": sb(a + "g", [S, C]), "b": sb(a + "b", [S, C])})
            mlp_w.append({"li2": sb(a + "li2", [C, FF]), "li2b": sb(a + "li2b", [128, 4]),
                          "li3": sb(a + "li3", [128, 4, C]), "li3b": sb(a + "li3b", [S, C]), "ln3": sb(a + "ln3", [C, 2])})
        router = sb("router", [C, NE])
        egu = sb("egu", [C, NE, 2 * EI])
        edn = sb("edn", [128, NE, 3, C])

        later = sb("later", [S, S])
        bc_f = sb("bc_f", [128, HG, 128])
        bc_sel = sb("bc_sel", [128, HG, 128], F32R)
        mhalf = sb("mhalf", [128, RH])

        def ctx_sized(buffer, k):
            half = B * CC // C
            return buffer[0:CT, k * half:(k + 1) * half, :].rearrange("p a b -> p (a b)").rearrange("p (b c) -> p b c", c=CC)

        ctx_in, cdev, csq = ctx_sized(xa, 0), ctx_sized(xa, 1), ctx_sized(xo, 0)
        token = sb("token", [S, B], I32)
        rank_code = sb("rank_code", [S, NE])
        tri = sb("tri", [S, S])
        tile_at = sb("tile_at", [S, NE, B])
        tile_no = sb("tile_no", [S, NT])

        def rows(ap, n=S):
            return ap.to_broadcast((n, ap.shape[1]))

        loads_first = [("ret", wqk[:, :], A["wqk"]), ("ret", wvg[:, :], A["wvg"]), ("ret", cos_t[:, :], A["cos"]),
                       ("ret", sin_t[:, :], A["sin"]), ("ret", ident[:, :], A["ident"]), ("ret", decay[:, :, :, :], A["decay"]),
                       ("ret", wo[:, :, :], A["wo"]), ("ret", gw[:, :], rows(A["gw"])),
                       ("ctx", ctx_in[:, :, :], A["ctx"].rearrange("b t c -> t b c")),
                       ("x", xin[:, :, :], A["x"].rearrange("b s c -> s b c"))]
        loads_later = [("const", bc_f[:, :, :], A["bc_sel"]), ("const", token[:, :], A["token"]), ("a1", later[:, :], A["later"])]
        for n, a in enumerate(("a1", "a2")):
            wa, wm = att_w[n], mlp_w[n]
            loads_later += [(a, wa["wq"][:, :], A[a + "_wq"]), (a, wa["wk"][:, :], A[a + "_wk"]), (a, wa["wv"][:, :], A[a + "_wv"]),
                            (a, wa["li1"][:, :, :], A[a + "_li1"]), (a, wa["li1b"][:, :], rows(A[a + "_li1b"])),
                            (a, wa["lnx"][:, :], A[a + "_lnx"]), (a, wa["lny"][:, :], A[a + "_lny"]),
                            (a, wa["g"][:, :], rows(A[a + "_g"])), (a, wa["b"][:, :], rows(A[a + "_b"]))]
            m = "m" + a[1]
            loads_later += [(m, wm["li2"][:, :], A[a + "_li2"]), (m, wm["li2b"][:, :], A[a + "_li2b"]), (m, wm["li3"][:, :, :], A[a + "_li3"]),
                            (m, wm["li3b"][:, :], rows(A[a + "_li3b"])), (m, wm["ln3"][:, :], A[a + "_ln3"])]
        loads_later += [("exp", router[:, :], A["router"]), ("exp", egu[:, :, :], A["egu"])]
        loads_later += [("exp", edn[0:n, :, c, :], A["edn"][c * 128:c * 128 + n, :, :]) for c, n in enumerate(EC)]
        loads_later += [("exp", rank_code[:, :], rows(A["rank_code"])), ("exp", tri[:, :], A["tri"]),
                        ("exp", tile_at[:, :, :].rearrange("p a b -> p (a b)"), rows(A["tile_at"])), ("exp", tile_no[:, :], rows(A["tile_no"]))]
        ld = {k: sem("ld_" + k) for k in ("ret", "ctx", "x", "const", "a1", "m1", "a2", "m2", "exp")}
        ld_n = {k: 16 * sum(g == k for g, _, _ in loads_first + loads_later) for k in ld}
        const_ready = sem("const_ready")
        made = sem("made")
        made2 = sem("made2")
        ctx_half = sb("ctx_half", [CT, B])

        arena = sb("arena", [128, 4 * 4 * 512])
        taken = [0]

        def carve(name, shape):
            n = int(np.prod(shape[1:]))
            ap = arena[0:shape[0], taken[0]:taken[0] + n]
            taken[0] += n
            if len(shape) == 3:
                ap = ap.rearrange("p (a b) -> p a b", b=shape[2])
            if len(shape) == 4:
                ap = ap.rearrange("p (a b c) -> p a b c", b=shape[2], c=shape[3])
            return ap

        xT = [sb(f"xT{p}", [C, S]) for p in range(2)]
        rope_c = carve("rope_c", [S, 2 * RH * RD])
        rope_s = carve("rope_s", [S, 2 * RH * RD])
        qkr = [carve(f"qkr{p}", [S, 2 * RH, 32]) for p in range(2)]
        rkT = [carve(f"rkT{p}", [128, 2, S]) for p in range(2)]
        kd = [sb(f"kd{p}", [128, HG, 4, S]) for p in range(2)]
        rqd = [kd[p][:, 0:2, :, :] for p in range(2)]
        rv = [carve(f"rv{p}", [S, RH * RV]) for p in range(2)]
        rsg = carve("rsg", [S, RH * RV])
        rgate = [carve(f"rgate{p}", [S, RH * RV]) for p in range(2)]
        rprob = [carve(f"rprob{p}", [S, 2, 4, S]) for p in range(2)]
        roT = carve("roT", [128, 2 * S])
        rnat = [carve(f"rnat{p}", [S, RH * RV]) for p in range(2)]
        rsq = carve("rsq", [S, RH * RV])
        rms = [carve(f"rms{p}", [S, RH]) for p in range(2)]
        rrs = [carve(f"rrs{p}", [S, RH]) for p in range(2)]
        ry0 = carve("ry_part", [S, RH * RV])
        ry = [carve(f"ry{p}", [S, RH * RV]) for p in range(2)]
        ryT = carve("ryT", [128, 2, S])
        taken[0] = 0
        zt = [sb(f"zt{p}", [S, C]) for p in range(2)]
        st = [sb(f"st{p}", [S, 6]) for p in range(2)]
        mv = [sb(f"mv{p}", [S, 2]) for p in range(2)]
        ve = [sb(f"ve{p}", [S, 1]) for p in range(2)]
        rs = [sb(f"rs{p}", [S, 1]) for p in range(2)]
        st2 = [sb(f"st2{p}", [S, 6]) for p in range(2)]
        mv2 = [sb(f"mv2{p}", [S, 2]) for p in range(2)]
        ve2 = [sb(f"ve2{p}", [S, 1]) for p in range(2)]
        rs2 = [sb(f"rs2{p}", [S, 1]) for p in range(2)]

        xT_in = [sem(f"xT_in{p}") for p in range(2)]
        R = {k: steps("r_" + k, n) for k, n in {
            "qk": 1, "vg": 1, "rope": 3, "t4": 1, "qkT": 5, "silu": 1, "v": 1, "gate": 1, "st": 2, "prob": 2, "av": 1,
            "oT": 1, "to": 1, "nat": 2, "ms": 2, "rs": 1, "y": 2, "ty": 1, "yT": 1, "wo": 1, "ln": 4, "lnp": 1, "x1": 1}.items()}
        bQK, bVG, bT, bY = bank[0], bank[1], bank[2], bank[3]
        bS, bA, bN = bank[4:6], bank[6], bank[7]

        def retention_sync(sp):
            @per_batch
            def load_xT(b, p):
                wait(sp, R["vg"], b - 2)
                sp.dma_start(xT[p][:, :], A["xT"][:, one(b), :]).then_inc(xT_in[p], 16)

            slots(sp, lambda at: load_xT(*at(0)), 2, 0)

        def retention_tensor(pe):
            pe.wait_ge(ld["ret"], ld_n["ret"])

            @per_batch
            def project_qk(b, p):
                pe.wait_ge(xT_in[p], (b - p) * 8 + 16)
                wait(pe, R["rope"], b - 1, 2)
                pe.matmul(bQK[:, 0:256], xT[p][:, :], wqk[:, :], start=True, stop=True).then_inc(R["qk"].sem, 1)

            @per_batch
            def project_vg(b, p):
                wait(pe, R["silu"], b - 1)
                wait(pe, R["v"], b - 1)
                pe.matmul(bVG[:, :], xT[p][:, :], wvg[:, :], start=True, stop=True).then_inc(R["vg"].sem, 1)

            @per_batch
            def transpose_qk(b, p):
                wait(pe, R["rope"], b)
                wait(pe, R["qkT"], b - 1)
                for c in range(4):
                    src = qkr[p][:, 4 * c:4 * c + 4, :].rearrange("p a b -> p (a b)")
                    last = pe.transpose(bT[:, c * 128:(c + 1) * 128], src, ident[:, :])
                last.then_inc(R["t4"].sem, 1)

            @per_batch
            def scores(b, p, c):
                wait(pe, R["qkT"], b)
                wait(pe, R["prob"], b - 1, c + 1)
                pe.matmul(bS[c][:, :], rkT[p][:, c, :], rqd[p][:, c, :, :].rearrange("p a b -> p (a b)"),
                          start=True, stop=True).then_inc(R["st"].sem, 1)

            @per_batch
            def weighted_values(b, p):
                wait(pe, R["prob"], b)
                wait(pe, R["v"], b)
                wait(pe, R["oT"], b - 1)
                for c in range(2):
                    for g in range(4):
                        h = 4 * c + g
                        last = pe.matmul(bA[32 * g:32 * g + 32, c * S:(c + 1) * S], rv[p][:, h * RV:(h + 1) * RV],
                                         rprob[p][:, c, g, :], start=True, stop=True)
                last.then_inc(R["av"].sem, 1)

            @per_batch
            def transpose_o(b, p):
                wait(pe, R["oT"], b)
                wait(pe, R["nat"], b - 1)
                for c in range(2):
                    last = pe.transpose(bN[:, c * 128:(c + 1) * 128], roT[:, c * S:(c + 1) * S], ident[:, :])
                last.then_inc(R["to"].sem, 1)

            @per_batch
            def transpose_y(b, p):
                wait(pe, R["y"], b)
                wait(pe, R["ln"], b - 1, 1)
                for c in range(2):
                    last = pe.transpose(bY[:, c * 128:(c + 1) * 128], ry[p][:, c * 128:(c + 1) * 128], ident[:, :])
                last.then_inc(R["ty"].sem, 1)

            @per_batch
            def project_out(b, p):
                wait(pe, R["yT"], b)
                for c in range(2):
                    last = pe.matmul(bY[:, 256:384], ryT[:, c, :], wo[:, c, :], start=(c == 0), stop=(c == 1))
                last.then_inc(R["wo"].sem, 1)

            def slot(at):
                project_vg(*at(1))
                transpose_o(*at(3))
                scores(*at(2), 0)
                transpose_y(*at(4))
                scores(*at(2), 1)
                transpose_qk(*at(1))
                project_out(*at(4))
                project_qk(*at(0))
                weighted_values(*at(2))
            slots(pe, slot, 6, 4)

        def retention_scalar(act):
            @per_batch
            def gate_silu(b, p):
                wait(act, R["vg"], b)
                wait(act, R["gate"], b - 1)
                act.activation(rsg[:, :], bVG[:, 256:512], ACT.Silu).then_inc(R["silu"].sem, 1)

            @per_batch
            def values(b, p):
                wait(act, R["vg"], b)
                wait(act, R["av"], b - 2)
                act.activation(rv[p][:, :], bVG[:, 0:256], ACT.Copy).then_inc(R["v"].sem, 1)

            @per_batch
            def qk_transposed(b, p):
                wait(act, R["t4"], b)
                wait(act, R["st"], b - 2)
                for g in range(4):
                    rows_g = slice(32 * g, 32 * g + 32)
                    act.activation(rqd[p][rows_g, :, g, :], bT[rows_g, 0:2 * S].rearrange("p (c s) -> p c s", c=2), ACT.Copy)\
                       .then_inc(R["qkT"].sem, 1)
                act.activation(rkT[p][:, :, :].rearrange("p a b -> p (a b)"), bT[:, 2 * S:4 * S], ACT.Copy).then_inc(R["qkT"].sem, 1)

            @per_batch
            def o_transposed(b, p):
                wait(act, R["av"], b)
                wait(act, R["to"], b - 1)
                act.activation(roT[:, :], bA[:, 0:256], ACT.Copy).then_inc(R["oT"].sem, 1)

            @per_batch
            def o_natural(b, p):
                wait(act, R["to"], b)
                wait(act, R["y"], b - 2, 1)
                act.activation(rnat[p][:, :], bN[:, 0:256], ACT.Copy).then_inc(R["nat"].sem, 1)

            @per_batch
            def o_squared(b, p):
                wait(act, R["ms"], b - 1, 1)
                act.activation(rsq[:, :], bN[:, 0:256], ACT.Square).then_inc(R["nat"].sem, 1)

            @per_batch
            def y_transposed(b, p):
                wait(act, R["ty"], b)
                wait(act, R["wo"], b - 1)
                act.activation(ryT[:, :, :].rearrange("p a b -> p (a b)"), bY[:, 0:256], ACT.Copy).then_inc(R["yT"].sem, 1)

            def slot(at):
                o_squared(*at(2))
                values(*at(0))
                gate_silu(*at(0))
                y_transposed(*at(3))
                qk_transposed(*at(0))
                o_transposed(*at(1))
                o_natural(*at(1))
            slots(act, slot, 6, 4)

        def retention_vector(dve):
            dve.wait_ge(ld["ret"], ld_n["ret"])
            dve.wait_ge(ld["x"], ld_n["x"])

            @per_batch
            def rotate(b, p):
                wait(dve, R["qk"], b)
                wait(dve, R["rope"], b - 1)
                dve.tensor_tensor(rope_c[:, :], bQK[:, 0:256], cos_t[:, :], ALU.mult).then_inc(R["rope"].sem, 1)
                swapped = bQK[:, 0:256].rearrange("p (n two) -> p n two", two=2)[:, :, ::-1]
                dve.tensor_tensor(rope_s[:, :].rearrange("p (n two) -> p n two", two=2), swapped,
                                  sin_t[:, :].rearrange("p (n two) -> p n two", two=2), ALU.mult).then_inc(R["rope"].sem, 1)

            @per_batch
            def rotated(b, p):
                wait(dve, R["rope"], b, 2)
                wait(dve, R["t4"], b - 2)
                dve.tensor_tensor(qkr[p][:, :, 0:RD], rope_c[:, :].rearrange("p (a b) -> p a b", b=RD),
                                  rope_s[:, :].rearrange("p (a b) -> p a b", b=RD), ALU.add).then_inc(R["rope"].sem, 1)

            @per_batch
            def decayed(b, p, c):
                wait(dve, R["av"], b - 2)
                wait(dve, R["st"], b, c + 1)
                dve.tensor_tensor(rprob[p][:, c, :, :].rearrange("p a b -> p (a b)"), bS[c][:, :],
                                  decay[:, c, :, :].rearrange("p a b -> p (a b)"), ALU.mult).then_inc(R["prob"].sem, 1)

            @per_batch
            def square_sums(b, p):
                wait(dve, R["nat"], b)
                wait(dve, R["rs"], b - 2)
                dve.tensor_reduce(rms[p][:, :], rsq[:, :].rearrange("p (h d) -> p h d", h=RH), AX.X, ALU.add).then_inc(R["ms"].sem, 1)

            @per_batch
            def mean_squares(b, p):
                wait(dve, R["ms"], b, 1)
                dve.tensor_scalar(rms[p][:, :], rms[p][:, :], 1.0 / RV, EPS, ALU.mult, ALU.add).then_inc(R["ms"].sem, 1)

            @per_batch
            def normed_o(b, p):
                wait(dve, R["rs"], b)
                wait(dve, R["y"], b - 1)
                rb = rrs[p][:, :].rearrange("p (h o) -> p h o", o=1).to_broadcast((S, RH, RV))
                dve.tensor_tensor(ry0[:, :].rearrange("p (h d) -> p h d", h=RH),
                                  rnat[p][:, :].rearrange("p (h d) -> p h d", h=RH), rb, ALU.mult).then_inc(R["y"].sem, 1)

            @per_batch
            def gated_y(b, p):
                wait(dve, R["y"], b, 1)
                wait(dve, R["gate"], b)
                wait(dve, R["ty"], b - 2)
                dve.tensor_tensor(ry[p][:, :], ry0[:, :], rgate[p][:, :], ALU.mult).then_inc(R["y"].sem, 1)

            @per_batch
            def residual(b, p):
                wait(dve, R["wo"], b)
                dve.tensor_tensor(zt[p][:, :], bY[:, 256:384], xin[:, one(b), :].rearrange("p a b -> p (a b)"), ALU.add)\
                   .then_inc(R["ln"].sem, 1)

            @per_batch
            def statistics(b, p):
                wait(dve, R["ln"], b, 1)
                free(dve)
                dve.bn_stats(st[p][:, :], zt[p][:, :]).then_inc(R["ln"].sem, 1)

            @per_batch
            def mean_and_variance(b, p):
                wait(dve, R["ln"], b, 2)
                free(dve)
                dve.bn_aggr(mv[p][:, :], st[p][:, :]).then_inc(R["ln"].sem, 1)

            @per_batch
            def guarded(b, p):
                wait(dve, R["ln"], b, 3)
                dve.tensor_scalar(ve[p][:, :], mv[p][:, 1:2], EPS, None, ALU.add).then_inc(R["ln"].sem, 1)

            @per_batch
            def normed(b, p):
                wait(dve, R["lnp"], b)
                dve.tensor_scalar(x1[:, one(b), :].rearrange("p a b -> p (a b)"), zt[p][:, :], mv[p][:, 0:1], rs[p][:, :],
                                  ALU.subtract, ALU.mult).then_inc(R["x1"].sem, 1)

            def slot(at):
                rotate(*at(0))
                gated_y(*at(3))
                rotated(*at(0))
                square_sums(*at(2))
                decayed(*at(1), 0)
                mean_squares(*at(2))
                decayed(*at(1), 1)
                normed(*at(4))
                residual(*at(3))
                statistics(*at(3))
                mean_and_variance(*at(3))
                normed_o(*at(2))
                guarded(*at(3))
            slots(dve, slot, 6, 4)

        def retention_gpsimd(pool):
            @per_batch
            def inverse_rms(b, p):
                wait(pool, R["ms"], b)
                wait(pool, R["y"], b - 2, 1)
                pool.tensor_tensor(rrs[p][:, :], rms[p][:, :], mhalf[:, :], ALU.pow).then_inc(R["rs"].sem, 1)

            @per_batch
            def inverse_deviation(b, p):
                wait(pool, R["ln"], b, 4)
                wait(pool, R["x1"], b - 2)
                pool.tensor_tensor(rs[p][:, :], ve[p][:, :], mhalf[:, 0:1], ALU.pow).then_inc(R["lnp"].sem, 1)

            @per_batch
            def gate(b, p):
                wait(pool, R["silu"], b)
                wait(pool, R["y"], b - 2)
                pool.tensor_tensor(rgate[p][:, :], rsg[:, :], gw[:, :], ALU.mult).then_inc(R["gate"].sem, 1)

            def slot(at):
                inverse_rms(*at(2))
                inverse_deviation(*at(3))
                gate(*at(0))
            slots(pool, slot, 6, 4)

        nat = [sb(f"nat{p}", [S, C]) for p in range(2)]
        cnat = [sb(f"cnat{p}", [CT, CC]) for p in range(2)]
        lnt = sb("lnt", [S, C])
        xnT = sb("xnT", [C, S])
        ynT = sb("ynT", [C, S])
        cnT = sb("cnT", [CC, CT])
        qT = [sb(f"qT{p}", [128, 512]) for p in range(2)]
        vv = [sb(f"vv{p}", [S, 512]) for p in range(2)]
        E = [carve(f"E{p}", [S, HG, 512]) for p in range(2)]
        ET = carve("ET", [S, HG, 512])
        mx = [sb(f"mx{p}", [S, 4, HG]) for p in range(2)]
        den = [sb(f"den{p}", [S, 4, HG]) for p in range(2)]
        rden = sb("rden", [S, 4, HG])
        parts = sb("parts", [S, 4, 32])
        partsT = sb("partsT", [128, S], F32R)
        rbs = sb("rbs", [128, 512])
        oN = sb("oN", [128, 512])
        r1 = [sb(f"r1{p}", [S, C]) for p in range(2)]

        A_STEPS = {k: steps("a_" + k, n) for k, n in {
            "ln": 4, "lnp": 1, "x": 4, "xp": 1, "nat": 1, "t": 1, "xy": 2, "q": 1, "qe": 1, "k": 1, "ke": 2, "kx": 2, "v": 1,
            "ve": 1, "s": 4, "max": 4, "exp": 4, "et": 4, "ete": 4, "rd": 3, "rt": 1, "rte": 1, "av": 1, "rb": 1, "rbe": 1, "mul": 1,
            "li": 1, "res": 1, "r1": 1}.items()}

        def attention(name, w, src, self_attention, before):
            TK, KC = (S, C) if self_attention else (CT, CC)
            keysT = ynT if self_attention else cnT
            if self_attention:
                P = A_STEPS
            else:
                P = {k: s.next_phase() for k, s in A_STEPS.items()}
                P["cn"] = steps("a_cn")
            bQ, bK, bO, bE = bank[0], bank[1], bank[2], bank[3]
            bS = bank[4:8]

            def k_rows(g):
                return bK[32 * g:32 * g + 32, 0:HG * TK].rearrange("p (h t) -> p h t", h=HG)

            def enter(eng):
                for s in before:
                    eng.wait_ge(s.sem, s.at(B - 1))

            def tensor(pe):
                enter(pe)
                pe.wait_ge(ld[name], ld_n[name])

                @per_batch
                def transpose_normed(b, p):
                    wait(pe, P["nat"], b)
                    wait(pe, P["ke"], b - 1)
                    wait(pe, P["kx"], b - 1)
                    free(pe)
                    last = pe.transpose(bK[:, 0:S], nat[p][:, :], ident[:, :])
                    if not self_attention:
                        wait(pe, P["cn"], b)
                        free(pe)
                        last = pe.transpose(bK[0:CC, S:S + CT], cnat[p][:, :], ident[0:CT, 0:CT])
                    last.then_inc(P["t"].sem, 1)

                @per_batch
                def project_q(b, p):
                    wait(pe, P["xy"], b)
                    wait(pe, P["ve"], b - 1)
                    for hg in range(HG):
                        last = pe.matmul(bQ[:, hg * S:(hg + 1) * S], w["wq"][:, hg * 128:(hg + 1) * 128], xnT[:, :],
                                         start=True, stop=True)
                    last.then_inc(P["q"].sem, 1)

                @per_batch
                def project_k(b, p):
                    wait(pe, P["xy"], b)
                    for hg in range(HG):
                        last = pe.matmul(bK[:, hg * TK:(hg + 1) * TK], w["wk"][:, hg * 128:(hg + 1) * 128], keysT[0:KC, 0:TK],
                                         start=True, stop=True)
                    last.then_inc(P["k"].sem, 1)

                @per_batch
                def project_v(b, p):
                    wait(pe, P["xy"], b)
                    wait(pe, P["qe"], b)
                    pe.matmul(bQ[0:TK, :], keysT[0:KC, 0:TK], w["wv"][:, :], start=True, stop=True).then_inc(P["v"].sem, 1)

                @per_batch
                def scores(b, p, hg):
                    wait(pe, P["qe"], b)
                    wait(pe, P["ke"], b)
                    wait(pe, P["kx"], b)
                    wait(pe, P["exp"], b - 1, hg + 1)
                    pe.matmul(bS[hg][:, 0:4 * TK], qT[p][:, hg * S:(hg + 1) * S], kd[p][:, hg, :, 0:TK],
                              start=True, stop=True).then_inc(P["s"].sem, 1)

                @per_batch
                def transpose_exp(b, p, hg):
                    wait(pe, P["exp"], b, hg + 1)
                    if hg:
                        wait(pe, P["ete"], b, hg)
                    else:
                        wait(pe, P["rbe"], b - 1)
                    free(pe)
                    for g in range(4):
                        last = pe.transpose(bE[0:TK, g * S:(g + 1) * S], E[p][:, hg, g * TK:(g + 1) * TK], ident[:, :])
                    last.then_inc(P["et"].sem, 1)

                @per_batch
                def weighted_values(b, p):
                    wait(pe, P["ve"], b)
                    wait(pe, P["ete"], b)
                    wait(pe, P["res"], b - 1)
                    for hg in range(HG):
                        for g in range(4):
                            h = 4 * hg + g
                            last = pe.matmul(bO[32 * g:32 * g + 32, hg * S:(hg + 1) * S], vv[p][0:TK, h * AD:(h + 1) * AD],
                                             ET[0:TK, hg, g * S:(g + 1) * S], start=True, stop=True)
                    last.then_inc(P["av"].sem, 1)

                @per_batch
                def transpose_reciprocals(b, p):
                    wait(pe, P["rd"], b)
                    wait(pe, P["ete"], b)
                    free(pe)
                    pe.transpose(bE[:, 0:S], parts[:, :, :].rearrange("p a b -> p (a b)"), ident[:, :]).then_inc(P["rt"].sem, 1)

                @per_batch
                def spread_reciprocals(b, p):
                    wait(pe, P["rte"], b)
                    for hg in range(HG):
                        last = pe.matmul(bE[:, hg * S:(hg + 1) * S], bc_sel[:, hg, :], partsT[:, :], start=True, stop=True)
                    last.then_inc(P["rb"].sem, 1)

                @per_batch
                def project_out(b, p):
                    wait(pe, P["mul"], b)
                    for hg in range(HG):
                        last = pe.matmul(bO[:, 0:C], oN[:, hg * S:(hg + 1) * S], w["li1"][:, hg, :],
                                         start=(hg == 0), stop=(hg == HG - 1))
                    last.then_inc(P["li"].sem, 1)

                def slot(at):
                    if self_attention:
                        weighted_values(*at(4))
                        transpose_exp(*at(3), 0)
                        scores(*at(3), 3)
                        project_v(*at(2))
                        transpose_exp(*at(3), 1)
                        transpose_normed(*at(1))
                        scores(*at(2), 0)
                        transpose_exp(*at(3), 2)
                        scores(*at(2), 1)
                        project_k(*at(1))
                        transpose_exp(*at(3), 3)
                        project_out(*at(4))
                        project_q(*at(1))
                        transpose_reciprocals(*at(3))
                        scores(*at(2), 2)
                        spread_reciprocals(*at(3))
                    else:
                        spread_reciprocals(*at(4))
                        weighted_values(*at(4))
                        transpose_exp(*at(3), 0)
                        scores(*at(2), 0)
                        scores(*at(2), 1)
                        transpose_exp(*at(3), 1)
                        project_v(*at(2))
                        transpose_exp(*at(3), 2)
                        transpose_normed(*at(1))
                        scores(*at(2), 2)
                        project_out(*at(4))
                        transpose_exp(*at(3), 3)
                        scores(*at(2), 3)
                        project_k(*at(1))
                        transpose_reciprocals(*at(3))
                        project_q(*at(1))
                slots(pe, slot, 6, 4)

            def scalar(act):
                enter(act)
                act.wait_ge(ld[name], ld_n[name])

                @per_batch
                def tokens_and_keys(b, p):
                    wait(act, P["t"], b)
                    wait(act, P["k"], b - 1)
                    wait(act, P["v"], b - 1)
                    act.activation(xnT[:, :], bK[:, 0:S], ACT.Identity, bias=w["lnx"][:, 1:2], scale=w["lnx"][:, 0:1])\
                       .then_inc(P["xy"].sem, 1)
                    ky = bK[0:KC, 0:S] if self_attention else bK[0:KC, S:S + CT]
                    act.activation(keysT[0:KC, 0:TK], ky, ACT.Identity, bias=w["lny"][:, 1:2], scale=w["lny"][:, 0:1])\
                       .then_inc(P["xy"].sem, 1)

                @per_batch
                def queries(b, p):
                    wait(act, P["q"], b)
                    wait(act, P["s"], b - 2)
                    act.activation(qT[p][:, :], bQ[:, :], ACT.Copy, scale=AD ** -0.5).then_inc(P["qe"].sem, 1)

                @per_batch
                def half_of_keys(b, p):
                    wait(act, P["k"], b)
                    wait(act, P["s"], b - 2)
                    for g in (0, 1):
                        act.activation(kd[p][32 * g:32 * g + 32, :, g, 0:TK], k_rows(g), ACT.Copy).then_inc(P["ke"].sem, 1)

                @per_batch
                def values(b, p):
                    wait(act, P["v"], b)
                    wait(act, P["av"], b - 2)
                    act.activation(vv[p][0:TK, :], bQ[0:TK, :], ACT.Copy).then_inc(P["ve"].sem, 1)

                @per_batch
                def exponentials(b, p, hg):
                    wait(act, P["max"], b, hg + 1)
                    wait(act, P["et"], b - 2, hg + 1)
                    wait(act, P["rd"], b - 2, 1)
                    for g in range(4):
                        last = act.activation(E[p][:, hg, g * TK:(g + 1) * TK], bS[hg][:, g * TK:(g + 1) * TK], ACT.Exp,
                                              bias=mx[p][:, hg, g:g + 1], accum_out=den[p][:, hg, g:g + 1])
                    last.then_inc(P["exp"].sem, 1)

                @per_batch
                def spread_reciprocals(b, p):
                    wait(act, P["rb"], b)
                    wait(act, P["mul"], b - 1)
                    act.activation(rbs[:, :], bE[:, :], ACT.Copy).then_inc(P["rbe"].sem, 1)

                def slot(at):
                    if self_attention:
                        queries(*at(2))
                        half_of_keys(*at(2))
                        exponentials(*at(3), 2)
                        exponentials(*at(3), 3)
                        tokens_and_keys(*at(1))
                        values(*at(2))
                        exponentials(*at(2), 0)
                        exponentials(*at(2), 1)
                        spread_reciprocals(*at(3))
                    else:
                        exponentials(*at(3), 2)
                        exponentials(*at(3), 3)
                        exponentials(*at(2), 0)
                        tokens_and_keys(*at(1))
                        values(*at(2))
                        exponentials(*at(2), 1)
                        half_of_keys(*at(1))
                        spread_reciprocals(*at(3))
                        queries(*at(1))
                slots(act, slot, 6, 4)

            def vector(dve):
                enter(dve)
                dve.wait_ge(ld[name], ld_n[name])

                def x_in(b):
                    return src[:, one(b), :].rearrange("p a b -> p (a b)")

                def x_out(b):
                    return xa[:, one(b), :].rearrange("p a b -> p (a b)")

                @per_batch
                def statistics(b, p):
                    wait(dve, P["ln"], b - 1)
                    free(dve)
                    dve.bn_stats(st[p][:, :], x_in(b)).then_inc(P["ln"].sem, 1)

                @per_batch
                def mean_and_variance(b, p):
                    wait(dve, P["ln"], b, 1)
                    free(dve)
                    dve.bn_aggr(mv[p][:, :], st[p][:, :]).then_inc(P["ln"].sem, 1)

                @per_batch
                def guarded(b, p):
                    wait(dve, P["ln"], b, 2)
                    wait(dve, P["lnp"], b - 2)
                    dve.tensor_scalar(ve[p][:, :], mv[p][:, 1:2], EPS, None, ALU.add).then_inc(P["ln"].sem, 1)

                @per_batch
                def centred(b, p):
                    wait(dve, P["ln"], b, 2)
                    wait(dve, P["x"], b - 1, 1)
                    dve.scalar_tensor_tensor(lnt[:, :], x_in(b), mv[p][:, 0:1], w["g"][:, :], ALU.subtract, ALU.mult)\
                       .then_inc(P["ln"].sem, 1)

                @per_batch
                def normed(b, p):
                    wait(dve, P["lnp"], b)
                    wait(dve, P["ln"], b, 4)
                    dve.scalar_tensor_tensor(x_out(b), lnt[:, :], rs[p][:, 0:1], w["b"][:, :], ALU.mult, ALU.add)\
                       .then_inc(P["x"].sem, 1)

                @per_batch
                def second_statistics(b, p):
                    wait(dve, P["x"], b, 1)
                    free(dve)
                    dve.bn_stats(st2[p][:, :], x_out(b)).then_inc(P["x"].sem, 1)

                @per_batch
                def second_mean_and_variance(b, p):
                    wait(dve, P["x"], b, 2)
                    free(dve)
                    dve.bn_aggr(mv2[p][:, :], st2[p][:, :]).then_inc(P["x"].sem, 1)

                @per_batch
                def second_guarded(b, p):
                    wait(dve, P["x"], b, 3)
                    wait(dve, P["xp"], b - 2)
                    dve.tensor_scalar(ve2[p][:, :], mv2[p][:, 1:2], EPS, None, ALU.add).then_inc(P["x"].sem, 1)

                @per_batch
                def second_normed(b, p):
                    wait(dve, P["xp"], b)
                    wait(dve, P["t"], b - 2)
                    dve.tensor_scalar(nat[p][:, :], x_out(b), mv2[p][:, 0:1], rs2[p][:, 0:1], ALU.subtract, ALU.mult)\
                       .then_inc(P["nat"].sem, 1)

                @per_batch
                def context(b, p):
                    wait(dve, P["t"], b - 2)
                    free(dve)
                    dve.tensor_copy(cnat[p][:, :], ctxn[:, one(b), :].rearrange("p a b -> p (a b)")).then_inc(P["cn"].sem, 1)

                @per_batch
                def half_of_keys(b, p):
                    wait(dve, P["k"], b)
                    wait(dve, P["s"], b - 2)
                    free(dve)
                    for g in (2, 3):
                        dve.tensor_copy(kd[p][32 * g:32 * g + 32, :, g, 0:TK], k_rows(g)).then_inc(P["kx"].sem, 1)

                @per_batch
                def maximum(b, p, hg):
                    wait(dve, P["exp"], b - 2, hg + 1)
                    wait(dve, P["s"], b, hg + 1)
                    dve.tensor_reduce(mx[p][:, hg, :], bS[hg][:, 0:HG * TK].rearrange("p (h t) -> p h t", h=HG), AX.X, ALU.max,
                                      negate=True).then_inc(P["max"].sem, 1)

                @per_batch
                def exp_transposed(b, p, hg):
                    wait(dve, P["et"], b, hg + 1)
                    wait(dve, P["av"], b - 1)
                    if self_attention:
                        dve.tensor_tensor(ET[:, hg, :].rearrange("p (h s) -> p h s", h=HG), bE[:, :].rearrange("p (h s) -> p h s", h=HG),
                                          later[:, :].rearrange("p (o s) -> p o s", o=1).to_broadcast((S, HG, S)), ALU.mult)\
                           .then_inc(P["ete"].sem, 1)
                    else:
                        dve.tensor_copy(ET[0:TK, hg, :], bE[0:TK, :]).then_inc(P["ete"].sem, 1)

                rden_g = rden[:, :, :].rearrange("p h g -> p g h")

                @per_batch
                def reciprocals(b, p):
                    wait(dve, P["exp"], b)
                    wait(dve, P["rd"], b - 1)
                    dve.reciprocal(rden[:, :, :], den[p][:, :, :]).then_inc(P["rd"].sem, 1)

                @per_batch
                def high_part(b, p):
                    wait(dve, P["rd"], b, 1)
                    wait(dve, P["rt"], b - 1)
                    dve.tensor_copy(parts[:, :, 0:HG].bitcast(F32R), rden_g).then_inc(P["rd"].sem, 1)

                @per_batch
                def low_part(b, p):
                    wait(dve, P["rd"], b, 2)
                    dve.tensor_tensor(parts[:, :, 16:16 + HG].bitcast(F32R), rden_g, parts[:, :, 0:HG], ALU.subtract)\
                       .then_inc(P["rd"].sem, 1)

                @per_batch
                def transposed_parts(b, p):
                    wait(dve, P["rt"], b)
                    wait(dve, P["rb"], b - 1)
                    dve.tensor_copy(partsT[:, :], bE[:, 0:S]).then_inc(P["rte"].sem, 1)

                @per_batch
                def divided(b, p):
                    wait(dve, P["av"], b)
                    wait(dve, P["rbe"], b)
                    wait(dve, P["li"], b - 1)
                    dve.tensor_tensor(oN[:, :], bO[:, :], rbs[:, :], ALU.mult).then_inc(P["mul"].sem, 1)

                @per_batch
                def residual(b, p):
                    wait(dve, P["li"], b)
                    wait(dve, P["r1"], b)
                    dve.tensor_tensor(xo[:, one(b), :].rearrange("p a b -> p (a b)"), bO[:, 0:C], r1[p][:, :], ALU.add)\
                       .then_inc(P["res"].sem, 1)

                def slot(at):
                    if self_attention:
                        transposed_parts(*at(4))
                        second_guarded(*at(1))
                        statistics(*at(0))
                        half_of_keys(*at(2))
                        maximum(*at(3), 2)
                        divided(*at(4))
                        second_normed(*at(1))
                        exp_transposed(*at(3), 0)
                        maximum(*at(3), 3)
                        mean_and_variance(*at(0))
                        exp_transposed(*at(3), 1)
                        guarded(*at(0))
                        centred(*at(0))
                        exp_transposed(*at(3), 2)
                        maximum(*at(2), 0)
                        normed(*at(0))
                        reciprocals(*at(3))
                        high_part(*at(3))
                        low_part(*at(3))
                        exp_transposed(*at(3), 3)
                        second_statistics(*at(0))
                        maximum(*at(2), 1)
                        residual(*at(4))
                        second_mean_and_variance(*at(0))
                    else:
                        maximum(*at(2), 0)
                        exp_transposed(*at(3), 1)
                        statistics(*at(0))
                        divided(*at(4))
                        maximum(*at(2), 1)
                        reciprocals(*at(3))
                        exp_transposed(*at(3), 2)
                        high_part(*at(3))
                        mean_and_variance(*at(0))
                        guarded(*at(0))
                        centred(*at(0))
                        low_part(*at(3))
                        exp_transposed(*at(3), 3)
                        normed(*at(0))
                        context(*at(0))
                        transposed_parts(*at(3))
                        residual(*at(4))
                        second_statistics(*at(0))
                        second_mean_and_variance(*at(0))
                        maximum(*at(2), 2)
                        maximum(*at(2), 3)
                        second_guarded(*at(0))
                        half_of_keys(*at(1))
                        second_normed(*at(0))
                        exp_transposed(*at(2), 0)
                slots(dve, slot, 6, 4)

            def gpsimd(pool):
                enter(pool)
                pool.wait_ge(ld[name], ld_n[name])

                @per_batch
                def inverse_deviation(b, p):
                    wait(pool, P["ln"], b, 3)
                    wait(pool, P["x"], b - 2, 1)
                    pool.tensor_tensor(rs[p][:, :], ve[p][:, :], mhalf[:, 0:1], ALU.pow).then_inc(P["lnp"].sem, 1)

                @per_batch
                def second_inverse_deviation(b, p):
                    wait(pool, P["x"], b, 4)
                    wait(pool, P["nat"], b - 2)
                    pool.tensor_tensor(rs2[p][:, :], ve2[p][:, :], mhalf[:, 0:1], ALU.pow).then_inc(P["xp"].sem, 1)

                @per_batch
                def residual_and_bias(b, p):
                    wait(pool, P["x"], b, 1)
                    wait(pool, P["res"], b - 2)
                    pool.tensor_tensor(r1[p][:, :], xa[:, one(b), :].rearrange("p a b -> p (a b)"), w["li1b"][:, :], ALU.add)\
                        .then_inc(P["r1"].sem, 1)

                def slot(at):
                    if self_attention:
                        second_inverse_deviation(*at(1))
                        inverse_deviation(*at(0))
                        residual_and_bias(*at(3))
                    else:
                        residual_and_bias(*at(3))
                        second_inverse_deviation(*at(1))
                        inverse_deviation(*at(0))
                slots(pool, slot, 6, 4)

            return {"tensor": tensor, "scalar": scalar, "vector": vector, "gpsimd": gpsimd, "steps": list(P.values())}

        n3T = [sb(f"n3T{p}", [C, S]) for p in range(2)]
        hT = [carve(f"hT{p}", [128, 4, S]) for p in range(2)]
        r2 = [sb(f"r2{p}", [S, C]) for p in range(2)]
        r2t = [sb(f"r2t{k}", [S, C]) for k in range(2)]

        x3T = [sb(f"x3T{p}", [C, S]) for p in range(2)]
        x3n = [sb(f"x3n{p}", [S, C]) for p in range(2)]
        logit = sb("logit", [S, B, NE])
        L = {k: steps("l_" + k, n) for k, n in {"ln": 3, "lnp": 1, "x3n": 1, "x3": 1, "t": 1, "te": 1, "mm": 1, "lg": 1}.items()}

        M_STEPS = {k: steps("m_" + k, n) for k, n in {
            "ln": 3, "lnp": 1, "nat": 1, "t": 1, "te": 1, "up": 1, "gelu": 4, "down": 1, "fin": 1}.items()}

        def mlp(name, w, residuals, before, routed):
            NR = len(residuals)
            if routed:
                P = {k: s.next_phase() for k, s in M_STEPS.items()}
            else:
                P = dict(M_STEPS)
            P["r2"] = steps(name + "_r2", NR)
            bT, bD, bX, bL = bank[0], bank[3], bank[4], bank[5]
            bU = bank[1:3]

            def enter(eng):
                for s in before:
                    eng.wait_ge(s.sem, s.at(B - 1))

            def tensor(pe):
                enter(pe)
                pe.wait_ge(ld[name], ld_n[name])
                if routed:
                    pe.wait_ge(ld["exp"], ld_n["exp"])

                @per_batch
                def transpose_normed(b, p):
                    wait(pe, P["nat"], b)
                    wait(pe, P["te"], b - 1)
                    free(pe)
                    pe.transpose(bT[:, 0:S], nat[p][:, :], ident[:, :]).then_inc(P["t"].sem, 1)

                @per_batch
                def up(b, p):
                    wait(pe, P["te"], b)
                    wait(pe, P["gelu"], b - 2)
                    for c in range(4):
                        last = pe.matmul(bU[p][:, c * S:(c + 1) * S], w["li2"][:, c * 128:(c + 1) * 128], n3T[p][:, :],
                                         start=True, stop=True)
                    last.then_inc(P["up"].sem, 1)

                @per_batch
                def down(b, p):
                    wait(pe, P["gelu"], b)
                    wait(pe, P["fin"], b - 1)
                    for c in range(4):
                        last = pe.matmul(bD[:, 0:C], hT[p][:, c, :], w["li3"][:, c, :], start=(c == 0), stop=(c == 3))
                    last.then_inc(P["down"].sem, 1)

                @per_batch
                def transpose_x3(b, p):
                    wait(pe, L["x3n"], b)
                    wait(pe, L["te"], b - 1)
                    free(pe)
                    pe.transpose(bX[:, 0:S], x3n[p][:, :], ident[:, :]).then_inc(L["t"].sem, 1)

                @per_batch
                def logits(b, p):
                    wait(pe, L["te"], b)
                    wait(pe, L["lg"], b - 1)
                    pe.matmul(bL[:, 0:NE], x3T[p][:, :], router[:, :], start=True, stop=True).then_inc(L["mm"].sem, 1)

                def slot(at):
                    if routed:
                        transpose_normed(*at(0))
                        down(*at(2))
                        logits(*at(4))
                        up(*at(0))
                        transpose_x3(*at(3))
                    else:
                        up(*at(3))
                        down(*at(4))
                        transpose_normed(*at(1))
                slots(pe, slot, 8, 6 if routed else 5)

            def scalar(act):
                enter(act)
                act.wait_ge(ld[name], ld_n[name])

                @per_batch
                def normed_transposed(b, p):
                    wait(act, P["t"], b)
                    wait(act, P["up"], b - 2)
                    act.activation(n3T[p][:, :], bT[:, 0:S], ACT.Identity, bias=w["ln3"][:, 1:2], scale=w["ln3"][:, 0:1])\
                       .then_inc(P["te"].sem, 1)

                @per_batch
                def gelus(b, p):
                    wait(act, P["up"], b)
                    wait(act, P["down"], b - 2)
                    for c in range(4):
                        act.activation(hT[p][:, c, :], bU[p][:, c * S:(c + 1) * S], ACT.Gelu, bias=w["li2b"][:, c:c + 1])\
                           .then_inc(P["gelu"].sem, 1)

                @per_batch
                def x3_transposed(b, p):
                    wait(act, L["t"], b)
                    wait(act, L["mm"], b - 2)
                    act.activation(x3T[p][:, :], bX[:, 0:S], ACT.Copy).then_inc(L["te"].sem, 1)

                @per_batch
                def x3_kept(b, p):
                    wait(act, L["x3n"], b)
                    act.activation(x3[:, one(b), 0:C].rearrange("p a b -> p (a b)"), x3n[p][:, :], ACT.Copy).then_inc(L["x3"].sem, 1)

                def slot(at):
                    if routed:
                        gelus(*at(2))
                        x3_transposed(*at(4))
                        normed_transposed(*at(0))
                        x3_kept(*at(4))
                    else:
                        normed_transposed(*at(1))
                        gelus(*at(2))
                slots(act, slot, 8, 6 if routed else 5)

            def vector(dve):
                enter(dve)

                def x_in(b):
                    return xo[:, one(b), :].rearrange("p a b -> p (a b)")

                def z_of(b):
                    return z[:, one(b), :].rearrange("p a b -> p (a b)")

                @per_batch
                def statistics(b, p):
                    wait(dve, P["ln"], b - 1)
                    free(dve)
                    dve.bn_stats(st[p][:, :], x_in(b)).then_inc(P["ln"].sem, 1)

                @per_batch
                def mean_and_variance(b, p):
                    wait(dve, P["ln"], b, 1)
                    wait(dve, P["nat"], b - 2)
                    free(dve)
                    dve.bn_aggr(mv[p][:, :], st[p][:, :]).then_inc(P["ln"].sem, 1)

                @per_batch
                def guarded(b, p):
                    wait(dve, P["ln"], b, 2)
                    wait(dve, P["lnp"], b - 2)
                    dve.tensor_scalar(ve[p][:, :], mv[p][:, 1:2], EPS, None, ALU.add).then_inc(P["ln"].sem, 1)

                @per_batch
                def normed(b, p):
                    wait(dve, P["lnp"], b)
                    wait(dve, P["t"], b - 2)
                    dve.tensor_scalar(nat[p][:, :], x_in(b), mv[p][:, 0:1], rs[p][:, 0:1], ALU.subtract, ALU.mult)\
                       .then_inc(P["nat"].sem, 1)

                @per_batch
                def finished(b, p):
                    wait(dve, P["down"], b)
                    wait(dve, P["r2"], b)
                    dve.tensor_tensor(z_of(b), bD[:, 0:C], r2[p][:, :], ALU.add).then_inc(P["fin"].sem, 1)

                @per_batch
                def z_statistics(b, p):
                    wait(dve, P["fin"], b)
                    free(dve)
                    dve.bn_stats(st2[p][:, :], z_of(b)).then_inc(L["ln"].sem, 1)

                @per_batch
                def z_mean_and_variance(b, p):
                    wait(dve, L["ln"], b, 1)
                    wait(dve, L["x3n"], b - 2)
                    free(dve)
                    dve.bn_aggr(mv2[p][:, :], st2[p][:, :]).then_inc(L["ln"].sem, 1)

                @per_batch
                def z_guarded(b, p):
                    wait(dve, L["ln"], b, 2)
                    wait(dve, L["lnp"], b - 2)
                    dve.tensor_scalar(ve2[p][:, :], mv2[p][:, 1:2], EPS, None, ALU.add).then_inc(L["ln"].sem, 1)

                @per_batch
                def z_normed(b, p):
                    wait(dve, L["lnp"], b)
                    wait(dve, L["t"], b - 2)
                    wait(dve, L["x3"], b - 2)
                    dve.tensor_scalar(x3n[p][:, :], z_of(b), mv2[p][:, 0:1], rs2[p][:, 0:1], ALU.subtract, ALU.mult)\
                       .then_inc(L["x3n"].sem, 1)

                @per_batch
                def logits_kept(b, p):
                    wait(dve, L["mm"], b)
                    free(dve)
                    dve.tensor_copy(logit[:, one(b), :].rearrange("p a b -> p (a b)"), bL[:, 0:NE]).then_inc(L["lg"].sem, 1)

                def slot(at):
                    if routed:
                        statistics(*at(0))
                        mean_and_variance(*at(0))
                        finished(*at(4))
                        z_normed(*at(5))
                        guarded(*at(0))
                        normed(*at(1))
                        z_statistics(*at(4))
                        z_mean_and_variance(*at(4))
                        z_guarded(*at(4))
                        logits_kept(*at(5))
                    else:
                        statistics(*at(0))
                        normed(*at(2))
                        mean_and_variance(*at(0))
                        guarded(*at(0))
                        finished(*at(5))
                slots(dve, slot, 8, 6 if routed else 5)

            def gpsimd(pool):
                enter(pool)
                pool.wait_ge(ld[name], ld_n[name])

                @per_batch
                def inverse_deviation(b, p):
                    wait(pool, P["ln"], b, 3)
                    wait(pool, P["nat"], b - 2)
                    pool.tensor_tensor(rs[p][:, :], ve[p][:, :], mhalf[:, 0:1], ALU.pow).then_inc(P["lnp"].sem, 1)

                @per_batch
                def residual_sum(b, p):
                    wait(pool, P["fin"], b - 2)
                    wait(pool, P["r2"], b - 1)
                    acc = w["li3b"][:, :]
                    for k, r in enumerate(residuals):
                        dst = r2[p] if k == NR - 1 else r2t[k % 2]
                        pool.tensor_tensor(dst[:, :], r[:, one(b), :].rearrange("p a b -> p (a b)"), acc, ALU.add)\
                            .then_inc(P["r2"].sem, 1)
                        if k < NR - 1:
                            wait(pool, P["r2"], b, k + 1)
                        acc = dst[:, :]

                @per_batch
                def z_inverse_deviation(b, p):
                    wait(pool, L["ln"], b, 3)
                    wait(pool, L["x3n"], b - 2)
                    pool.tensor_tensor(rs2[p][:, :], ve2[p][:, :], mhalf[:, 0:1], ALU.pow).then_inc(L["lnp"].sem, 1)

                def slot(at):
                    if routed:
                        inverse_deviation(*at(1))
                        z_inverse_deviation(*at(5))
                        residual_sum(*at(3))
                    else:
                        inverse_deviation(*at(1))
                        residual_sum(*at(4))
                slots(pool, slot, 8, 6 if routed else 5)

            return {"tensor": tensor, "scalar": scalar, "vector": vector, "gpsimd": gpsimd, "steps": list(P.values())}

        self_att = attention("a1", att_w[0], x1, True, list(R.values()))
        mlp1 = mlp("m1", mlp_w[0], [xa, xo], self_att["steps"], False)
        cross_att = attention("a2", att_w[1], z, False, mlp1["steps"])
        mlp2 = mlp("m2", mlp_w[1], [xa, xo, x1], cross_att["steps"], True)
        phases = [self_att, mlp1, cross_att, mlp2]

        taken[0] = 0
        lmax = sb("lmax", [S, B])
        code = carve("code", [S, B, NE])
        cmax = sb("cmax", [S, B])
        hot = carve("hot", [S, B, NE])
        ones = sb("ones", [S, S])
        base_b = sb("base_b", [S, NE, B + 1])
        tot1 = sb("tot1", [S, NE, B + 1])
        goes_on = sb("goes_on", [S, NE, B + 1])
        one_e = sb("one_e", [S, NE])
        full = carve("full", [S, NE, B])
        ntile = sb("ntile", [S, NE])
        tend = sb("tend", [S, NE + 1])
        start_e = sb("start_e", [S, NE])
        pos = carve("pos", [S, B, NE])
        pos2 = carve("pos2", [S, B, NE])
        place_f = sb("place_f", [S, B])
        place = sb("place", [S, B], I32)
        after = carve("after", [S, NE, NT])
        eid_f = sb("eid_f", [S, NT])
        eid = sb("eid", [S, NT], I32)
        placing = sem("placing")
        placed_mm = sem("placed_mm")
        n_place = [0]
        marks = {}

        def place_vector(dve):
            def link(ins, mark=None):
                n_place[0] += 1
                ins.then_inc(placing, 1)
                dve.wait_ge(placing, n_place[0])
                if mark:
                    marks[mark] = n_place[0]

            def bc(ap, shape):
                return ap.to_broadcast(shape)

            dve.wait_ge(L["lg"].sem, L["lg"].at(B - 1))
            link(dve.tensor_reduce(lmax[:, :], logit[:, :, :], AX.X, ALU.max))
            link(dve.tensor_tensor(code[:, :, :], logit[:, :, :], bc(lmax[:, :].rearrange("p (b o) -> p b o", o=1), (S, B, NE)), ALU.is_ge))
            link(dve.tensor_tensor(code[:, :, :], code[:, :, :], bc(rank_code[:, :].rearrange("p (o e) -> p o e", o=1), (S, B, NE)), ALU.mult))
            link(dve.tensor_reduce(cmax[:, :], code[:, :, :], AX.X, ALU.max))
            link(dve.tensor_tensor(hot[:, :, :], bc(rank_code[:, :].rearrange("p (o e) -> p o e", o=1), (S, B, NE)),
                                   bc(cmax[:, :].rearrange("p (b o) -> p b o", o=1), (S, B, NE)), ALU.is_equal), "hot")
            dve.wait_ge(placed_mm, 2)
            link(dve.tensor_copy(tot1[:, :, 1:B + 1], bank[2][:, 0:B * NE].rearrange("p (b e) -> p e b", e=NE)))
            link(dve.tensor_tensor_scan(base_b[:, :, :].rearrange("p e b -> p (e b)"), goes_on[:, :, :].rearrange("p e b -> p (e b)"),
                                        tot1[:, :, :].rearrange("p e b -> p (e b)"), 0.0, ALU.mult, ALU.add))
            link(dve.tensor_tensor(full[:, :, :], bc(base_b[:, :, B:B + 1], (S, NE, B)), tile_at[:, :, :], ALU.is_gt))
            link(dve.tensor_reduce(ntile[:, :], full[:, :, :], AX.X, ALU.add))
            link(dve.tensor_tensor_scan(tend[:, 1:NE + 1], one_e[:, :], ntile[:, :], 0.0, ALU.mult, ALU.add))
            link(dve.tensor_scalar(start_e[:, :], tend[:, 0:NE], float(S), None, ALU.mult))
            link(dve.tensor_tensor(pos[:, :, :], bank[1][:, 0:B * NE].rearrange("p (b e) -> p b e", e=NE),
                                   base_b[:, :, 0:B].rearrange("p e b -> p b e"), ALU.add))
            link(dve.tensor_tensor(pos2[:, :, :], pos[:, :, :], bc(start_e[:, :].rearrange("p (o e) -> p o e", o=1), (S, B, NE)), ALU.add))
            link(dve.tensor_tensor(pos[:, :, :], pos2[:, :, :], hot[:, :, :], ALU.mult))
            link(dve.tensor_reduce(place_f[:, :], pos[:, :, :], AX.X, ALU.add))
            link(dve.tensor_copy(place[:, :], place_f[:, :]), "place")
            link(dve.tensor_tensor(after[:, :, :], bc(tile_no[:, :].rearrange("p (o j) -> p o j", o=1), (S, NE, NT)),
                                   bc(tend[:, 1:NE + 1].rearrange("p (e o) -> p e o", o=1), (S, NE, NT)), ALU.is_ge))
            link(dve.tensor_reduce(eid_f[:, :], after[:, :, :].rearrange("p e j -> p j e"), AX.X, ALU.add))
            link(dve.tensor_scalar(eid_f[:, :], eid_f[:, :], float(NE - 1), None, ALU.min))
            link(dve.tensor_copy(eid[:, :], eid_f[:, :]), "eid")

        def place_tensor(pe):
            pe.wait_ge(placing, 5)
            hot2 = hot[:, :, :].rearrange("p b e -> p (b e)")
            pe.wait_ge(L["lg"].sem, L["lg"].at(B - 1))
            pe.matmul(bank[1][:, 0:B * NE], tri[:, :], hot2, start=True, stop=True).then_inc(placed_mm, 1)
            pe.matmul(bank[2][:, 0:B * NE], ones[:, :], hot2, start=True, stop=True).then_inc(placed_mm, 1)

        scattered, blanked = sem("scattered"), sem("blanked")

        def place_gpsimd(pool):
            pool.wait_ge(placing, marks["place"])
            pool.wait_ge(L["x3"].sem, L["x3"].at(B - 1))
            pool.wait_ge(blanked, 16)
            pool.wait_ge(const_ready, 2)
            for b in range(B):
                pool.indirect_dma_start(xs_dram, bass.IndirectOffsetOnAxis(ap=place[:, b:b + 1], axis=0), x3[:, b, :], None)\
                    .then_inc(scattered, 16)

        xt = arena[:, taken[0]:taken[0] + NT * CW].rearrange("p (j c) -> p j c", c=CW)
        taken[0] += NT * CW
        xc = [carve(f"xc{p}", [S, C]) for p in range(2)]
        xtT = [carve(f"xtT{p}", [C, S]) for p in range(2)]
        gs = [carve(f"gs{p}", [S, EI]) for p in range(2)]
        he = [carve(f"he{p}", [S, EI]) for p in range(2)]
        heT = [carve(f"heT{p}", [128, 3, S]) for p in range(2)]
        yr = [carve(f"yr{p}", [S, C]) for p in range(2)]
        yo = [sb(f"yo{p}", [S, C]) for p in range(2)]
        number = [sb(f"number{p}", [S, 1], I32) for p in range(2)]
        X = {k: steps("x_" + k, n) for k, n in {
            "cp": 1, "t": 1, "te": 1, "up": 1, "silu": 1, "h": 1, "ht": 1, "hte": 2, "dn": 1, "ye": 1, "ln": 3, "lnp": 1, "no": 1, "yo": 1}.items()}
        xt_in = [sem(f"xt_in{p}") for p in range(2)]
        y_out = [sem(f"y_out{p}") for p in range(2)]
        bankT, bankG, bankU, bankH, bankY = bank[0], bank[1], bank[2], bank[3], bank[4]
        per_tile = per_batch_of(NT)

        def experts_sync(sp):
            sp.wait_ge(scattered, 16 * B)

            @per_tile
            def load_tile(b, p):
                if not isinstance(b, int) or b >= 2:
                    sp.wait_ge(xt_in[p], (b - p) * 8)
                sp.dma_start(xt[:, one(b), :], xs_dram.rearrange("(j p) c -> p j c", p=S)[:, one(b), :]).then_inc(xt_in[p], 16)

            slots(sp, lambda at: load_tile(*at(0)), 2, 0, NT)
            for p in range(2):
                sp.wait_ge(y_out[p], 16 * ((NT - p + 1) // 2))

        def experts_tensor(pe):
            pe.wait_ge(placing, marks["eid"])

            def expert(b):
                return pe.value_load(eid[0:1, one(b)], min_val=0, max_val=NE - 1)

            @per_tile
            def transpose_tile(b, p):
                wait(pe, X["cp"], b)
                wait(pe, X["te"], b - 1)
                free(pe)
                pe.transpose(bankT[:, 0:S], xc[p][:, :], ident[:, :]).then_inc(X["t"].sem, 1)

            @per_tile
            def gate_and_up(b, p):
                e = expert(b)
                wait(pe, X["te"], b)
                wait(pe, X["h"], b - 1)
                pe.matmul(bankG[:, 0:EI], xtT[p][:, :], egu[:, one(e), 0:EI], start=True, stop=True)
                pe.matmul(bankU[:, 0:EI], xtT[p][:, :], egu[:, one(e), EI:2 * EI], start=True, stop=True).then_inc(X["up"].sem, 1)

            @per_tile
            def transpose_hidden(b, p):
                wait(pe, X["h"], b)
                wait(pe, X["hte"], b - 1)
                for c, n in enumerate(EC):
                    last = pe.transpose(bankH[0:n, c * S:(c + 1) * S], he[p][:, c * 128:c * 128 + n], ident[:, :])
                last.then_inc(X["ht"].sem, 1)

            @per_tile
            def down(b, p):
                e = expert(b)
                wait(pe, X["hte"], b)
                wait(pe, X["ye"], b - 1)
                for c, n in enumerate(EC):
                    last = pe.matmul(bankY[:, 0:C], heT[p][0:n, c, :], edn[0:n, one(e), c, :], start=(c == 0), stop=(c == 2))
                last.then_inc(X["dn"].sem, 1)

            def slot(at):
                gate_and_up(*at(2))
                transpose_tile(*at(1))
                transpose_hidden(*at(3))
                down(*at(4))
            slots(pe, slot, 8, 6, NT)

        def experts_scalar(act):
            @per_tile
            def tile_transposed(b, p):
                wait(act, X["t"], b)
                wait(act, X["up"], b - 2)
                act.activation(xtT[p][:, :], bankT[:, 0:S], ACT.Copy).then_inc(X["te"].sem, 1)

            @per_tile
            def silus(b, p):
                wait(act, X["up"], b)
                wait(act, X["h"], b - 2)
                act.activation(gs[p][:, :], bankG[:, 0:EI], ACT.Silu).then_inc(X["silu"].sem, 1)

            @per_tile
            def hidden_transposed(b, p):
                wait(act, X["ht"], b)
                wait(act, X["dn"], b - 2)
                act.activation(heT[p][:, 0:2, :].rearrange("p a b -> p (a b)"), bankH[:, 0:2 * S], ACT.Copy).then_inc(X["hte"].sem, 1)
                act.activation(heT[p][0:EC[2], 2, :], bankH[0:EC[2], 2 * S:3 * S], ACT.Copy).then_inc(X["hte"].sem, 1)

            def slot(at):
                silus(*at(2))
                tile_transposed(*at(1))
                hidden_transposed(*at(3))
            slots(act, slot, 8, 6, NT)

        def experts_vector(dve):
            @per_tile
            def tile_copied(b, p):
                dve.wait_ge(xt_in[p], (b - p) * 8 + 16)
                wait(dve, X["t"], b - 2)
                free(dve)
                dve.tensor_copy(xc[p][:, :], xt[:, one(b), 0:C].rearrange("p a b -> p (a b)")).then_inc(X["cp"].sem, 1)

            @per_tile
            def hidden(b, p):
                wait(dve, X["silu"], b)
                wait(dve, X["ht"], b - 2)
                dve.tensor_tensor(he[p][:, :], bankU[:, 0:EI], gs[p][:, :], ALU.mult).then_inc(X["h"].sem, 1)

            @per_tile
            def residual(b, p):
                wait(dve, X["dn"], b)
                wait(dve, X["yo"], b - 2)
                dve.tensor_tensor(yr[p][:, :], bankY[:, 0:C], xt[:, one(b), 0:C].rearrange("p a b -> p (a b)"), ALU.add)\
                   .then_inc(X["ye"].sem, 1)

            @per_tile
            def statistics(b, p):
                wait(dve, X["ye"], b)
                free(dve)
                dve.bn_stats(st[p][:, :], yr[p][:, :]).then_inc(X["ln"].sem, 1)

            @per_tile
            def mean_and_variance(b, p):
                wait(dve, X["ln"], b, 1)
                free(dve)
                dve.bn_aggr(mv[p][:, :], st[p][:, :]).then_inc(X["ln"].sem, 1)

            @per_tile
            def guarded(b, p):
                wait(dve, X["ln"], b, 2)
                wait(dve, X["lnp"], b - 2)
                dve.tensor_scalar(ve[p][:, :], mv[p][:, 1:2], EPS, None, ALU.add).then_inc(X["ln"].sem, 1)

            @per_tile
            def token_numbers(b, p):
                if not isinstance(b, int) or b >= 2:
                    dve.wait_ge(y_out[p], (b - p) * 8)
                free(dve)
                dve.tensor_copy(number[p][:, :], xt[:, one(b), C:C + 1].rearrange("p a b -> p (a b)").bitcast(I32)).then_inc(X["no"].sem, 1)

            @per_tile
            def normed(b, p):
                wait(dve, X["lnp"], b)
                dve.tensor_scalar(yo[p][:, :], yr[p][:, :], mv[p][:, 0:1], rs[p][:, 0:1], ALU.subtract, ALU.mult).then_inc(X["yo"].sem, 1)

            def slot(at):
                residual(*at(5))
                statistics(*at(5))
                tile_copied(*at(0))
                mean_and_variance(*at(5))
                guarded(*at(5))
                token_numbers(*at(6))
                normed(*at(6))
                hidden(*at(2))
            slots(dve, slot, 8, 6, NT)

        def experts_gpsimd(pool):
            @per_tile
            def inverse_deviation(b, p):
                wait(pool, X["ln"], b, 3)
                wait(pool, X["yo"], b - 2)
                pool.tensor_tensor(rs[p][:, :], ve[p][:, :], mhalf[:, 0:1], ALU.pow).then_inc(X["lnp"].sem, 1)

            @per_tile
            def scatter(b, p):
                wait(pool, X["no"], b)
                wait(pool, X["yo"], b)
                free(pool)
                pool.indirect_dma_start(out.rearrange("b s c -> (b s) c"), bass.IndirectOffsetOnAxis(ap=number[p][:, :], axis=0),
                                        yo[p][:, :], None, bounds_check=B * S - 1, oob_is_err=False).then_inc(y_out[p], 16)

            def slot(at):
                scatter(*at(6))
                inverse_deviation(*at(5))
            slots(pool, slot, 8, 6, NT)

        cmean = sb("cmean", [CT, B])
        cvar = sb("cvar", [CT, B])
        crs = sb("crs", [CT, B])
        c_steps = sem("c_steps")
        c_rs = sem("c_rs")

        def setup_vector(dve):
            def link(ins, n):
                ins.then_inc(c_steps, 1)
                dve.wait_ge(c_steps, n)

            for t in (qkr[0], qkr[1]):
                dve.memset(t[:, :, :], 0.0)
            for t in (kd[0], kd[1]):
                dve.memset(t[:, :, :, :], 0.0)
            dve.memset(parts[:, :, :], 0.0)
            dve.memset(ones[:, :], 1.0)
            dve.memset(tot1[:, :, 0:1], 0.0)
            dve.memset(goes_on[:, :, 0:1], 0.0)
            dve.memset(goes_on[:, :, 1:B + 1], 1.0)
            dve.memset(one_e[:, :], 1.0)
            dve.memset(tend[:, 0:1], 0.0).then_inc(made, 1)
            dve.wait_ge(made, 1)
            dve.wait_ge(ld["ctx"], ld_n["ctx"])

            def per_token(ap):
                return ap.rearrange("p (b o) -> p b o", o=1).to_broadcast((CT, B, CC))

            link(dve.tensor_reduce(cmean[:, :], ctx_in[:, :, :], AX.X, ALU.add), 1)
            link(dve.tensor_scalar(cmean[:, :], cmean[:, :], 1.0 / CC, None, ALU.mult), 2)
            link(dve.tensor_tensor(cdev[:, :, :], ctx_in[:, :, :], per_token(cmean[:, :]), ALU.subtract), 3)
            link(dve.tensor_tensor(csq[:, :, :], cdev[:, :, :], cdev[:, :, :], ALU.mult), 4)
            link(dve.tensor_reduce(cvar[:, :], csq[:, :, :], AX.X, ALU.add), 5)
            link(dve.tensor_scalar(cvar[:, :], cvar[:, :], 1.0 / CC, EPS, ALU.mult, ALU.add), 6)
            dve.wait_ge(c_rs, 1)
            link(dve.tensor_tensor(ctxn[:, :, :], cdev[:, :, :], per_token(crs[:, :]), ALU.mult), 7)

        def constants_vector(dve):
            dve.wait_ge(ld["const"], ld_n["const"])
            dve.tensor_copy(bc_sel[:, :, :], bc_f[:, :, :]).then_inc(const_ready, 1)
            dve.tensor_copy(x3[:, :, C:CW].rearrange("p b o -> p (b o)").bitcast(I32), token[:, :]).then_inc(const_ready, 1)

        block = ctx.enter_context(nc.Block())

        @block.vector
        def _(dve):
            setup_vector(dve)
            retention_vector(dve)
            constants_vector(dve)
            for phase in phases:
                phase["vector"](dve)
            place_vector(dve)
            experts_vector(dve)

        @block.sync
        def _(sp):
            def load(group, dst, src):
                sp.dma_start(dst, src).then_inc(ld[group], 16)
            for group, dst, src in loads_first:
                load(group, dst, src)
            retention_sync(sp)
            for group, dst, src in loads_later:
                load(group, dst, src)
            sp.dma_start(xs_dram, A["blank_rows"]).then_inc(blanked, 16)
            experts_sync(sp)

        @block.tensor
        def _(pe):
            retention_tensor(pe)
            pe.wait_ge(const_ready, 1)
            for phase in phases:
                phase["tensor"](pe)
            place_tensor(pe)
            experts_tensor(pe)

        @block.scalar
        def _(act):
            retention_scalar(act)
            for phase in phases:
                phase["scalar"](act)
            experts_scalar(act)

        @block.gpsimd
        def _(pool):
            pool.memset(mhalf[:, :], -0.5).then_inc(made2, 1)
            pool.memset(ctx_half[:, :], -0.5).then_inc(made2, 1)
            pool.wait_ge(made2, 2)
            pool.wait_ge(c_steps, 6)
            pool.tensor_tensor(crs[:, :], cvar[:, :], ctx_half[:, :], ALU.pow).then_inc(c_rs, 1)
            pool.wait_ge(ld["ret"], ld_n["ret"])
            retention_gpsimd(pool)
            for phase in phases:
                phase["gpsimd"](pool)
            place_gpsimd(pool)
            experts_gpsimd(pool)


def constants():
    f = np.float32
    inv = (f(1.0) / f(10000.0) ** (np.arange(0, RD, 2, dtype=f) / f(RD))).astype(f)
    ang = np.arange(S, dtype=f)[:, None] * inv[None, :]
    cos, sin = np.cos(ang), np.sin(ang)
    cos = np.repeat(cos, 2, axis=1)
    sin = np.stack([-sin, sin], axis=-1).reshape(S, RD)
    decay = np.zeros((S, 2, 4, S))
    diff = np.arange(S)[None, :] - np.arange(S)[:, None]
    for h in range(RH):
        slope = np.log2(1.0 - 2.0 ** (-5.0 - h))
        decay[:, h // 4, h % 4, :] = np.where(diff >= 0, np.exp2(np.maximum(diff, 0) * slope), 0.0) * RD ** -0.5
    bc = np.zeros((128, HG, 128))
    for hg in range(HG):
        for g in range(4):
            for j in (hg, 16 + hg):
                bc[32 * g + j, hg, 32 * g:32 * g + 32] = 1.0
    out = {"cos": np.tile(cos, (1, 2 * RH)), "sin": np.tile(sin, (1, 2 * RH)), "decay": decay, "ident": np.eye(128),
           "bc_sel": bc, "later": np.tril(np.ones((S, S)), -1), "tri": np.triu(np.ones((S, S)), 1),
           "rank_code": NE - np.arange(NE)[None, :], "tile_at": np.tile(S * np.arange(B), NE)[None, :], "tile_no": np.arange(NT)[None, :]}
    out = {k: np.ascontiguousarray(v.astype(f)) for k, v in out.items()}
    out["token"] = np.ascontiguousarray(np.arange(B * S, dtype=np.int32).reshape(B, S).T)
    blank = np.zeros((NT * S, C + 1), np.int32)
    blank[:, C] = B * S + np.arange(NT * S)
    out["blank_rows"] = blank.view(f)
    return out


def laid_out(i):
    t = {"x": i["x"], "xT": i["x"].transpose(2, 0, 1), "ctx": i["ctx_512"],
         "wqk": np.concatenate([i["L0_attn_Wq"], i["L0_attn_Wk"]], 1), "wvg": np.concatenate([i["L0_attn_Wv"], i["L0_attn_Wg"]], 1),
         "wo": i["L0_attn_Wo"].reshape(2, 128, C).transpose(1, 0, 2), "gw": np.tile(i["L0_attn_g_norm_w"], RH)[None, :],
         "router": i["L0_ffn_router_w"].T,
         "egu": np.concatenate([i["L0_ffn_gate_w"], i["L0_ffn_up_w"]], 1).transpose(2, 0, 1),
         "edn": i["L0_ffn_down_w"].transpose(2, 0, 1)}
    for n, a in enumerate(("a1", "a2")):
        p = f"L0_xattn_{a}_"
        for k in ("wq", "wk", "wv"):
            w = i[p + k]
            t[f"{a}_{k}"] = w.transpose(1, 0, 2).reshape(w.shape[1], AH * AD)
        t[a + "_li1"] = i[p + "li1_w"].reshape(HG, 128, C).transpose(1, 0, 2)
        t[a + "_li1b"] = i[p + "li1_b"][None, :]
        for k in ("lnx", "lny", "ln3"):
            t[f"{a}_{k}"] = np.stack([i[p + k + "_g"], i[p + k + "_b"]], 1)
        t[a + "_g"] = i[f"L0_xattn_ln{n + 1}_g"][None, :]
        t[a + "_b"] = i[f"L0_xattn_ln{n + 1}_b"][None, :]
        t[a + "_li2"] = i[p + "li2_w"]
        t[a + "_li2b"] = i[p + "li2_b"].reshape(4, 128).T
        t[a + "_li3"] = i[p + "li3_w"].reshape(4, 128, C).transpose(1, 0, 2)
        t[a + "_li3b"] = i[p + "li3_b"][None, :]
    return {k: np.ascontiguousarray(v) for k, v in t.items()} | constants()


def kernel(**inputs):
    import concourse.bacc as _bacc
    from concourse.bass_utils import run_bass_kernel_spmd as _run

    arrays = laid_out({k: np.asarray(v) for k, v in inputs.items()})
    nc = _bacc.Bacc("TRN2", target_bir_lowering=False, num_devices=1)
    aps = {k: nc.dram_tensor("in_" + k, v.shape, mybir.dt.from_np(v.dtype), kind="ExternalInput").ap() for k, v in arrays.items()}
    out = nc.dram_tensor("out", (B, S, C), F32, kind="ExternalOutput").ap()
    build(nc, aps, out)
    r = _run(nc, [{"in_" + k: v for k, v in arrays.items()}], core_ids=[0])
    return r.results[0]["out"]
```

```python
import concourse.bass as bass
import numpy as np
from concourse import mybir
from contextlib import ExitStack

F32 = mybir.dt.float32
F32R = mybir.dt.float32r
I32 = mybir.dt.int32
ACT = mybir.ActivationFunctionType
ALU = mybir.AluOpType
AX = mybir.AxisListType

B, S, C = 16, 128, 128
CT, CC = 77, 64
RH, RD, RV = 8, 16, 32
AH, AD = 16, 32
HG = AH // 4
FF = 4 * C
NE, EI = 8, 352
EC = [128, 128, 96]
NT = B + NE - 1
EPS = 1e-5


class Steps:

    def __init__(self, sem, per, start=0):
        self.sem, self.per, self.start = sem, per, start

    def next_phase(self):
        return Steps(self.sem, self.per, self.start + B)

    def at(self, b, k=None):
        return (b + self.start) * self.per + (self.per if k is None else k)


def wait(eng, steps, b, k=None):
    if isinstance(b, int) and b + steps.start < 0:
        return
    eng.wait_ge(steps.sem, steps.at(b, k))


def after(eng, b, freed):
    if isinstance(b, int) and b == 0:
        for steps in freed:
            wait(eng, steps, B - 1)


def live(b, n=B):
    return not isinstance(b, int) or 0 <= b < n


def per_batch_of(n):
    def per_batch(step):
        def run(b, p, *which):
            if live(b, n):
                step(b, p, *which)
        return run
    return per_batch


per_batch = per_batch_of(B)


def batch_at(t, parity):
    return lambda k: (t - k, (parity + k) % 2)


def run_phases(eng, name, phases):
    slot, begun = phases[0][name](eng), 0
    for n, phase in enumerate(phases):
        for t in range(begun, phase["peel"]):
            slot(batch_at(t, t % 2))
        if phase["peel"] < B:
            with eng.Fori(phase["peel"] // 2, B // 2) as i:
                slot(batch_at(i * 2, 0))
                slot(batch_at(i * 2 + 1, 1))
        following, begun = phases[n + 1][name](eng) if n + 1 < len(phases) else None, 0
        for t in range(B, B + phase["skew"]):
            slot(batch_at(t, t % 2))
            if following and t >= B + phase["join"][name]:
                following(batch_at(begun, begun % 2))
                begun += 1
        slot = following


def slots(eng, slot, peel, skew, n=B):
    last = peel + (n - peel) // 2 * 2
    for t in range(peel):
        slot(batch_at(t, t % 2))
    with eng.Fori(peel // 2, last // 2) as i:
        slot(batch_at(i * 2, 0))
        slot(batch_at(i * 2 + 1, 1))
    for t in range(last, n + skew):
        slot(batch_at(t, t % 2))


def one(b):
    return bass.ds(b, 1)


def build(nc, A, out):
    ctx = ExitStack()
    with ctx:
        def sb(name, shape, dt=F32):
            return ctx.enter_context(nc.sbuf_tensor(name, shape, dt))

        def sem(name):
            return ctx.enter_context(nc.semaphore(name))

        ticks = sem("ticks")

        def free(eng):
            eng.sem_inc(ticks, 1)

        def stats(name, n):
            return [sb(f"{name}{p}", [S, n]) for p in range(2)]

        def steps(name, per=1):
            return Steps(sem(name), per)

        bank = [ctx.enter_context(nc.psum_tensor(f"bank{k}", [128, 512], F32)) for k in range(8)]
        CW = C + 1
        xs_dram = nc.dram_tensor("sorted_x", [NT * S, CW], F32, kind="Internal").ap()

        xin = sb("xin", [S, B, C])
        x1 = sb("x1", [S, B, C])
        xa = sb("xa", [S, B, C])
        xo = sb("xo", [S, B, C])
        z = xin
        x3 = sb("x3", [S, B, CW])
        ctxn = sb("ctxn", [CT, B, CC])

        wqk = sb("wqk", [C, 2 * RH * RD])
        wvg = sb("wvg", [C, 2 * RH * RV])
        wo = sb("wo", [128, 2, C])
        gw = sb("gw", [S, RH * RV])
        cos_t = sb("cos_t", [S, 2 * RH * RD])
        sin_t = sb("sin_t", [S, 2 * RH * RD])
        decay = sb("decay", [S, 2, 4, S])
        ident = sb("ident", [128, 128])
        att_w, mlp_w = [], []
        for a, kc in (("a1", C), ("a2", CC)):
            att_w.append({"wq": sb(a + "wq", [C, 512]), "wk": sb(a + "wk", [kc, 512]), "wv": sb(a + "wv", [kc, 512]),
                          "li1": sb(a + "li1", [128, HG, C]), "li1b": sb(a + "li1b", [S, C]),
                          "lnx": sb(a + "lnx", [C, 2]), "lny": sb(a + "lny", [kc, 2]),
                          "g": sb(a + "g", [S, C]), "b": sb(a + "b", [S, C])})
            mlp_w.append({"li2": sb(a + "li2", [C, FF]), "li2b": sb(a + "li2b", [128, 4]),
                          "li3": sb(a + "li3", [128, 4, C]), "li3b": sb(a + "li3b", [S, C]), "ln3": sb(a + "ln3", [C, 2])})
        router = sb("router", [C, NE])
        egu = sb("egu", [C, NE, 2 * EI])
        edn = sb("edn", [128, NE, 3, C])

        later = sb("later", [S, S])
        bc_f = sb("bc_f", [128, HG, 128])
        bc_sel = sb("bc_sel", [128, HG, 128], F32R)
        mhalf = sb("mhalf", [128, RH])

        ctx_in, cdev = (x3[0:CT, :, :].rearrange("p b c -> p (b c)")[:, k * B * CC:(k + 1) * B * CC].rearrange("p (b c) -> p b c", c=CC)
                        for k in range(2))
        csq = ctxn

        token = sb("token", [S, B], I32)
        rank_code = sb("rank_code", [S, NE])
        tri = sb("tri", [S, S])
        tile_at = sb("tile_at", [S, NE, B])
        tile_no = sb("tile_no", [S, NT])

        def rows(ap, n=S):
            return ap.to_broadcast((n, ap.shape[1]))

        loads_first = [("proj", wqk[:, :], A["wqk"]), ("rope", cos_t[:, :], A["cos"]), ("rope", sin_t[:, :], A["sin"]),
                       ("proj2", wvg[:, :], A["wvg"]), ("ret", ident[:, :], A["ident"]), ("ret", gw[:, :], rows(A["gw"])),
                       ("ret", decay[:, :, :, :], A["decay"]), ("ret", wo[:, :, :], A["wo"]),
                       ("ctx", ctx_in[:, :, :], A["ctx"].rearrange("b t c -> t b c")),
                       ("x", xin[:, :, :], A["x"].rearrange("b s c -> s b c"))]
        loads_later = [("const", bc_f[:, :, :], A["bc_sel"]), ("const", token[:, :], A["token"]), ("a1", later[:, :], A["later"])]
        for n, a in enumerate(("a1", "a2")):
            wa, wm = att_w[n], mlp_w[n]
            loads_later += [(a, wa["wq"][:, :], A[a + "_wq"]), (a, wa["wk"][:, :], A[a + "_wk"]), (a, wa["wv"][:, :], A[a + "_wv"]),
                            (a, wa["li1"][:, :, :], A[a + "_li1"]), (a, wa["li1b"][:, :], rows(A[a + "_li1b"])),
                            (a, wa["lnx"][:, :], A[a + "_lnx"]), (a, wa["lny"][:, :], A[a + "_lny"]),
                            (a, wa["g"][:, :], rows(A[a + "_g"])), (a, wa["b"][:, :], rows(A[a + "_b"]))]
            m = "m" + a[1]
            loads_later += [(m, wm["li2"][:, :], A[a + "_li2"]), (m, wm["li2b"][:, :], A[a + "_li2b"]), (m, wm["li3"][:, :, :], A[a + "_li3"]),
                            (m, wm["li3b"][:, :], rows(A[a + "_li3b"])), (m, wm["ln3"][:, :], A[a + "_ln3"])]
        loads_later += [("exp", router[:, :], A["router"]), ("exp", egu[:, :, :], A["egu"])]
        loads_later += [("exp", edn[0:n, :, c, :], A["edn"][c * 128:c * 128 + n, :, :]) for c, n in enumerate(EC)]
        loads_later += [("exp", rank_code[:, :], rows(A["rank_code"])), ("exp", tri[:, :], A["tri"]),
                        ("exp", tile_at[:, :, :].rearrange("p a b -> p (a b)"), rows(A["tile_at"])), ("exp", tile_no[:, :], rows(A["tile_no"]))]
        ld = {k: sem("ld_" + k) for k in ("proj", "rope", "proj2", "ret", "ctx", "x", "const", "a1", "m1", "a2", "m2", "exp")}
        ld_n = {k: 16 * sum(g == k for g, _, _ in loads_first + loads_later) for k in ld}
        const_ready = sem("const_ready")
        vector_made = sem("vector_made")
        pool_made = sem("pool_made")
        ctx_half = sb("ctx_half", [CT, B])

        arena = sb("arena", [128, 4 * 4 * 512])
        taken = [0]

        def carve(name, shape):
            n = int(np.prod(shape[1:]))
            ap = arena[0:shape[0], taken[0]:taken[0] + n]
            taken[0] += n
            if len(shape) == 3:
                ap = ap.rearrange("p (a b) -> p a b", b=shape[2])
            if len(shape) == 4:
                ap = ap.rearrange("p (a b c) -> p a b c", b=shape[2], c=shape[3])
            return ap

        xT = [sb(f"xT{p}", [C, S]) for p in range(2)]
        kd = [sb(f"kd{p}", [128, HG, 4, S]) for p in range(2)]
        rqd = [kd[p][:, 0:2, :, :] for p in range(2)]
        rope_c = carve("rope_c", [S, 2 * RH * RD])
        rope_s = carve("rope_s", [S, 2 * RH * RD])
        qkr = [carve(f"qkr{p}", [S, 2 * RH, 32]) for p in range(2)]
        rkT = [carve(f"rkT{p}", [128, 2, S]) for p in range(2)]
        rv = [carve(f"rv{p}", [S, RH * RV]) for p in range(2)]
        rprob = [carve(f"rprob{p}", [S, 2, 4, S]) for p in range(2)]
        rsg = carve("rsg", [S, RH * RV])
        rgate = [carve(f"rgate{p}", [S, RH * RV]) for p in range(2)]
        roT = carve("roT", [128, 2 * S])
        rnat = [carve(f"rnat{p}", [S, RH * RV]) for p in range(2)]
        rsq = carve("rsq", [S, RH * RV])
        rms = [carve(f"rms{p}", [S, RH]) for p in range(2)]
        rrs = [carve(f"rrs{p}", [S, RH]) for p in range(2)]
        ry0 = carve("ry_part", [S, RH * RV])
        ry = [carve(f"ry{p}", [S, RH * RV]) for p in range(2)]
        ryT = carve("ryT", [128, 2, S])
        taken[0] = 0
        zt = [sb(f"zt{p}", [S, C]) for p in range(2)]
        st = [sb(f"st{p}", [S, 6]) for p in range(2)]
        mv = [sb(f"mv{p}", [S, 2]) for p in range(2)]
        ve = [sb(f"ve{p}", [S, 1]) for p in range(2)]
        rs = [sb(f"rs{p}", [S, 1]) for p in range(2)]
        st2 = [sb(f"st2{p}", [S, 6]) for p in range(2)]
        mv2 = [sb(f"mv2{p}", [S, 2]) for p in range(2)]
        ve2 = [sb(f"ve2{p}", [S, 1]) for p in range(2)]
        rs2 = [sb(f"rs2{p}", [S, 1]) for p in range(2)]

        xT_in = [sem(f"xT_in{p}") for p in range(2)]
        R = {k: steps("r_" + k, n) for k, n in {
            "qk": 1, "vg": 1, "rope": 3, "t4": 1, "qkT": 5, "silu": 1, "v": 1, "gate": 1, "st": 2, "prob": 2, "av": 1,
            "oT": 1, "to": 1, "nat": 2, "ms": 2, "rs": 1, "y": 2, "ty": 1, "yT": 1, "wo": 1, "ln": 4, "lnp": 1, "x1": 1}.items()}
        r_st, r_mv, r_ve, r_rs = stats("r_st", 6), stats("r_mv", 2), stats("r_ve", 1), stats("r_rs", 1)
        bQK, bVG, bT, bY = bank[0], bank[1], bank[2], bank[3]
        bS, bA, bN = bank[4:6], bank[6], bank[7]

        def retention_sync(sp):
            @per_batch
            def load_xT(b, p):
                wait(sp, R["vg"], b - 2)
                sp.dma_start(xT[p][:, :], A["xT"][:, one(b), :]).then_inc(xT_in[p], 16)

            load_xT(0, 0)
            load_xT(1, 1)
            for group, dst, src in loads_first:
                sp.dma_start(dst, src).then_inc(ld[group], 16)
            for b in (2, 3):
                load_xT(b, b % 2)
                for group, dst, src in loads_later:
                    if group == ("const", "a1")[b - 2]:
                        sp.dma_start(dst, src).then_inc(ld[group], 16)
            with sp.Fori(2, B // 2) as i:
                load_xT(i * 2, 0)
                load_xT(i * 2 + 1, 1)

        def retention_tensor(pe):
            pe.wait_ge(ld["proj"], ld_n["proj"])

            @per_batch
            def project_qk(b, p):
                pe.wait_ge(xT_in[p], (b - p) * 8 + 16)
                wait(pe, R["rope"], b - 1, 2)
                pe.matmul(bQK[:, 0:256], xT[p][:, :], wqk[:, :], start=True, stop=True).then_inc(R["qk"].sem, 1)

            @per_batch
            def project_vg(b, p):
                if isinstance(b, int) and b == 0:
                    pe.wait_ge(ld["proj2"], ld_n["proj2"])
                wait(pe, R["silu"], b - 1)
                wait(pe, R["v"], b - 1)
                pe.matmul(bVG[:, :], xT[p][:, :], wvg[:, :], start=True, stop=True).then_inc(R["vg"].sem, 1)

            @per_batch
            def transpose_qk(b, p):
                if isinstance(b, int) and b == 0:
                    pe.wait_ge(ld["ret"], ld_n["ret"])
                wait(pe, R["rope"], b)
                wait(pe, R["qkT"], b - 1)
                for c in range(4):
                    src = qkr[p][:, 4 * c:4 * c + 4, :].rearrange("p a b -> p (a b)")
                    last = pe.transpose(bT[:, c * 128:(c + 1) * 128], src, ident[:, :])
                last.then_inc(R["t4"].sem, 1)

            @per_batch
            def scores(b, p, c):
                wait(pe, R["qkT"], b)
                wait(pe, R["prob"], b - 1, c + 1)
                pe.matmul(bS[c][:, :], rkT[p][:, c, :], rqd[p][:, c, :, :].rearrange("p a b -> p (a b)"),
                          start=True, stop=True).then_inc(R["st"].sem, 1)

            @per_batch
            def weighted_values(b, p):
                wait(pe, R["prob"], b)
                wait(pe, R["v"], b)
                wait(pe, R["oT"], b - 1)
                for c in range(2):
                    for g in range(4):
                        h = 4 * c + g
                        last = pe.matmul(bA[32 * g:32 * g + 32, c * S:(c + 1) * S], rv[p][:, h * RV:(h + 1) * RV],
                                         rprob[p][:, c, g, :], start=True, stop=True)
                last.then_inc(R["av"].sem, 1)

            @per_batch
            def transpose_o(b, p):
                wait(pe, R["oT"], b)
                wait(pe, R["nat"], b - 1)
                for c in range(2):
                    last = pe.transpose(bN[:, c * 128:(c + 1) * 128], roT[:, c * S:(c + 1) * S], ident[:, :])
                last.then_inc(R["to"].sem, 1)

            @per_batch
            def transpose_y(b, p):
                wait(pe, R["y"], b)
                wait(pe, R["ln"], b - 1, 1)
                for c in range(2):
                    last = pe.transpose(bY[:, c * 128:(c + 1) * 128], ry[p][:, c * 128:(c + 1) * 128], ident[:, :])
                last.then_inc(R["ty"].sem, 1)

            @per_batch
            def project_out(b, p):
                wait(pe, R["yT"], b)
                for c in range(2):
                    last = pe.matmul(bY[:, 256:384], ryT[:, c, :], wo[:, c, :], start=(c == 0), stop=(c == 1))
                last.then_inc(R["wo"].sem, 1)

            def slot(at):
                project_vg(*at(1))
                transpose_o(*at(3))
                scores(*at(2), 0)
                transpose_y(*at(4))
                scores(*at(2), 1)
                transpose_qk(*at(1))
                project_out(*at(4))
                project_qk(*at(0))
                weighted_values(*at(2))
            return slot

        def retention_scalar(act):
            @per_batch
            def gate_silu(b, p):
                wait(act, R["vg"], b)
                wait(act, R["gate"], b - 1)
                act.activation(rsg[:, :], bVG[:, 256:512], ACT.Silu).then_inc(R["silu"].sem, 1)

            @per_batch
            def values(b, p):
                wait(act, R["vg"], b)
                wait(act, R["av"], b - 2)
                act.activation(rv[p][:, :], bVG[:, 0:256], ACT.Copy).then_inc(R["v"].sem, 1)

            @per_batch
            def qk_transposed(b, p):
                if isinstance(b, int) and b == 0:
                    act.wait_ge(pool_made, 4)
                wait(act, R["t4"], b)
                wait(act, R["st"], b - 2)
                for g in range(4):
                    rows_g = slice(32 * g, 32 * g + 32)
                    act.activation(rqd[p][rows_g, :, g, :], bT[rows_g, 0:2 * S].rearrange("p (c s) -> p c s", c=2), ACT.Copy)\
                       .then_inc(R["qkT"].sem, 1)
                act.activation(rkT[p][:, :, :].rearrange("p a b -> p (a b)"), bT[:, 2 * S:4 * S], ACT.Copy).then_inc(R["qkT"].sem, 1)

            @per_batch
            def o_transposed(b, p):
                wait(act, R["av"], b)
                wait(act, R["to"], b - 1)
                act.activation(roT[:, :], bA[:, 0:256], ACT.Copy).then_inc(R["oT"].sem, 1)

            @per_batch
            def o_natural(b, p):
                wait(act, R["to"], b)
                wait(act, R["y"], b - 2, 1)
                act.activation(rnat[p][:, :], bN[:, 0:256], ACT.Copy).then_inc(R["nat"].sem, 1)

            @per_batch
            def o_squared(b, p):
                wait(act, R["ms"], b - 1, 1)
                act.activation(rsq[:, :], bN[:, 0:256], ACT.Square).then_inc(R["nat"].sem, 1)

            @per_batch
            def y_transposed(b, p):
                wait(act, R["ty"], b)
                wait(act, R["wo"], b - 1)
                act.activation(ryT[:, :, :].rearrange("p a b -> p (a b)"), bY[:, 0:256], ACT.Copy).then_inc(R["yT"].sem, 1)

            def slot(at):
                o_squared(*at(2))
                values(*at(0))
                gate_silu(*at(0))
                y_transposed(*at(3))
                qk_transposed(*at(0))
                o_transposed(*at(1))
                o_natural(*at(1))
            return slot

        cmean, cvar, crs = (sb(n, [CT, B]) for n in ("cmean", "cvar", "crs"))
        c_steps, c_rs = sem("c_steps"), sem("c_rs")

        def context_norm(dve, t):
            def per_token(ap):
                return ap.rearrange("p (b o) -> p b o", o=1).to_broadcast((CT, B, CC))

            if t:
                dve.wait_ge(c_steps, t)
            else:
                dve.wait_ge(ld["ctx"], ld_n["ctx"])
            if t == 0:
                dve.tensor_reduce(cmean[:, :], ctx_in[:, :, :], AX.X, ALU.add).then_inc(c_steps, 1)
            if t == 1:
                dve.tensor_scalar(cmean[:, :], cmean[:, :], 1.0 / CC, None, ALU.mult).then_inc(c_steps, 1)
            if t == 2:
                dve.tensor_tensor(cdev[:, :, :], ctx_in[:, :, :], per_token(cmean[:, :]), ALU.subtract).then_inc(c_steps, 1)
            if t == 3:
                dve.tensor_tensor(csq[:, :, :], cdev[:, :, :], cdev[:, :, :], ALU.mult).then_inc(c_steps, 1)
            if t == 4:
                dve.tensor_reduce(cvar[:, :], csq[:, :, :], AX.X, ALU.add).then_inc(c_steps, 1)
            if t == 5:
                dve.tensor_scalar(cvar[:, :], cvar[:, :], 1.0 / CC, EPS, ALU.mult, ALU.add).then_inc(c_steps, 1)
            if t == 6:
                dve.wait_ge(c_rs, 1)
                dve.tensor_tensor(ctxn[:, :, :], cdev[:, :, :], per_token(crs[:, :]), ALU.mult).then_inc(c_steps, 1)

        def constants_vector(dve):
            dve.wait_ge(ld["const"], ld_n["const"])
            dve.tensor_copy(bc_sel[:, :, :], bc_f[:, :, :]).then_inc(const_ready, 1)

        def retention_vector(dve):
            dve.wait_ge(ld["rope"], ld_n["rope"])

            @per_batch
            def rotate(b, p):
                wait(dve, R["qk"], b)
                wait(dve, R["rope"], b - 1)
                dve.tensor_tensor(rope_c[:, :], bQK[:, 0:256], cos_t[:, :], ALU.mult).then_inc(R["rope"].sem, 1)
                swapped = bQK[:, 0:256].rearrange("p (n two) -> p n two", two=2)[:, :, ::-1]
                dve.tensor_tensor(rope_s[:, :].rearrange("p (n two) -> p n two", two=2), swapped,
                                  sin_t[:, :].rearrange("p (n two) -> p n two", two=2), ALU.mult).then_inc(R["rope"].sem, 1)

            @per_batch
            def rotated(b, p):
                wait(dve, R["rope"], b, 2)
                wait(dve, R["t4"], b - 2)
                dve.tensor_tensor(qkr[p][:, :, 0:RD], rope_c[:, :].rearrange("p (a b) -> p a b", b=RD),
                                  rope_s[:, :].rearrange("p (a b) -> p a b", b=RD), ALU.add).then_inc(R["rope"].sem, 1)

            @per_batch
            def decayed(b, p, c):
                if isinstance(b, int) and b == 0:
                    dve.wait_ge(ld["ret"], ld_n["ret"])
                wait(dve, R["av"], b - 2)
                wait(dve, R["st"], b, c + 1)
                dve.tensor_tensor(rprob[p][:, c, :, :].rearrange("p a b -> p (a b)"), bS[c][:, :],
                                  decay[:, c, :, :].rearrange("p a b -> p (a b)"), ALU.mult).then_inc(R["prob"].sem, 1)

            @per_batch
            def square_sums(b, p):
                wait(dve, R["nat"], b)
                wait(dve, R["rs"], b - 2)
                dve.tensor_reduce(rms[p][:, :], rsq[:, :].rearrange("p (h d) -> p h d", h=RH), AX.X, ALU.add).then_inc(R["ms"].sem, 1)

            @per_batch
            def mean_squares(b, p):
                wait(dve, R["ms"], b, 1)
                dve.tensor_scalar(rms[p][:, :], rms[p][:, :], 1.0 / RV, EPS, ALU.mult, ALU.add).then_inc(R["ms"].sem, 1)

            @per_batch
            def normed_o(b, p):
                wait(dve, R["rs"], b)
                wait(dve, R["y"], b - 1)
                rb = rrs[p][:, :].rearrange("p (h o) -> p h o", o=1).to_broadcast((S, RH, RV))
                dve.tensor_tensor(ry0[:, :].rearrange("p (h d) -> p h d", h=RH),
                                  rnat[p][:, :].rearrange("p (h d) -> p h d", h=RH), rb, ALU.mult).then_inc(R["y"].sem, 1)

            @per_batch
            def gated_y(b, p):
                wait(dve, R["y"], b, 1)
                wait(dve, R["gate"], b)
                wait(dve, R["ty"], b - 2)
                dve.tensor_tensor(ry[p][:, :], ry0[:, :], rgate[p][:, :], ALU.mult).then_inc(R["y"].sem, 1)

            @per_batch
            def residual(b, p):
                if isinstance(b, int) and b == 0:
                    dve.wait_ge(ld["x"], ld_n["x"])
                wait(dve, R["wo"], b)
                dve.tensor_tensor(zt[p][:, :], bY[:, 256:384], xin[:, one(b), :].rearrange("p a b -> p (a b)"), ALU.add)\
                   .then_inc(R["ln"].sem, 1)

            @per_batch
            def statistics(b, p):
                wait(dve, R["ln"], b, 1)
                free(dve)
                dve.bn_stats(r_st[p][:, :], zt[p][:, :]).then_inc(R["ln"].sem, 1)

            @per_batch
            def mean_and_variance(b, p):
                wait(dve, R["ln"], b, 2)
                free(dve)
                dve.bn_aggr(r_mv[p][:, :], r_st[p][:, :]).then_inc(R["ln"].sem, 1)

            @per_batch
            def guarded(b, p):
                wait(dve, R["ln"], b, 3)
                dve.tensor_scalar(r_ve[p][:, :], r_mv[p][:, 1:2], EPS, None, ALU.add).then_inc(R["ln"].sem, 1)

            @per_batch
            def normed(b, p):
                wait(dve, R["lnp"], b)
                dve.tensor_scalar(x1[:, one(b), :].rearrange("p a b -> p (a b)"), zt[p][:, :], r_mv[p][:, 0:1], r_rs[p][:, :],
                                  ALU.subtract, ALU.mult).then_inc(R["x1"].sem, 1)

            def slot(at):
                rotate(*at(0))
                gated_y(*at(3))
                rotated(*at(0))
                square_sums(*at(2))
                decayed(*at(1), 0)
                mean_squares(*at(2))
                decayed(*at(1), 1)
                normed(*at(4))
                residual(*at(3))
                statistics(*at(3))
                mean_and_variance(*at(3))
                normed_o(*at(2))
                guarded(*at(3))
                t, _ = at(0)
                if isinstance(t, int) and t >= 1:
                    for k in {1: [0, 1], 2: [2], 3: [3], 4: [4, 5]}.get(t, []):
                        context_norm(dve, k)
                    if t == 5:
                        constants_vector(dve)
            return slot

        def retention_gpsimd(pool):
            @per_batch
            def inverse_rms(b, p):
                wait(pool, R["ms"], b)
                wait(pool, R["y"], b - 2, 1)
                pool.tensor_tensor(rrs[p][:, :], rms[p][:, :], mhalf[:, :], ALU.pow).then_inc(R["rs"].sem, 1)

            @per_batch
            def inverse_deviation(b, p):
                wait(pool, R["ln"], b, 4)
                wait(pool, R["x1"], b - 2)
                pool.tensor_tensor(r_rs[p][:, :], r_ve[p][:, :], mhalf[:, 0:1], ALU.pow).then_inc(R["lnp"].sem, 1)

            @per_batch
            def gate(b, p):
                wait(pool, R["silu"], b)
                wait(pool, R["y"], b - 2)
                pool.tensor_tensor(rgate[p][:, :], rsg[:, :], gw[:, :], ALU.mult).then_inc(R["gate"].sem, 1)

            def slot(at):
                inverse_rms(*at(2))
                inverse_deviation(*at(3))
                gate(*at(0))
                t, _ = at(0)
                if isinstance(t, int) and t == 5:
                    pool.wait_ge(c_steps, 6)
                    pool.tensor_tensor(crs[:, :], cvar[:, :], ctx_half[:, :], ALU.pow).then_inc(c_rs, 1)
            return slot

        nat = [sb(f"nat{p}", [S, C]) for p in range(2)]
        cnat = [sb(f"cnat{p}", [CT, CC]) for p in range(2)]
        lnt = sb("lnt", [S, C])
        xnT = sb("xnT", [C, S])
        ynT = sb("ynT", [C, S])
        cnT = sb("cnT", [CC, CT])
        qT = [sb(f"qT{p}", [128, 512]) for p in range(2)]
        vv = [sb(f"vv{p}", [S, 512]) for p in range(2)]
        E = [carve(f"E{p}", [S, HG, 512]) for p in range(2)]
        ET = carve("ET", [S, HG, 512])
        mx = [sb(f"mx{p}", [S, 4, HG]) for p in range(2)]
        den = [sb(f"den{p}", [S, 4, HG]) for p in range(2)]
        rden = sb("rden", [S, 4, HG])
        parts = sb("parts", [S, 4, 32])
        partsT = sb("partsT", [128, S], F32R)
        rbs = sb("rbs", [128, 512])
        oN = sb("oN", [128, 512])
        r1 = [sb(f"r1{p}", [S, C]) for p in range(2)]

        A_STEPS = {k: steps("a_" + k, n) for k, n in {
            "ln": 4, "lnp": 1, "x": 4, "xp": 1, "nat": 1, "t": 1, "xy": 2, "q": 1, "qe": 1, "k": 1, "ke": 2, "kx": 2, "v": 1,
            "ve": 1, "s": 4, "max": 4, "exp": 4, "et": 4, "ete": 4, "rd": 3, "rt": 1, "rte": 1, "av": 1, "rb": 1, "rbe": 1, "mul": 1,
            "li": 1, "res": 1, "r1": 1}.items()}

        def attention(name, w, src, self_attention, src_ready, freed, early_residual=None):
            TK, KC = (S, C) if self_attention else (CT, CC)
            keysT = ynT if self_attention else cnT
            if self_attention:
                P = A_STEPS
            else:
                P = {k: s.next_phase() for k, s in A_STEPS.items()}
                P["cn"] = steps("a_cn")
            if early_residual:
                P["sum"] = steps("a_sum", 2)
            bQ, bK, bO, bE = bank[0], bank[1], bank[2], bank[3]
            bS = bank[4:8]

            def k_rows(g):
                return bK[32 * g:32 * g + 32, 0:HG * TK].rearrange("p (h t) -> p h t", h=HG)


            def tensor(pe):
                pe.wait_ge(ld[name], ld_n[name])

                @per_batch
                def transpose_normed(b, p):
                    after(pe, b, freed["bK"])
                    wait(pe, P["nat"], b)
                    wait(pe, P["ke"], b - 1)
                    wait(pe, P["kx"], b - 1)
                    free(pe)
                    last = pe.transpose(bK[:, 0:S], nat[p][:, :], ident[:, :])
                    if not self_attention:
                        wait(pe, P["cn"], b)
                        free(pe)
                        last = pe.transpose(bK[0:CC, S:S + CT], cnat[p][:, :], ident[0:CT, 0:CT])
                    last.then_inc(P["t"].sem, 1)

                @per_batch
                def project_q(b, p):
                    after(pe, b, freed["bQ"])
                    wait(pe, P["xy"], b)
                    wait(pe, P["ve"], b - 1)
                    for hg in range(HG):
                        last = pe.matmul(bQ[:, hg * S:(hg + 1) * S], w["wq"][:, hg * 128:(hg + 1) * 128], xnT[:, :],
                                         start=True, stop=True)
                    last.then_inc(P["q"].sem, 1)

                @per_batch
                def project_k(b, p):
                    wait(pe, P["xy"], b)
                    for hg in range(HG):
                        last = pe.matmul(bK[:, hg * TK:(hg + 1) * TK], w["wk"][:, hg * 128:(hg + 1) * 128], keysT[0:KC, 0:TK],
                                         start=True, stop=True)
                    last.then_inc(P["k"].sem, 1)

                @per_batch
                def project_v(b, p):
                    wait(pe, P["xy"], b)
                    wait(pe, P["qe"], b)
                    pe.matmul(bQ[0:TK, :], keysT[0:KC, 0:TK], w["wv"][:, :], start=True, stop=True).then_inc(P["v"].sem, 1)

                @per_batch
                def scores(b, p, hg):
                    wait(pe, P["qe"], b)
                    wait(pe, P["ke"], b)
                    wait(pe, P["kx"], b)
                    if hg == 0:
                        after(pe, b, freed["bS"])
                    wait(pe, P["exp"], b - 1, hg + 1)
                    pe.matmul(bS[hg][:, 0:4 * TK], qT[p][:, hg * S:(hg + 1) * S], kd[p][:, hg, :, 0:TK],
                              start=True, stop=True).then_inc(P["s"].sem, 1)

                @per_batch
                def transpose_exp(b, p, hg):
                    if hg == 0:
                        after(pe, b, freed["bE"])
                    wait(pe, P["exp"], b, hg + 1)
                    if hg:
                        wait(pe, P["ete"], b, hg)
                    else:
                        wait(pe, P["rbe"], b - 1)
                    free(pe)
                    for g in range(4):
                        last = pe.transpose(bE[0:TK, g * S:(g + 1) * S], E[p][:, hg, g * TK:(g + 1) * TK], ident[:, :])
                    last.then_inc(P["et"].sem, 1)

                @per_batch
                def weighted_values(b, p):
                    after(pe, b, freed["bO"])
                    wait(pe, P["ve"], b)
                    wait(pe, P["ete"], b)
                    wait(pe, P["res"], b - 1)
                    for hg in range(HG):
                        for g in range(4):
                            h = 4 * hg + g
                            last = pe.matmul(bO[32 * g:32 * g + 32, hg * S:(hg + 1) * S], vv[p][0:TK, h * AD:(h + 1) * AD],
                                             ET[0:TK, hg, g * S:(g + 1) * S], start=True, stop=True)
                    last.then_inc(P["av"].sem, 1)

                @per_batch
                def transpose_reciprocals(b, p):
                    wait(pe, P["rd"], b)
                    wait(pe, P["ete"], b)
                    free(pe)
                    pe.transpose(bE[:, 0:S], parts[:, :, :].rearrange("p a b -> p (a b)"), ident[:, :]).then_inc(P["rt"].sem, 1)

                @per_batch
                def spread_reciprocals(b, p):
                    if isinstance(b, int) and b == 0:
                        pe.wait_ge(const_ready, 1)
                    wait(pe, P["rte"], b)
                    for hg in range(HG):
                        last = pe.matmul(bE[:, hg * S:(hg + 1) * S], bc_sel[:, hg, :], partsT[:, :], start=True, stop=True)
                    last.then_inc(P["rb"].sem, 1)

                @per_batch
                def project_out(b, p):
                    wait(pe, P["mul"], b)
                    for hg in range(HG):
                        last = pe.matmul(bO[:, 0:C], oN[:, hg * S:(hg + 1) * S], w["li1"][:, hg, :],
                                         start=(hg == 0), stop=(hg == HG - 1))
                    last.then_inc(P["li"].sem, 1)

                def slot(at):
                    if self_attention:
                        weighted_values(*at(4))
                        transpose_exp(*at(3), 0)
                        scores(*at(3), 3)
                        project_v(*at(2))
                        transpose_exp(*at(3), 1)
                        transpose_normed(*at(1))
                        scores(*at(2), 0)
                        transpose_exp(*at(3), 2)
                        scores(*at(2), 1)
                        project_k(*at(1))
                        transpose_exp(*at(3), 3)
                        project_out(*at(4))
                        project_q(*at(1))
                        transpose_reciprocals(*at(3))
                        scores(*at(2), 2)
                        spread_reciprocals(*at(3))
                    else:
                        spread_reciprocals(*at(4))
                        weighted_values(*at(4))
                        transpose_exp(*at(3), 0)
                        scores(*at(2), 0)
                        project_v(*at(2))
                        transpose_exp(*at(3), 1)
                        transpose_normed(*at(1))
                        project_out(*at(4))
                        transpose_exp(*at(3), 2)
                        scores(*at(2), 1)
                        scores(*at(2), 2)
                        transpose_exp(*at(3), 3)
                        project_k(*at(1))
                        scores(*at(2), 3)
                        transpose_reciprocals(*at(3))
                        project_q(*at(1))
                return slot

            def scalar(act):
                act.wait_ge(ld[name], ld_n[name])

                @per_batch
                def tokens_and_keys(b, p):
                    wait(act, P["t"], b)
                    wait(act, P["k"], b - 1)
                    wait(act, P["v"], b - 1)
                    act.activation(xnT[:, :], bK[:, 0:S], ACT.Identity, bias=w["lnx"][:, 1:2], scale=w["lnx"][:, 0:1])\
                       .then_inc(P["xy"].sem, 1)
                    ky = bK[0:KC, 0:S] if self_attention else bK[0:KC, S:S + CT]
                    act.activation(keysT[0:KC, 0:TK], ky, ACT.Identity, bias=w["lny"][:, 1:2], scale=w["lny"][:, 0:1])\
                       .then_inc(P["xy"].sem, 1)

                @per_batch
                def queries(b, p):
                    wait(act, P["q"], b)
                    wait(act, P["s"], b - 2)
                    act.activation(qT[p][:, :], bQ[:, :], ACT.Copy, scale=AD ** -0.5).then_inc(P["qe"].sem, 1)

                @per_batch
                def half_of_keys(b, p):
                    after(act, b, freed["kd"])
                    wait(act, P["k"], b)
                    wait(act, P["s"], b - 2)
                    for g in (0, 1):
                        act.activation(kd[p][32 * g:32 * g + 32, :, g, 0:TK], k_rows(g), ACT.Copy).then_inc(P["ke"].sem, 1)

                @per_batch
                def values(b, p):
                    wait(act, P["v"], b)
                    wait(act, P["av"], b - 2)
                    act.activation(vv[p][0:TK, :], bQ[0:TK, :], ACT.Copy).then_inc(P["ve"].sem, 1)

                @per_batch
                def exponentials(b, p, hg):
                    if hg == 0:
                        after(act, b, freed["E"])
                    wait(act, P["max"], b, hg + 1)
                    wait(act, P["et"], b - 2, hg + 1)
                    wait(act, P["rd"], b - 2, 1)
                    for g in range(4):
                        last = act.activation(E[p][:, hg, g * TK:(g + 1) * TK], bS[hg][:, g * TK:(g + 1) * TK], ACT.Exp,
                                              bias=mx[p][:, hg, g:g + 1], accum_out=den[p][:, hg, g:g + 1])
                    last.then_inc(P["exp"].sem, 1)

                @per_batch
                def spread_reciprocals(b, p):
                    wait(act, P["rb"], b)
                    wait(act, P["mul"], b - 1)
                    act.activation(rbs[:, :], bE[:, :], ACT.Copy).then_inc(P["rbe"].sem, 1)

                def slot(at):
                    if self_attention:
                        queries(*at(2))
                        half_of_keys(*at(2))
                        exponentials(*at(3), 2)
                        exponentials(*at(3), 3)
                        tokens_and_keys(*at(1))
                        values(*at(2))
                        exponentials(*at(2), 0)
                        exponentials(*at(2), 1)
                        spread_reciprocals(*at(3))
                    else:
                        spread_reciprocals(*at(4))
                        exponentials(*at(3), 1)
                        exponentials(*at(3), 2)
                        exponentials(*at(3), 3)
                        values(*at(2))
                        tokens_and_keys(*at(1))
                        exponentials(*at(2), 0)
                        half_of_keys(*at(1))
                        queries(*at(1))
                return slot

            def vector(dve):
                dve.wait_ge(ld[name], ld_n[name])

                def x_in(b):
                    return src[:, one(b), :].rearrange("p a b -> p (a b)")

                def x_out(b):
                    return xa[:, one(b), :].rearrange("p a b -> p (a b)")

                @per_batch
                def statistics(b, p):
                    wait(dve, src_ready, b)
                    wait(dve, P["ln"], b - 1)
                    free(dve)
                    dve.bn_stats(st[p][:, :], x_in(b)).then_inc(P["ln"].sem, 1)

                @per_batch
                def mean_and_variance(b, p):
                    wait(dve, P["ln"], b, 1)
                    free(dve)
                    dve.bn_aggr(mv[p][:, :], st[p][:, :]).then_inc(P["ln"].sem, 1)

                @per_batch
                def guarded(b, p):
                    wait(dve, P["ln"], b, 2)
                    wait(dve, P["lnp"], b - 2)
                    dve.tensor_scalar(ve[p][:, :], mv[p][:, 1:2], EPS, None, ALU.add).then_inc(P["ln"].sem, 1)

                @per_batch
                def centred(b, p):
                    wait(dve, P["ln"], b, 2)
                    wait(dve, P["x"], b - 1, 1)
                    dve.scalar_tensor_tensor(lnt[:, :], x_in(b), mv[p][:, 0:1], w["g"][:, :], ALU.subtract, ALU.mult)\
                       .then_inc(P["ln"].sem, 1)

                @per_batch
                def normed(b, p):
                    for s in freed["xa"]:
                        wait(dve, s, b)
                    wait(dve, P["lnp"], b)
                    wait(dve, P["ln"], b, 4)
                    dve.scalar_tensor_tensor(x_out(b), lnt[:, :], rs[p][:, 0:1], w["b"][:, :], ALU.mult, ALU.add)\
                       .then_inc(P["x"].sem, 1)

                @per_batch
                def second_statistics(b, p):
                    wait(dve, P["x"], b, 1)
                    free(dve)
                    dve.bn_stats(st2[p][:, :], x_out(b)).then_inc(P["x"].sem, 1)

                @per_batch
                def second_mean_and_variance(b, p):
                    wait(dve, P["x"], b, 2)
                    free(dve)
                    dve.bn_aggr(mv2[p][:, :], st2[p][:, :]).then_inc(P["x"].sem, 1)

                @per_batch
                def second_guarded(b, p):
                    wait(dve, P["x"], b, 3)
                    wait(dve, P["xp"], b - 2)
                    dve.tensor_scalar(ve2[p][:, :], mv2[p][:, 1:2], EPS, None, ALU.add).then_inc(P["x"].sem, 1)

                @per_batch
                def second_normed(b, p):
                    wait(dve, P["xp"], b)
                    wait(dve, P["t"], b - 2)
                    dve.tensor_scalar(nat[p][:, :], x_out(b), mv2[p][:, 0:1], rs2[p][:, 0:1], ALU.subtract, ALU.mult)\
                       .then_inc(P["nat"].sem, 1)

                @per_batch
                def context(b, p):
                    dve.wait_ge(c_steps, 7)
                    wait(dve, P["t"], b - 2)
                    free(dve)
                    dve.tensor_copy(cnat[p][:, :], ctxn[:, one(b), :].rearrange("p a b -> p (a b)")).then_inc(P["cn"].sem, 1)

                @per_batch
                def half_of_keys(b, p):
                    after(dve, b, freed["kd"])
                    wait(dve, P["k"], b)
                    wait(dve, P["s"], b - 2)
                    free(dve)
                    for g in (2, 3):
                        dve.tensor_copy(kd[p][32 * g:32 * g + 32, :, g, 0:TK], k_rows(g)).then_inc(P["kx"].sem, 1)

                @per_batch
                def maximum(b, p, hg):
                    wait(dve, P["exp"], b - 2, hg + 1)
                    wait(dve, P["s"], b, hg + 1)
                    dve.tensor_reduce(mx[p][:, hg, :], bS[hg][:, 0:HG * TK].rearrange("p (h t) -> p h t", h=HG), AX.X, ALU.max,
                                      negate=True).then_inc(P["max"].sem, 1)

                @per_batch
                def exp_transposed(b, p, hg):
                    if hg == 0:
                        after(dve, b, freed["ET"])
                    wait(dve, P["et"], b, hg + 1)
                    wait(dve, P["av"], b - 1)
                    if self_attention:
                        dve.tensor_tensor(ET[:, hg, :].rearrange("p (h s) -> p h s", h=HG), bE[:, :].rearrange("p (h s) -> p h s", h=HG),
                                          later[:, :].rearrange("p (o s) -> p o s", o=1).to_broadcast((S, HG, S)), ALU.mult)\
                           .then_inc(P["ete"].sem, 1)
                    else:
                        dve.tensor_copy(ET[0:TK, hg, :], bE[0:TK, :]).then_inc(P["ete"].sem, 1)

                rden_g = rden[:, :, :].rearrange("p h g -> p g h")

                @per_batch
                def reciprocals(b, p):
                    wait(dve, P["exp"], b)
                    wait(dve, P["rd"], b - 1)
                    dve.reciprocal(rden[:, :, :], den[p][:, :, :]).then_inc(P["rd"].sem, 1)

                @per_batch
                def high_part(b, p):
                    wait(dve, P["rd"], b, 1)
                    wait(dve, P["rt"], b - 1)
                    dve.tensor_copy(parts[:, :, 0:HG].bitcast(F32R), rden_g).then_inc(P["rd"].sem, 1)

                @per_batch
                def low_part(b, p):
                    wait(dve, P["rd"], b, 2)
                    dve.tensor_tensor(parts[:, :, 16:16 + HG].bitcast(F32R), rden_g, parts[:, :, 0:HG], ALU.subtract)\
                       .then_inc(P["rd"].sem, 1)

                @per_batch
                def transposed_parts(b, p):
                    wait(dve, P["rt"], b)
                    wait(dve, P["rb"], b - 1)
                    dve.tensor_copy(partsT[:, :], bE[:, 0:S]).then_inc(P["rte"].sem, 1)

                @per_batch
                def divided(b, p):
                    wait(dve, P["av"], b)
                    wait(dve, P["rbe"], b)
                    wait(dve, P["li"], b - 1)
                    dve.tensor_tensor(oN[:, :], bO[:, :], rbs[:, :], ALU.mult).then_inc(P["mul"].sem, 1)

                @per_batch
                def residual(b, p):
                    for s in freed["xo"]:
                        wait(dve, s, b)
                    wait(dve, P["li"], b)
                    wait(dve, P["r1"], b)
                    dve.tensor_tensor(xo[:, one(b), :].rearrange("p a b -> p (a b)"), bO[:, 0:C], r1[p][:, :], ALU.add)\
                       .then_inc(P["res"].sem, 1)

                def slot(at):
                    if self_attention:
                        transposed_parts(*at(4))
                        second_guarded(*at(1))
                        statistics(*at(0))
                        half_of_keys(*at(2))
                        maximum(*at(3), 2)
                        divided(*at(4))
                        second_normed(*at(1))
                        exp_transposed(*at(3), 0)
                        mean_and_variance(*at(0))
                        maximum(*at(3), 3)
                        exp_transposed(*at(3), 1)
                        guarded(*at(0))
                        centred(*at(0))
                        exp_transposed(*at(3), 2)
                        maximum(*at(2), 0)
                        normed(*at(0))
                        reciprocals(*at(3))
                        high_part(*at(3))
                        second_statistics(*at(0))
                        low_part(*at(3))
                        exp_transposed(*at(3), 3)
                        maximum(*at(2), 1)
                        residual(*at(4))
                        second_mean_and_variance(*at(0))
                    else:
                        statistics(*at(0))
                        mean_and_variance(*at(0))
                        exp_transposed(*at(3), 2)
                        reciprocals(*at(3))
                        guarded(*at(0))
                        high_part(*at(3))
                        maximum(*at(2), 0)
                        low_part(*at(3))
                        exp_transposed(*at(3), 3)
                        centred(*at(0))
                        context(*at(0))
                        residual(*at(4))
                        transposed_parts(*at(3))
                        normed(*at(0))
                        half_of_keys(*at(1))
                        second_statistics(*at(0))
                        maximum(*at(2), 1)
                        second_mean_and_variance(*at(0))
                        maximum(*at(2), 2)
                        second_guarded(*at(0))
                        maximum(*at(2), 3)
                        exp_transposed(*at(2), 0)
                        second_normed(*at(0))
                        divided(*at(3))
                        exp_transposed(*at(2), 1)
                return slot

            def gpsimd(pool):
                pool.wait_ge(ld[name], ld_n[name])

                @per_batch
                def inverse_deviation(b, p):
                    wait(pool, P["ln"], b, 3)
                    wait(pool, P["x"], b - 2, 1)
                    pool.tensor_tensor(rs[p][:, :], ve[p][:, :], mhalf[:, 0:1], ALU.pow).then_inc(P["lnp"].sem, 1)

                @per_batch
                def second_inverse_deviation(b, p):
                    wait(pool, P["x"], b, 4)
                    wait(pool, P["nat"], b - 2)
                    pool.tensor_tensor(rs2[p][:, :], ve2[p][:, :], mhalf[:, 0:1], ALU.pow).then_inc(P["xp"].sem, 1)

                @per_batch
                def residual_and_bias(b, p):
                    wait(pool, P["x"], b, 1)
                    wait(pool, P["res"], b - 2)
                    pool.tensor_tensor(r1[p][:, :], xa[:, one(b), :].rearrange("p a b -> p (a b)"), w["li1b"][:, :], ALU.add)\
                        .then_inc(P["r1"].sem, 1)

                @per_batch
                def sum_early(b, p):
                    wait(pool, P["x"], b, 1)
                    to, bias, loaded = early_residual
                    if isinstance(b, int) and b == 0:
                        pool.wait_ge(ld[loaded], ld_n[loaded])
                    here = to[:, one(b), :].rearrange("p a b -> p (a b)")
                    free(pool)
                    pool.tensor_tensor(here, here, xa[:, one(b), :].rearrange("p a b -> p (a b)"), ALU.add).then_inc(P["sum"].sem, 1)
                    wait(pool, P["sum"], b, 1)
                    free(pool)
                    pool.tensor_tensor(here, here, bias[:, :], ALU.add).then_inc(P["sum"].sem, 1)

                def slot(at):
                    if self_attention:
                        second_inverse_deviation(*at(1))
                        inverse_deviation(*at(0))
                        residual_and_bias(*at(3))
                    else:
                        inverse_deviation(*at(0))
                        second_inverse_deviation(*at(0))
                        residual_and_bias(*at(2))
                    if early_residual:
                        sum_early(*at(3))
                return slot

            return {"tensor": tensor, "scalar": scalar, "vector": vector, "gpsimd": gpsimd, "steps": P, "peel": 6, "skew": 4}

        n3T = [sb(f"n3T{p}", [C, S]) for p in range(2)]
        hT = [carve(f"hT{p}", [128, 4, S]) for p in range(2)]
        r2 = [sb(f"r2{p}", [S, C]) for p in range(2)]
        r2t = [sb(f"r2t{k}", [S, C]) for k in range(2)]

        x3T = [sb(f"x3T{p}", [C, S]) for p in range(2)]
        x3n = [sb(f"x3n{p}", [S, C]) for p in range(2)]
        logit = sb("logit", [S, B, NE])
        L = {k: steps("l_" + k, n) for k, n in {"ln": 3, "lnp": 1, "x3n": 1, "x3": 1, "t": 1, "te": 1, "mm": 1, "lg": 1}.items()}

        m_st, m_mv, m_ve, m_rs = stats("m_st", 6), stats("m_mv", 2), stats("m_ve", 1), stats("m_rs", 1)
        m_st2, m_mv2, m_ve2, m_rs2 = stats("m_st2", 6), stats("m_mv2", 2), stats("m_ve2", 1), stats("m_rs2", 1)
        m_nat = [sb(f"m_nat{p}", [S, C]) for p in range(2)]
        M_STEPS = {k: steps("m_" + k, n) for k, n in {
            "ln": 3, "lnp": 1, "nat": 1, "t": 1, "te": 1, "up": 1, "gelu": 4, "down": 1, "fin": 1}.items()}

        def mlp(name, w, residuals, att, routed):
            NR = len(residuals) - 1
            if routed:
                P = {k: s.next_phase() for k, s in M_STEPS.items()}
            else:
                P = dict(M_STEPS)
            P["r2"] = steps(name + "_r2", NR)
            bT, bD, bX, bL = bank[0], bank[5], bank[6], bank[7]
            bU = [bank[1], bank[4]]


            def tensor(pe):
                pe.wait_ge(ld[name], ld_n[name])
                if routed:
                    pe.wait_ge(ld["exp"], ld_n["exp"])

                @per_batch
                def transpose_normed(b, p):
                    after(pe, b, [att["ve"]])
                    wait(pe, P["nat"], b)
                    wait(pe, P["te"], b - 1)
                    free(pe)
                    pe.transpose(bT[:, 0:S], m_nat[p][:, :], ident[:, :]).then_inc(P["t"].sem, 1)

                @per_batch
                def up(b, p):
                    after(pe, b, [att["ke"], att["kx"]])
                    after(pe, b - 1, [att["exp"]])
                    wait(pe, P["te"], b)
                    wait(pe, P["gelu"], b - 2)
                    for c in range(4):
                        last = pe.matmul(bU[p][:, c * S:(c + 1) * S], w["li2"][:, c * 128:(c + 1) * 128], n3T[p][:, :],
                                         start=True, stop=True)
                    last.then_inc(P["up"].sem, 1)

                @per_batch
                def down(b, p):
                    after(pe, b, [att["exp"]])
                    wait(pe, P["gelu"], b)
                    wait(pe, P["fin"], b - 1)
                    for c in range(4):
                        last = pe.matmul(bD[:, 0:C], hT[p][:, c, :], w["li3"][:, c, :], start=(c == 0), stop=(c == 3))
                    last.then_inc(P["down"].sem, 1)

                @per_batch
                def transpose_x3(b, p):
                    wait(pe, L["x3n"], b)
                    wait(pe, L["te"], b - 1)
                    free(pe)
                    pe.transpose(bX[:, 0:S], x3n[p][:, :], ident[:, :]).then_inc(L["t"].sem, 1)

                @per_batch
                def logits(b, p):
                    wait(pe, L["te"], b)
                    wait(pe, L["lg"], b - 1)
                    pe.matmul(bL[:, 0:NE], x3T[p][:, :], router[:, :], start=True, stop=True).then_inc(L["mm"].sem, 1)

                def slot(at):
                    if routed:
                        down(*at(3))
                        logits(*at(6))
                        transpose_x3(*at(5))
                        up(*at(1))
                        transpose_normed(*at(0))
                    else:
                        up(*at(3))
                        down(*at(4))
                        transpose_normed(*at(1))
                return slot

            def scalar(act):
                act.wait_ge(ld[name], ld_n[name])

                @per_batch
                def normed_transposed(b, p):
                    wait(act, P["t"], b)
                    wait(act, P["up"], b - 2)
                    act.activation(n3T[p][:, :], bT[:, 0:S], ACT.Identity, bias=w["ln3"][:, 1:2], scale=w["ln3"][:, 0:1])\
                       .then_inc(P["te"].sem, 1)

                @per_batch
                def gelus(b, p):
                    wait(act, P["up"], b)
                    wait(act, P["down"], b - 2)
                    for c in range(4):
                        act.activation(hT[p][:, c, :], bU[p][:, c * S:(c + 1) * S], ACT.Gelu, bias=w["li2b"][:, c:c + 1])\
                           .then_inc(P["gelu"].sem, 1)

                @per_batch
                def x3_transposed(b, p):
                    wait(act, L["t"], b)
                    wait(act, L["mm"], b - 2)
                    act.activation(x3T[p][:, :], bX[:, 0:S], ACT.Copy).then_inc(L["te"].sem, 1)

                @per_batch
                def x3_kept(b, p):
                    wait(act, L["x3n"], b)
                    act.activation(x3[:, one(b), 0:C].rearrange("p a b -> p (a b)"), x3n[p][:, :], ACT.Copy).then_inc(L["x3"].sem, 1)

                def slot(at):
                    if routed:
                        gelus(*at(2))
                        x3_transposed(*at(5))
                        normed_transposed(*at(0))
                        x3_kept(*at(5))
                    else:
                        normed_transposed(*at(1))
                        gelus(*at(2))
                return slot

            def vector(dve):

                def x_in(b):
                    return xo[:, one(b), :].rearrange("p a b -> p (a b)")

                def z_of(b):
                    return z[:, one(b), :].rearrange("p a b -> p (a b)")

                @per_batch
                def statistics(b, p):
                    wait(dve, att["res"], b)
                    wait(dve, P["ln"], b - 1)
                    free(dve)
                    dve.bn_stats(m_st[p][:, :], x_in(b)).then_inc(P["ln"].sem, 1)

                @per_batch
                def mean_and_variance(b, p):
                    wait(dve, P["ln"], b, 1)
                    wait(dve, P["nat"], b - 2)
                    free(dve)
                    dve.bn_aggr(m_mv[p][:, :], m_st[p][:, :]).then_inc(P["ln"].sem, 1)

                @per_batch
                def guarded(b, p):
                    wait(dve, P["ln"], b, 2)
                    wait(dve, P["lnp"], b - 2)
                    dve.tensor_scalar(m_ve[p][:, :], m_mv[p][:, 1:2], EPS, None, ALU.add).then_inc(P["ln"].sem, 1)

                @per_batch
                def normed(b, p):
                    wait(dve, P["lnp"], b)
                    wait(dve, P["t"], b - 2)
                    dve.tensor_scalar(m_nat[p][:, :], x_in(b), m_mv[p][:, 0:1], m_rs[p][:, 0:1], ALU.subtract, ALU.mult)\
                       .then_inc(P["nat"].sem, 1)

                @per_batch
                def finished(b, p):
                    wait(dve, P["down"], b)
                    wait(dve, P["r2"], b)
                    dve.tensor_tensor(z_of(b), bD[:, 0:C], r2[p][:, :], ALU.add).then_inc(P["fin"].sem, 1)

                @per_batch
                def z_statistics(b, p):
                    wait(dve, P["fin"], b)
                    free(dve)
                    dve.bn_stats(m_st2[p][:, :], z_of(b)).then_inc(L["ln"].sem, 1)

                @per_batch
                def z_mean_and_variance(b, p):
                    wait(dve, L["ln"], b, 1)
                    wait(dve, L["x3n"], b - 2)
                    free(dve)
                    dve.bn_aggr(m_mv2[p][:, :], m_st2[p][:, :]).then_inc(L["ln"].sem, 1)

                @per_batch
                def z_guarded(b, p):
                    wait(dve, L["ln"], b, 2)
                    wait(dve, L["lnp"], b - 2)
                    dve.tensor_scalar(m_ve2[p][:, :], m_mv2[p][:, 1:2], EPS, None, ALU.add).then_inc(L["ln"].sem, 1)

                @per_batch
                def z_normed(b, p):
                    wait(dve, L["lnp"], b)
                    wait(dve, L["t"], b - 2)
                    wait(dve, L["x3"], b - 2)
                    dve.tensor_scalar(x3n[p][:, :], z_of(b), m_mv2[p][:, 0:1], m_rs2[p][:, 0:1], ALU.subtract, ALU.mult)\
                       .then_inc(L["x3n"].sem, 1)

                @per_batch
                def logits_kept(b, p):
                    wait(dve, L["mm"], b)
                    free(dve)
                    dve.tensor_copy(logit[:, one(b), :].rearrange("p a b -> p (a b)"), bL[:, 0:NE]).then_inc(L["lg"].sem, 1)

                def slot(at):
                    if routed:
                        statistics(*at(0))
                        normed(*at(1))
                        mean_and_variance(*at(0))
                        z_statistics(*at(4))
                        guarded(*at(0))
                        z_mean_and_variance(*at(4))
                        z_normed(*at(5))
                        z_guarded(*at(4))
                        finished(*at(3))
                        logits_kept(*at(6))
                    else:
                        statistics(*at(0))
                        normed(*at(2))
                        mean_and_variance(*at(0))
                        guarded(*at(0))
                        finished(*at(5))
                    t, _ = at(0)
                    if not routed and isinstance(t, int) and t == 4:
                        context_norm(dve, 6)
                        dve.wait_ge(c_steps, 7)
                        dve.tensor_copy(x3[:, :, C:CW].rearrange("p b o -> p (b o)").bitcast(I32), token[:, :]).then_inc(const_ready, 1)

                return slot

            def gpsimd(pool):
                pool.wait_ge(ld[name], ld_n[name])

                @per_batch
                def inverse_deviation(b, p):
                    wait(pool, P["ln"], b, 3)
                    wait(pool, P["nat"], b - 2)
                    pool.tensor_tensor(m_rs[p][:, :], m_ve[p][:, :], mhalf[:, 0:1], ALU.pow).then_inc(P["lnp"].sem, 1)

                @per_batch
                def residual_sum(b, p):
                    wait(pool, att["res"], b)
                    wait(pool, P["fin"], b - 2)
                    wait(pool, P["r2"], b - 1)
                    if "sum" in att:
                        wait(pool, att["sum"], b)
                    acc, *rest = (r[:, :] if r is w["li3b"] else r[:, one(b), :].rearrange("p a b -> p (a b)") for r in residuals)
                    for k, r in enumerate(rest):
                        dst = r2[p] if k == NR - 1 else r2t[k % 2]
                        pool.tensor_tensor(dst[:, :], r, acc, ALU.add)\
                            .then_inc(P["r2"].sem, 1)
                        if k < NR - 1:
                            wait(pool, P["r2"], b, k + 1)
                        acc = dst[:, :]

                @per_batch
                def z_inverse_deviation(b, p):
                    wait(pool, L["ln"], b, 3)
                    wait(pool, L["x3n"], b - 2)
                    pool.tensor_tensor(m_rs2[p][:, :], m_ve2[p][:, :], mhalf[:, 0:1], ALU.pow).then_inc(L["lnp"].sem, 1)

                def slot(at):
                    if routed:
                        inverse_deviation(*at(1))
                        residual_sum(*at(3))
                        z_inverse_deviation(*at(5))
                    else:
                        inverse_deviation(*at(1))
                        residual_sum(*at(4))
                return slot

            return {"tensor": tensor, "scalar": scalar, "vector": vector, "gpsimd": gpsimd, "steps": P, "peel": B, "skew": 6 if routed else 5}

        R_ALL = [s for k, s in R.items() if k not in ("x1", "lnp")]
        self_att = attention("a1", att_w[0], x1, True, R["x1"],
                             {"bQ": [R["rope"]], "bK": [R["silu"], R["v"]], "bO": [R["qkT"]], "bE": [R["ln"]], "bS": [R["prob"], R["oT"], R["nat"]],
                              "kd": [R["st"]], "E": [R["av"], R["t4"]], "ET": R_ALL, "xa": [], "xo": []})
        mlp1 = mlp("m1", mlp_w[0], [mlp_w[0]["li3b"], xa, xo], self_att["steps"], False)
        m1 = mlp1["steps"]
        cross_att = attention("a2", att_w[1], z, False, m1["fin"],
                              {"bQ": [m1["te"]], "bK": [m1["gelu"]], "bO": [], "bE": [], "bS": [m1["gelu"], m1["fin"]],
                               "kd": [], "E": [], "ET": [], "xa": [m1["r2"]], "xo": [m1["nat"], m1["r2"]]},
                              (x1, mlp_w[1]["li3b"], "m2"))
        mlp2 = mlp("m2", mlp_w[1], [xo, x1], cross_att["steps"], True)
        retention = {"tensor": retention_tensor, "scalar": retention_scalar, "vector": retention_vector, "gpsimd": retention_gpsimd,
                     "peel": 6, "skew": 4}
        phases = [retention, self_att, mlp1, cross_att, mlp2]
        for phase, join in zip(phases, [(2, 2, 0, 0), (3, 3, 0, 0), (3, 3, 2, 2), (3, 3, 1, 1)]):
            phase["join"] = dict(zip(("tensor", "scalar", "vector", "gpsimd"), join))

        taken[0] = 0
        lmax = sb("lmax", [S, B])
        code = carve("code", [S, B, NE])
        cmax = sb("cmax", [S, B])
        hot = carve("hot", [S, B, NE])
        ones = sb("ones", [S, S])
        base_b = sb("base_b", [S, NE, B + 1])
        tot1 = sb("tot1", [S, NE, B + 1])
        goes_on = sb("goes_on", [S, NE, B + 1])
        one_e = sb("one_e", [S, NE])
        full = carve("full", [S, NE, B])
        ntile = sb("ntile", [S, NE])
        tend = sb("tend", [S, NE + 1])
        start_e = sb("start_e", [S, NE])
        pos = carve("pos", [S, B, NE])
        pos2 = carve("pos2", [S, B, NE])
        place_f = sb("place_f", [S, B])
        place = sb("place", [S, B], I32)
        ended = carve("ended", [S, NE, NT])
        eid_f = sb("eid_f", [S, NT])
        eid = sb("eid", [S, NT], I32)
        placing = sem("placing")
        placed_mm = sem("placed_mm")
        n_place = [0]
        marks = {}

        def place_vector(dve):
            def link(ins, mark=None):
                n_place[0] += 1
                ins.then_inc(placing, 1)
                dve.wait_ge(placing, n_place[0])
                if mark:
                    marks[mark] = n_place[0]

            def bc(ap, shape):
                return ap.to_broadcast(shape)

            dve.wait_ge(L["lg"].sem, L["lg"].at(B - 1))
            link(dve.tensor_reduce(lmax[:, :], logit[:, :, :], AX.X, ALU.max))
            link(dve.tensor_tensor(code[:, :, :], logit[:, :, :], bc(lmax[:, :].rearrange("p (b o) -> p b o", o=1), (S, B, NE)), ALU.is_ge))
            link(dve.tensor_tensor(code[:, :, :], code[:, :, :], bc(rank_code[:, :].rearrange("p (o e) -> p o e", o=1), (S, B, NE)), ALU.mult))
            link(dve.tensor_reduce(cmax[:, :], code[:, :, :], AX.X, ALU.max))
            link(dve.tensor_tensor(hot[:, :, :], bc(rank_code[:, :].rearrange("p (o e) -> p o e", o=1), (S, B, NE)),
                                   bc(cmax[:, :].rearrange("p (b o) -> p b o", o=1), (S, B, NE)), ALU.is_equal), "hot")
            dve.wait_ge(placed_mm, 2)
            link(dve.tensor_copy(tot1[:, :, 1:B + 1], bank[2][:, 0:B * NE].rearrange("p (b e) -> p e b", e=NE)))
            link(dve.tensor_tensor_scan(base_b[:, :, :].rearrange("p e b -> p (e b)"), goes_on[:, :, :].rearrange("p e b -> p (e b)"),
                                        tot1[:, :, :].rearrange("p e b -> p (e b)"), 0.0, ALU.mult, ALU.add))
            link(dve.tensor_tensor(full[:, :, :], bc(base_b[:, :, B:B + 1], (S, NE, B)), tile_at[:, :, :], ALU.is_gt))
            link(dve.tensor_reduce(ntile[:, :], full[:, :, :], AX.X, ALU.add))
            link(dve.tensor_tensor_scan(tend[:, 1:NE + 1], one_e[:, :], ntile[:, :], 0.0, ALU.mult, ALU.add))
            link(dve.tensor_scalar(start_e[:, :], tend[:, 0:NE], float(S), None, ALU.mult))
            link(dve.tensor_tensor(pos[:, :, :], bank[1][:, 0:B * NE].rearrange("p (b e) -> p b e", e=NE),
                                   base_b[:, :, 0:B].rearrange("p e b -> p b e"), ALU.add))
            link(dve.tensor_tensor(pos2[:, :, :], pos[:, :, :], bc(start_e[:, :].rearrange("p (o e) -> p o e", o=1), (S, B, NE)), ALU.add))
            link(dve.tensor_tensor(pos[:, :, :], pos2[:, :, :], hot[:, :, :], ALU.mult))
            link(dve.tensor_reduce(place_f[:, :], pos[:, :, :], AX.X, ALU.add))
            link(dve.tensor_copy(place[:, :], place_f[:, :]), "place")
            link(dve.tensor_tensor(ended[:, :, :], bc(tile_no[:, :].rearrange("p (o j) -> p o j", o=1), (S, NE, NT)),
                                   bc(tend[:, 1:NE + 1].rearrange("p (e o) -> p e o", o=1), (S, NE, NT)), ALU.is_ge))
            link(dve.tensor_reduce(eid_f[:, :], ended[:, :, :].rearrange("p e j -> p j e"), AX.X, ALU.add))
            link(dve.tensor_scalar(eid_f[:, :], eid_f[:, :], float(NE - 1), None, ALU.min))
            link(dve.tensor_copy(eid[:, :], eid_f[:, :]), "eid")

        def place_tensor(pe):
            pe.wait_ge(placing, 5)
            hot2 = hot[:, :, :].rearrange("p b e -> p (b e)")
            pe.wait_ge(L["lg"].sem, L["lg"].at(B - 1))
            pe.matmul(bank[1][:, 0:B * NE], tri[:, :], hot2, start=True, stop=True).then_inc(placed_mm, 1)
            pe.matmul(bank[2][:, 0:B * NE], ones[:, :], hot2, start=True, stop=True).then_inc(placed_mm, 1)

        scattered, blanked = sem("scattered"), sem("blanked")

        def place_gpsimd(pool):
            pool.wait_ge(placing, marks["place"])
            pool.wait_ge(L["x3"].sem, L["x3"].at(B - 1))
            pool.wait_ge(blanked, 16)
            pool.wait_ge(const_ready, 2)
            for b in range(B):
                pool.indirect_dma_start(xs_dram, bass.IndirectOffsetOnAxis(ap=place[:, b:b + 1], axis=0), x3[:, b, :], None)\
                    .then_inc(scattered, 16)

        xt = arena[:, taken[0]:taken[0] + NT * CW].rearrange("p (j c) -> p j c", c=CW)
        taken[0] += NT * CW
        xc = [carve(f"xc{p}", [S, C]) for p in range(2)]
        xtT = [carve(f"xtT{p}", [C, S]) for p in range(2)]
        gs = [carve(f"gs{p}", [S, EI]) for p in range(2)]
        he = [carve(f"he{p}", [S, EI]) for p in range(2)]
        heT = [carve(f"heT{p}", [128, 3, S]) for p in range(2)]
        yr = [carve(f"yr{p}", [S, C]) for p in range(2)]
        yo = [sb(f"yo{p}", [S, C]) for p in range(2)]
        number = [sb(f"number{p}", [S, 1], I32) for p in range(2)]
        X = {k: steps("x_" + k, n) for k, n in {
            "cp": 1, "t": 1, "te": 1, "up": 1, "silu": 1, "h": 1, "ht": 1, "hte": 2, "dn": 1, "ye": 1, "ln": 3, "lnp": 1, "no": 1, "yo": 1}.items()}
        xt_in = [sem(f"xt_in{p}") for p in range(2)]
        y_out = [sem(f"y_out{p}") for p in range(2)]
        bankT, bankG, bankU, bankH, bankY = bank[0], bank[1], bank[2], bank[3], bank[4]
        per_tile = per_batch_of(NT)

        def experts_sync(sp):
            sp.wait_ge(scattered, 16 * B)

            @per_tile
            def load_tile(b, p):
                if not isinstance(b, int) or b >= 2:
                    sp.wait_ge(xt_in[p], (b - p) * 8)
                sp.dma_start(xt[:, one(b), :], xs_dram.rearrange("(j p) c -> p j c", p=S)[:, one(b), :]).then_inc(xt_in[p], 16)

            slots(sp, lambda at: load_tile(*at(0)), 2, 0, NT)
            for p in range(2):
                sp.wait_ge(y_out[p], 16 * ((NT - p + 1) // 2))

        def experts_tensor(pe):
            pe.wait_ge(placing, marks["eid"])

            def expert(b):
                return pe.value_load(eid[0:1, one(b)], min_val=0, max_val=NE - 1)

            @per_tile
            def transpose_tile(b, p):
                wait(pe, X["cp"], b)
                wait(pe, X["te"], b - 1)
                free(pe)
                pe.transpose(bankT[:, 0:S], xc[p][:, :], ident[:, :]).then_inc(X["t"].sem, 1)

            @per_tile
            def gate_and_up(b, p):
                e = expert(b)
                wait(pe, X["te"], b)
                wait(pe, X["h"], b - 1)
                pe.matmul(bankG[:, 0:EI], xtT[p][:, :], egu[:, one(e), 0:EI], start=True, stop=True)
                pe.matmul(bankU[:, 0:EI], xtT[p][:, :], egu[:, one(e), EI:2 * EI], start=True, stop=True).then_inc(X["up"].sem, 1)

            @per_tile
            def transpose_hidden(b, p):
                wait(pe, X["h"], b)
                wait(pe, X["hte"], b - 1)
                for c, n in enumerate(EC):
                    last = pe.transpose(bankH[0:n, c * S:(c + 1) * S], he[p][:, c * 128:c * 128 + n], ident[:, :])
                last.then_inc(X["ht"].sem, 1)

            @per_tile
            def down(b, p):
                e = expert(b)
                wait(pe, X["hte"], b)
                wait(pe, X["ye"], b - 1)
                for c, n in enumerate(EC):
                    last = pe.matmul(bankY[:, 0:C], heT[p][0:n, c, :], edn[0:n, one(e), c, :], start=(c == 0), stop=(c == 2))
                last.then_inc(X["dn"].sem, 1)

            def slot(at):
                gate_and_up(*at(2))
                transpose_tile(*at(1))
                transpose_hidden(*at(3))
                down(*at(4))
            slots(pe, slot, 8, 6, NT)

        def experts_scalar(act):
            @per_tile
            def tile_transposed(b, p):
                wait(act, X["t"], b)
                wait(act, X["up"], b - 2)
                act.activation(xtT[p][:, :], bankT[:, 0:S], ACT.Copy).then_inc(X["te"].sem, 1)

            @per_tile
            def silus(b, p):
                wait(act, X["up"], b)
                wait(act, X["h"], b - 2)
                act.activation(gs[p][:, :], bankG[:, 0:EI], ACT.Silu).then_inc(X["silu"].sem, 1)

            @per_tile
            def hidden_transposed(b, p):
                wait(act, X["ht"], b)
                wait(act, X["dn"], b - 2)
                act.activation(heT[p][:, 0:2, :].rearrange("p a b -> p (a b)"), bankH[:, 0:2 * S], ACT.Copy).then_inc(X["hte"].sem, 1)
                act.activation(heT[p][0:EC[2], 2, :], bankH[0:EC[2], 2 * S:3 * S], ACT.Copy).then_inc(X["hte"].sem, 1)

            def slot(at):
                silus(*at(2))
                tile_transposed(*at(1))
                hidden_transposed(*at(3))
            slots(act, slot, 8, 6, NT)

        def experts_vector(dve):
            @per_tile
            def tile_copied(b, p):
                dve.wait_ge(xt_in[p], (b - p) * 8 + 16)
                wait(dve, X["t"], b - 2)
                free(dve)
                dve.tensor_copy(xc[p][:, :], xt[:, one(b), 0:C].rearrange("p a b -> p (a b)")).then_inc(X["cp"].sem, 1)

            @per_tile
            def hidden(b, p):
                wait(dve, X["silu"], b)
                wait(dve, X["ht"], b - 2)
                dve.tensor_tensor(he[p][:, :], bankU[:, 0:EI], gs[p][:, :], ALU.mult).then_inc(X["h"].sem, 1)

            @per_tile
            def residual(b, p):
                wait(dve, X["dn"], b)
                wait(dve, X["yo"], b - 2)
                dve.tensor_tensor(yr[p][:, :], bankY[:, 0:C], xt[:, one(b), 0:C].rearrange("p a b -> p (a b)"), ALU.add)\
                   .then_inc(X["ye"].sem, 1)

            @per_tile
            def statistics(b, p):
                wait(dve, X["ye"], b)
                free(dve)
                dve.bn_stats(st[p][:, :], yr[p][:, :]).then_inc(X["ln"].sem, 1)

            @per_tile
            def mean_and_variance(b, p):
                wait(dve, X["ln"], b, 1)
                free(dve)
                dve.bn_aggr(mv[p][:, :], st[p][:, :]).then_inc(X["ln"].sem, 1)

            @per_tile
            def guarded(b, p):
                wait(dve, X["ln"], b, 2)
                wait(dve, X["lnp"], b - 2)
                dve.tensor_scalar(ve[p][:, :], mv[p][:, 1:2], EPS, None, ALU.add).then_inc(X["ln"].sem, 1)

            @per_tile
            def token_numbers(b, p):
                if not isinstance(b, int) or b >= 2:
                    dve.wait_ge(y_out[p], (b - p) * 8)
                free(dve)
                dve.tensor_copy(number[p][:, :], xt[:, one(b), C:C + 1].rearrange("p a b -> p (a b)").bitcast(I32)).then_inc(X["no"].sem, 1)

            @per_tile
            def normed(b, p):
                wait(dve, X["lnp"], b)
                dve.tensor_scalar(yo[p][:, :], yr[p][:, :], mv[p][:, 0:1], rs[p][:, 0:1], ALU.subtract, ALU.mult).then_inc(X["yo"].sem, 1)

            def slot(at):
                residual(*at(5))
                statistics(*at(5))
                tile_copied(*at(0))
                mean_and_variance(*at(5))
                guarded(*at(5))
                token_numbers(*at(6))
                normed(*at(6))
                hidden(*at(2))
            slots(dve, slot, 8, 6, NT)

        def experts_gpsimd(pool):
            @per_tile
            def inverse_deviation(b, p):
                wait(pool, X["ln"], b, 3)
                wait(pool, X["yo"], b - 2)
                pool.tensor_tensor(rs[p][:, :], ve[p][:, :], mhalf[:, 0:1], ALU.pow).then_inc(X["lnp"].sem, 1)

            @per_tile
            def scatter(b, p):
                wait(pool, X["no"], b)
                wait(pool, X["yo"], b)
                free(pool)
                pool.indirect_dma_start(out.rearrange("b s c -> (b s) c"), bass.IndirectOffsetOnAxis(ap=number[p][:, :], axis=0),
                                        yo[p][:, :], None, bounds_check=B * S - 1, oob_is_err=False).then_inc(y_out[p], 16)

            def slot(at):
                scatter(*at(6))
                inverse_deviation(*at(5))
            slots(pool, slot, 8, 6, NT)

        def setup_vector(dve):
            for t in (qkr[0], qkr[1]):
                dve.memset(t[:, :, :], 0.0)
            dve.memset(parts[:, :, :], 0.0)
            dve.memset(ones[:, :], 1.0)
            dve.memset(tot1[:, :, 0:1], 0.0)
            dve.memset(goes_on[:, :, 0:1], 0.0)
            dve.memset(goes_on[:, :, 1:B + 1], 1.0)
            dve.memset(one_e[:, :], 1.0)
            dve.memset(tend[:, 0:1], 0.0).then_inc(vector_made, 1)
            dve.wait_ge(vector_made, 1)

        block = ctx.enter_context(nc.Block())

        @block.vector
        def _(dve):
            setup_vector(dve)
            run_phases(dve, "vector", phases)
            place_vector(dve)
            experts_vector(dve)

        @block.sync
        def _(sp):
            retention_sync(sp)
            for group, dst, src in loads_later:
                if group not in ("const", "a1"):
                    sp.dma_start(dst, src).then_inc(ld[group], 16)
            sp.dma_start(xs_dram, A["blank_rows"]).then_inc(blanked, 16)
            experts_sync(sp)

        @block.tensor
        def _(pe):
            run_phases(pe, "tensor", phases)
            place_tensor(pe)
            experts_tensor(pe)

        @block.scalar
        def _(act):
            run_phases(act, "scalar", phases)
            experts_scalar(act)

        @block.gpsimd
        def _(pool):
            pool.memset(mhalf[:, :], -0.5).then_inc(pool_made, 1)
            pool.memset(ctx_half[:, :], -0.5).then_inc(pool_made, 1)
            for t in kd:
                pool.memset(t[:, :, :, :], 0.0).then_inc(pool_made, 1)
            pool.wait_ge(pool_made, 4)
            pool.wait_ge(ld["ret"], ld_n["ret"])
            run_phases(pool, "gpsimd", phases)
            place_gpsimd(pool)
            experts_gpsimd(pool)


def constants():
    f = np.float32
    inv = (f(1.0) / f(10000.0) ** (np.arange(0, RD, 2, dtype=f) / f(RD))).astype(f)
    ang = np.arange(S, dtype=f)[:, None] * inv[None, :]
    cos, sin = np.cos(ang), np.sin(ang)
    cos = np.repeat(cos, 2, axis=1)
    sin = np.stack([-sin, sin], axis=-1).reshape(S, RD)
    decay = np.zeros((S, 2, 4, S))
    diff = np.arange(S)[None, :] - np.arange(S)[:, None]
    for h in range(RH):
        slope = np.log2(1.0 - 2.0 ** (-5.0 - h))
        decay[:, h // 4, h % 4, :] = np.where(diff >= 0, np.exp2(np.maximum(diff, 0) * slope), 0.0) * RD ** -0.5
    bc = np.zeros((128, HG, 128))
    for hg in range(HG):
        for g in range(4):
            for j in (hg, 16 + hg):
                bc[32 * g + j, hg, 32 * g:32 * g + 32] = 1.0
    out = {"cos": np.tile(cos, (1, 2 * RH)), "sin": np.tile(sin, (1, 2 * RH)), "decay": decay, "ident": np.eye(128),
           "bc_sel": bc, "later": np.tril(np.ones((S, S)), -1), "tri": np.triu(np.ones((S, S)), 1),
           "rank_code": NE - np.arange(NE)[None, :], "tile_at": np.tile(S * np.arange(B), NE)[None, :], "tile_no": np.arange(NT)[None, :]}
    out = {k: np.ascontiguousarray(v.astype(f)) for k, v in out.items()}
    out["token"] = np.ascontiguousarray(np.arange(B * S, dtype=np.int32).reshape(B, S).T)
    blank = np.zeros((NT * S, C + 1), np.int32)
    blank[:, C] = B * S + np.arange(NT * S)
    out["blank_rows"] = blank.view(f)
    return out


def laid_out(i):
    t = {"x": i["x"], "xT": i["x"].transpose(2, 0, 1), "ctx": i["ctx_512"],
         "wqk": np.concatenate([i["L0_attn_Wq"], i["L0_attn_Wk"]], 1), "wvg": np.concatenate([i["L0_attn_Wv"], i["L0_attn_Wg"]], 1),
         "wo": i["L0_attn_Wo"].reshape(2, 128, C).transpose(1, 0, 2), "gw": np.tile(i["L0_attn_g_norm_w"], RH)[None, :],
         "router": i["L0_ffn_router_w"].T,
         "egu": np.concatenate([i["L0_ffn_gate_w"], i["L0_ffn_up_w"]], 1).transpose(2, 0, 1),
         "edn": i["L0_ffn_down_w"].transpose(2, 0, 1)}
    for n, a in enumerate(("a1", "a2")):
        p = f"L0_xattn_{a}_"
        for k in ("wq", "wk", "wv"):
            w = i[p + k]
            t[f"{a}_{k}"] = w.transpose(1, 0, 2).reshape(w.shape[1], AH * AD)
        t[a + "_li1"] = i[p + "li1_w"].reshape(HG, 128, C).transpose(1, 0, 2)
        t[a + "_li1b"] = i[p + "li1_b"][None, :]
        for k in ("lnx", "lny", "ln3"):
            t[f"{a}_{k}"] = np.stack([i[p + k + "_g"], i[p + k + "_b"]], 1)
        t[a + "_g"] = i[f"L0_xattn_ln{n + 1}_g"][None, :]
        t[a + "_b"] = i[f"L0_xattn_ln{n + 1}_b"][None, :]
        t[a + "_li2"] = i[p + "li2_w"]
        t[a + "_li2b"] = i[p + "li2_b"].reshape(4, 128).T
        t[a + "_li3"] = i[p + "li3_w"].reshape(4, 128, C).transpose(1, 0, 2)
        t[a + "_li3b"] = i[p + "li3_b"][None, :]
    return {k: np.ascontiguousarray(v) for k, v in t.items()} | constants()


def kernel(**inputs):
    import concourse.bacc as _bacc
    from concourse.bass_utils import run_bass_kernel_spmd as _run

    arrays = laid_out({k: np.asarray(v) for k, v in inputs.items()})
    nc = _bacc.Bacc("TRN2", target_bir_lowering=False, num_devices=1)
    aps = {k: nc.dram_tensor("in_" + k, v.shape, mybir.dt.from_np(v.dtype), kind="ExternalInput").ap() for k, v in arrays.items()}
    out = nc.dram_tensor("out", (B, S, C), F32, kind="ExternalOutput").ap()
    build(nc, aps, out)
    r = _run(nc, [{"in_" + k: v for k, v in arrays.items()}], core_ids=[0])
    return r.results[0]["out"]
```
